# Optimizing a Trainium2 kernel written in Bass

```python
import numpy as np
import jax
import jax.numpy as jnp

def _softmax(x, axis=-1):
    return jax.nn.softmax(x, axis=axis)

def _gelu(x):
    return jax.nn.gelu(x, approximate=True)

def _silu(x):
    return jax.nn.silu(x)

def _sigmoid(x):
    return jax.nn.sigmoid(x)

def _layernorm(x, axis=-1, eps=1e-05):
    m = jnp.mean(x, axis=axis, keepdims=True)
    v = jnp.var(x, axis=axis, keepdims=True)
    return (x - m) / jnp.sqrt(v + eps)

def _scatter_add(tgt, idx, src, axis=0):
    return tgt.at[idx].add(src)

def _segment_sum(src, seg, n):
    return jax.ops.segment_sum(src, seg, n)
kernel_name = 'mk_vit_tower_d2_tok_img768_r4_295ada'

def setup_inputs(seed: int=0):
    np.random.seed(seed)
    _w = jnp.asarray

    def _rec_inputs():
        import jax
        import jax.numpy as jnp
        _rk = jax.random.key(seed)
        x = -0.00016672 + 0.999947 * jax.random.normal(jax.random.fold_in(_rk, 1), (64, 3, 224, 224), jnp.float32)
        return x
    x = _rec_inputs()

    def _L0_tok_setup():
        import jax, jax.numpy as jnp
        import numpy as np
        CHANNEL = 3
        PATCH = 16
        D_MODEL = 192
        key = jax.random.key(seed)
        kx, kw = jax.random.split(key)
        x = jax.random.normal(kx, (64, CHANNEL, 96, 96), dtype=jnp.float32)
        fan_in = PATCH * PATCH * CHANNEL
        bound = 1.0 / np.sqrt(fan_in)
        W = jax.random.uniform(kw, (D_MODEL, fan_in), dtype=jnp.float32, minval=-bound, maxval=bound)
        return {'x': x, 'W': W}
    _L0_tok_all = _L0_tok_setup()
    _L0_tok_in = {k: v for k, v in _L0_tok_all.items() if k in ('W',)}
    del _L0_tok_all

    def _L0_attn_setup():
        import jax, jax.numpy as jnp
        import numpy as np
        NH, DK, DV, D = (8, 64, 64, 192)
        DECAY = 0.95
        WRITE_STRENGTH = 0.1
        key = jax.random.key(seed)
        ks = jax.random.split(key, 6)
        s = 0.02
        return {'x': jax.random.normal(ks[0], (4, 1024, D), dtype=jnp.float32), 'w_key': jax.random.normal(ks[1], (NH * DK, D), dtype=jnp.float32) * s, 'w_value': jax.random.normal(ks[2], (NH * DV, D), dtype=jnp.float32) * s, 'w_query': jax.random.normal(ks[3], (NH * DK, D), dtype=jnp.float32) * s, 'w_gate': jax.random.normal(ks[4], (NH, D), dtype=jnp.float32) * s, 'w_out': jax.random.normal(ks[5], (D, NH * DV), dtype=jnp.float32) * s}
    _L0_attn_all = _L0_attn_setup()
    _L0_attn_in = {k: v for k, v in _L0_attn_all.items() if k in ('w_key', 'w_value', 'w_query', 'w_gate', 'w_out')}
    del _L0_attn_all

    def _L0_ffn_setup():
        import jax, jax.numpy as jnp
        import numpy as np
        B, S, D_IN, D_HID, D_OUT = (32, 128, 192, 768, 192)
        key = jax.random.key(seed)
        k1, k2, k3, k4 = jax.random.split(key, 4)
        init_k = float(np.sqrt(1.0 / D_IN))
        init_k2 = float(np.sqrt(1.0 / D_HID))
        x = jax.random.normal(k1, (B, S, D_IN), dtype=jnp.float32)
        in_weight = jax.random.uniform(k2, (D_HID, D_IN), dtype=jnp.float32, minval=-init_k, maxval=init_k)
        in_bias = jax.random.uniform(k3, (D_HID,), dtype=jnp.float32, minval=-init_k, maxval=init_k)
        out_weight = jax.random.uniform(k4, (D_HID, D_OUT), dtype=jnp.float32, minval=-init_k2, maxval=init_k2)
        return {'x': x, 'in_weight': in_weight, 'in_bias': in_bias, 'out_weight': out_weight}
    _L0_ffn_all = _L0_ffn_setup()
    _L0_ffn_in = {k: v for k, v in _L0_ffn_all.items() if k in ('in_weight', 'in_bias', 'out_weight')}
    del _L0_ffn_all

    def _L1_attn_setup():
        import jax, jax.numpy as jnp
        import numpy as np

        def silu(x):
            return x * jax.nn.sigmoid(x)
        key = jax.random.key(seed)
        ks = jax.random.split(key, 12)
        B, S, Dm = (2, 512, 192)
        I, N, R, K = (384, 16, 48, 4)
        s = 0.02
        return {'input_states': jax.random.normal(ks[0], (B, S, Dm), jnp.float32), 'in_proj_w': jax.random.normal(ks[1], (2 * I, Dm), jnp.float32) * s, 'conv_w': jax.random.normal(ks[2], (I, 1, K), jnp.float32) * s, 'conv_b': jax.random.normal(ks[3], (I,), jnp.float32) * s, 'x_proj_w': jax.random.normal(ks[4], (R + 2 * N, I), jnp.float32) * s, 'dt_proj_w': jax.random.normal(ks[5], (I, R), jnp.float32) * s, 'dt_proj_b': jax.random.normal(ks[6], (I,), jnp.float32) * s, 'A_log': jax.random.normal(ks[7], (I, N), jnp.float32) * 0.5, 'D': jax.random.normal(ks[8], (I,), jnp.float32) * s, 'out_proj_w': jax.random.normal(ks[9], (Dm, I), jnp.float32) * s, 'alpha': jax.random.uniform(ks[10], (I,), jnp.float32), 'feature_gating': jax.random.uniform(ks[11], (I,), jnp.float32)}
    _L1_attn_all = _L1_attn_setup()
    _L1_attn_in = {k: v for k, v in _L1_attn_all.items() if k in ('in_proj_w', 'conv_w', 'conv_b', 'x_proj_w', 'dt_proj_w', 'dt_proj_b', 'A_log', 'D', 'out_proj_w', 'alpha', 'feature_gating')}
    del _L1_attn_all

    def _L1_ffn_setup():
        import jax, jax.numpy as jnp
        import numpy as np
        EPS_NORM = 1e-06
        EPS_Q = 1e-05

        def rmsnorm(x, g):
            return x * jax.lax.rsqrt(jnp.mean(x * x, axis=-1, keepdims=True) + EPS_NORM) * g

        def activation_quant(x):
            scale = 127.0 / jnp.maximum(jnp.max(jnp.abs(x), axis=-1, keepdims=True), EPS_Q)
            return jnp.clip(jnp.round(x * scale), -128, 127) / scale

        def weight_quant(w):
            scale = 1.0 / jnp.maximum(jnp.mean(jnp.abs(w)), EPS_Q)
            return jnp.clip(jnp.round(w * scale), -1, 1) / scale

        def bitlinear(x, w, g):
            x_norm = rmsnorm(x, g)
            x_q = x_norm + jax.lax.stop_gradient(activation_quant(x_norm) - x_norm)
            w_q = w + jax.lax.stop_gradient(weight_quant(w) - w)
            return jnp.einsum('bsd,od->bso', x_q, w_q)
        key = jax.random.key(seed)
        k1, k2, k3 = jax.random.split(key, 3)
        B, S, D, H = (8, 1024, 192, 512)
        x = jax.random.normal(k1, (B, S, D), dtype=jnp.float32)
        w_in = jax.random.normal(k2, (2 * H, D), dtype=jnp.float32) * 0.002
        w_out = jax.random.normal(k3, (D, H), dtype=jnp.float32) * 0.002
        g_in = jnp.ones((D,), dtype=jnp.float32)
        g_out = jnp.ones((H,), dtype=jnp.float32)
        return {'x': x, 'w_in': w_in, 'g_in': g_in, 'w_out': w_out, 'g_out': g_out}
    _L1_ffn_all = _L1_ffn_setup()
    _L1_ffn_in = {k: v for k, v in _L1_ffn_all.items() if k in ('w_in', 'g_in', 'w_out', 'g_out')}
    del _L1_ffn_all
    return {'x': x, 'L0_tok_W': _L0_tok_in['W'], 'L0_attn_w_key': _L0_attn_in['w_key'], 'L0_attn_w_value': _L0_attn_in['w_value'], 'L0_attn_w_query': _L0_attn_in['w_query'], 'L0_attn_w_gate': _L0_attn_in['w_gate'], 'L0_attn_w_out': _L0_attn_in['w_out'], 'L0_ffn_in_weight': _L0_ffn_in['in_weight'], 'L0_ffn_in_bias': _L0_ffn_in['in_bias'], 'L0_ffn_out_weight': _L0_ffn_in['out_weight'], 'L1_attn_in_proj_w': _L1_attn_in['in_proj_w'], 'L1_attn_conv_w': _L1_attn_in['conv_w'], 'L1_attn_conv_b': _L1_attn_in['conv_b'], 'L1_attn_x_proj_w': _L1_attn_in['x_proj_w'], 'L1_attn_dt_proj_w': _L1_attn_in['dt_proj_w'], 'L1_attn_dt_proj_b': _L1_attn_in['dt_proj_b'], 'L1_attn_A_log': _L1_attn_in['A_log'], 'L1_attn_D': _L1_attn_in['D'], 'L1_attn_out_proj_w': _L1_attn_in['out_proj_w'], 'L1_attn_alpha': _L1_attn_in['alpha'], 'L1_attn_feature_gating': _L1_attn_in['feature_gating'], 'L1_ffn_w_in': _L1_ffn_in['w_in'], 'L1_ffn_g_in': _L1_ffn_in['g_in'], 'L1_ffn_w_out': _L1_ffn_in['w_out'], 'L1_ffn_g_out': _L1_ffn_in['g_out']}

def reference(x, L0_tok_W, L0_attn_w_key, L0_attn_w_value, L0_attn_w_query, L0_attn_w_gate, L0_attn_w_out, L0_ffn_in_weight, L0_ffn_in_bias, L0_ffn_out_weight, L1_attn_in_proj_w, L1_attn_conv_w, L1_attn_conv_b, L1_attn_x_proj_w, L1_attn_dt_proj_w, L1_attn_dt_proj_b, L1_attn_A_log, L1_attn_D, L1_attn_out_proj_w, L1_attn_alpha, L1_attn_feature_gating, L1_ffn_w_in, L1_ffn_g_in, L1_ffn_w_out, L1_ffn_g_out):
    import jax
    import jax.numpy as jnp

    def _L0_tok_ref(x, W):
        import jax, jax.numpy as jnp
        import numpy as np
        CHANNEL = 3
        PATCH = 16
        D_MODEL = 192
        B, C, H, Wd = x.shape
        p = PATCH
        nH, nW = (H // p, Wd // p)
        patches = x.reshape(B, C, nH, p, nW, p)
        patches = patches.transpose(0, 2, 4, 3, 5, 1)
        flat = patches.reshape(B, nH * nW, p * p * C)
        return jnp.einsum('bnk,dk->bnd', flat, W)

    def _L0_attn_ref(x, w_key, w_value, w_query, w_gate, w_out):
        import jax, jax.numpy as jnp
        import numpy as np
        NH, DK, DV, D = (8, 64, 64, 192)
        DECAY = 0.95
        WRITE_STRENGTH = 0.1
        B, S, _ = x.shape
        k = (x @ w_key.T).reshape(B, S, NH, DK)
        v = (x @ w_value.T).reshape(B, S, NH, DV)
        q = (x @ w_query.T).reshape(B, S, NH, DK)
        gate = jax.nn.sigmoid(x @ w_gate.T)
        k0 = k[0]
        v0 = v[0]
        g0 = gate[0]

        def step(fw, inp):
            q_t, k0_t, v0_t, g0_t = inp
            retrieved = jnp.einsum('bhk,hkv->bhv', q_t, fw)
            write = (WRITE_STRENGTH * g0_t)[:, None, None] * (k0_t[:, :, None] * v0_t[:, None, :])
            fw_new = DECAY * fw + jax.lax.stop_gradient(write)
            return (fw_new, retrieved)
        fw0 = jnp.zeros((NH, DK, DV), dtype=x.dtype)
        inputs = (q.transpose(1, 0, 2, 3), k0, v0, g0)
        _, retrieved = jax.lax.scan(step, fw0, inputs)
        retrieved = retrieved.transpose(1, 0, 2, 3).reshape(B, S, NH * DV)
        return x + retrieved @ w_out.T

    def _L0_ffn_ref(x, in_weight, in_bias, out_weight):
        import jax, jax.numpy as jnp
        import numpy as np
        B, S, D_IN, D_HID, D_OUT = (32, 128, 192, 768, 192)
        lead = x.shape[:-1]
        xt = x.reshape(-1, in_weight.shape[1])
        h = jax.nn.gelu(jnp.einsum('td,hd->th', xt, in_weight) + in_bias, approximate=False)
        out = jnp.einsum('th,ho->to', h, out_weight)
        return out.reshape(*lead, out_weight.shape[1])

    def _L1_attn_ref(input_states, in_proj_w, conv_w, conv_b, x_proj_w, dt_proj_w, dt_proj_b, A_log, D, out_proj_w, alpha, feature_gating):
        import jax, jax.numpy as jnp
        import numpy as np

        def silu(x):
            return x * jax.nn.sigmoid(x)
        Bsz, S, _ = input_states.shape
        I, N = A_log.shape
        R = dt_proj_w.shape[1]
        K = conv_w.shape[-1]
        proj = jnp.einsum('bsd,ed->bse', input_states, in_proj_w)
        hidden, gate = jnp.split(proj.transpose(0, 2, 1), 2, axis=1)
        h = jax.lax.conv_general_dilated(hidden, conv_w, window_strides=(1,), padding=[(K - 1, 0)], dimension_numbers=('NCH', 'OIH', 'NCH'), feature_group_count=I)
        h = silu(h + conv_b[None, :, None])
        ssm_p = jnp.einsum('bis,ei->bse', h, x_proj_w)
        ts, Bm, Cm = jnp.split(ssm_p, [R, R + N], axis=-1)
        dt = jax.nn.softplus(jnp.einsum('bsr,ir->bsi', ts, dt_proj_w) + dt_proj_b)
        dt = dt.transpose(0, 2, 1)
        dt = dt.at[:, :, -1].multiply(alpha[None, :])
        A = -jnp.exp(A_log.astype(jnp.float32))
        dA = jnp.exp(A[None, :, None, :] * dt[:, :, :, None])
        dBu = dt[:, :, :, None] * Bm[:, None, :, :] * h[:, :, :, None]

        def step(state, xs):
            dA_t, dBu_t, C_t = xs
            state = dA_t * state + dBu_t
            y = jnp.einsum('bin,bn->bi', state, C_t)
            return (state, y)
        init = jnp.zeros((Bsz, I, N), input_states.dtype)
        _, ys = jax.lax.scan(step, init, (dA.transpose(2, 0, 1, 3), dBu.transpose(2, 0, 1, 3), Cm.transpose(1, 0, 2)))
        y = ys.transpose(1, 2, 0)
        y = (y + h * D[None, :, None]) * silu(gate)
        y = y.at[:, :, -1].multiply(feature_gating[None, :])
        return jnp.einsum('bis,di->bsd', y, out_proj_w)

    def _L1_ffn_ref(x, w_in, g_in, w_out, g_out):
        import jax, jax.numpy as jnp
        import numpy as np
        EPS_NORM = 1e-06
        EPS_Q = 1e-05

        def rmsnorm(x, g):
            return x * jax.lax.rsqrt(jnp.mean(x * x, axis=-1, keepdims=True) + EPS_NORM) * g

        def activation_quant(x):
            scale = 127.0 / jnp.maximum(jnp.max(jnp.abs(x), axis=-1, keepdims=True), EPS_Q)
            return jnp.clip(jnp.round(x * scale), -128, 127) / scale

        def weight_quant(w):
            scale = 1.0 / jnp.maximum(jnp.mean(jnp.abs(w)), EPS_Q)
            return jnp.clip(jnp.round(w * scale), -1, 1) / scale

        def bitlinear(x, w, g):
            x_norm = rmsnorm(x, g)
            x_q = x_norm + jax.lax.stop_gradient(activation_quant(x_norm) - x_norm)
            w_q = w + jax.lax.stop_gradient(weight_quant(w) - w)
            return jnp.einsum('bsd,od->bso', x_q, w_q)
        h = bitlinear(x, w_in, g_in)
        up, gate = jnp.split(h, 2, axis=-1)
        y = jax.nn.silu(gate) * up
        return bitlinear(y, w_out, g_out)
    h = _L0_tok_ref(x, L0_tok_W)
    h = h + _L0_attn_ref(_layernorm(h, axis=-1), L0_attn_w_key, L0_attn_w_value, L0_attn_w_query, L0_attn_w_gate, L0_attn_w_out)
    h = h + _L0_ffn_ref(_layernorm(h, axis=-1), L0_ffn_in_weight, L0_ffn_in_bias, L0_ffn_out_weight)
    h = h + _L1_attn_ref(_layernorm(h, axis=-1), L1_attn_in_proj_w, L1_attn_conv_w, L1_attn_conv_b, L1_attn_x_proj_w, L1_attn_dt_proj_w, L1_attn_dt_proj_b, L1_attn_A_log, L1_attn_D, L1_attn_out_proj_w, L1_attn_alpha, L1_attn_feature_gating)
    h = h + _L1_ffn_ref(_layernorm(h, axis=-1), L1_ffn_w_in, L1_ffn_g_in, L1_ffn_w_out, L1_ffn_g_out)
    return h

_drawn_inputs = setup_inputs


def setup_inputs(seed=0):
    import zlib

    import numpy as np

    out = dict(_drawn_inputs(seed))
    spreads = {'L1_ffn_g_in': (1.0, 0.6), 'L1_ffn_g_out': (1.0, 0.6)}
    factors = {'L0_attn_w_key': 6.747,
     'L0_attn_w_value': 6.717,
     'L0_attn_w_query': 6.776,
     'L0_attn_w_gate': 8.0,
     'L0_attn_w_out': 6.766,
     'L0_ffn_in_bias': 35.136,
     'L1_attn_in_proj_w': 8.0,
     'L1_attn_conv_w': 8.0,
     'L1_attn_conv_b': 8.0,
     'L1_attn_x_proj_w': 8.0,
     'L1_attn_dt_proj_b': 8.0,
     'L1_attn_A_log': 8.0,
     'L1_attn_D': 64.0,
     'L1_attn_out_proj_w': 8.0,
     'L1_attn_alpha': 8.0,
     'L1_attn_feature_gating': 8.0,
     'L1_ffn_w_in': 64.0,
     'L1_ffn_w_out': 64.0,
     'L0_ffn_in_weight': 4.972,
     'L0_ffn_out_weight': 3.64}
    for name, (base, spread) in spreads.items():
        noise = np.random.default_rng([zlib.crc32(name.encode()), seed]).standard_normal(out[name].shape)
        drawn = base * np.exp(spread * noise) if base else spread * noise
        out[name] = jnp.asarray(drawn.astype(out[name].dtype))
    for name, factor in factors.items():
        out[name] = (out[name] * factor).astype(out[name].dtype)
    return out
```

```python
from contextlib import ExitStack

import concourse.bass as bass
from concourse import mybir

ALU = mybir.AluOpType
ACT = mybir.ActivationFunctionType
AX_X = mybir.AxisListType.X
F32 = mybir.dt.float32
BF16 = mybir.dt.bfloat16

B, T, D, PIX = 64, 196, 192, 768
GB = 4
NG = B // GB
TC = 28
J = T // TC
TT = GB * TC
GT = GB * T
HB = GT // 2
DH = D // 2
KC = PIX // 128
NH, DK = 8, 64
TS = 14
NR = TC // TS
RB = NH * TS
HID = 768
HC = HID // 128
I, N, R, K = 384, 16, 48, 4
IC = I // 128
FH = 512
FC = FH // 128
DECAY, WRITE = 0.95, 0.1
LN_EPS, RMS_EPS, Q_EPS = 1e-5, 1e-6, 1e-5
MAGIC = 12582912.0
PAIRS = [(0, 2), (2, 4), (4, 6), (6, 7)]
XBUF = 4


class Signal:

    def __init__(self, sem, order, credit=0):
        self.sem = sem
        self.start, n = {}, 0
        for key, count in order:
            self.start[key] = n
            n += count
        self.per_turn = n
        self.credit = n if credit == "turn" else credit

    def at(self, g, key, extra=0):
        return self.sem, g * self.per_turn + (extra + (self.start[key] + 1 + self.credit))

    def last_turn(self, g, key, extra=0):
        assert self.credit == self.per_turn
        return self.sem, g * self.per_turn + (extra + (self.start[key] + 1))


def program(nc, xt, x0t, w_tok, w_key, w_query, w_value, w_outt, w_gate, ffn_in, ffn_out,
            w_inp, conv_w, conv_b, w_xp, w_bc, w_dt, b_dt, a_log, d_skip, w_op, alpha, fgate,
            q_in, g_in, q_out, g_out, ident_c, identb_c, mask_c, dec_c, decp_c, sel_c, saved, out):
    with ExitStack() as ctx:
        def sb(name, shape, dt=F32):
            return ctx.enter_context(nc.sbuf_tensor(name, shape, dt))

        def sem(name):
            return ctx.enter_context(nc.semaphore(name))

        bank = ctx.enter_context(nc.psum_tensor("bank", [128, 8, 512], F32))
        ident = sb("ident", [128, 128])
        identb = sb("identb", [128, 128], BF16)
        mask = sb("mask", [RB, 2 * NR * TT])
        decp = sb("decp", [TT, 1])
        sel = sb("sel", [96, 2 * N], BF16)
        wtok = sb("wtok", [128, KC, D])
        wfi = sb("wfi", [DH + 1, 2, HID])
        wfo = sb("wfo", [128, HC, D])
        winp = sb("winp", [DH, 2, 2 * I])
        wxp = sb("wxp", [128, IC, R])
        wbc = sb("wbc", [128, IC, 96])
        wdt = sb("wdt", [R, I])
        wop = sb("wop", [128, IC, D])
        cw = sb("cw", [128, IC, K])
        cvec = sb("cvec", [128, 5, IC])
        amat = sb("amat", [128, IC, N])
        qwi = sb("qwi", [DH, 2, 2 * FH], BF16)
        qwo = sb("qwo", [128, FC, D], BF16)
        gin = sb("gin", [TT, D])
        gout = sb("gout", [TT, FH])
        wsc = sb("wsc", [128, 16])
        amask = sb("amask", [DH, 2, J, NR, RB])
        bmat = sb("bmat", [RB, J, NR, D])
        mmat = sb("mmat", [DH, J, 2, D])
        xst = sb("xst", [128, XBUF, KC, TT])
        h = sb("h", [TT, J, D])
        xln = sb("xln", [TT, J, D])
        stats = sb("stats", [TT, J, 6])
        small = sb("small", [TT, 16, J])
        xT = sb("xT", [DH + 1, 2, GT])
        scT = sb("scT", [RB, 2, 2, NR, TT])
        gT = sb("gT", [128, HC, 2 * TT])
        mix = sb("mix", [128, 4, IC, GT])
        hh, dt, sg, u = (mix[:, i] for i in range(4))
        dbu = sb("dbu", [128, 2, GT])
        st = sb("st", [128, 2, GT])
        stk = sb("stk", [96, GT], BF16)

        arena = sb("arena", [128, N, GT])
        consts = sb("consts", [128, 4])
        nhalf = sb("nhalf", [TT, J])
        ones = sb("ones", [128, 128])

        class Carve:

            def __init__(self, whole):
                self.whole, self.used = whole, 0

            def __call__(self, parts, shape, dt=F32):
                n = 1
                for s in shape:
                    n *= s
                words = n if dt == F32 else (n + 1) // 2
                ap = self.whole[0:parts, self.used:self.used + words]
                self.used += words
                assert self.used <= self.whole.shape[1]
                if dt != F32:
                    ap = ap.bitcast(dt)
                if len(shape) == 1:
                    return ap
                names = "abcd"[:len(shape)]
                return ap.rearrange(f"p ({' '.join(names)}) -> p {' '.join(names)}",
                                    **{names[i]: shape[i] for i in range(len(shape))})

        cb = arena
        flat = arena[:].rearrange("p n t -> p (n t)")
        cv = Carve(flat)
        x0, x0ln, x0T = cv(128, [KC, T]), cv(98, [2, D]), cv(DH, [2, T])
        wk, wq, gk = cv(DK, [NH, D]), cv(DK, [NH, D]), cv(DH, [NH, 2, D])
        wg, wgr, gate0, dec = cv(DH, [2, NH]), cv(DH, [2, NH, DH]), cv(DH, [NH, T]), cv(DH, [T])
        cv2 = Carve(mix[:].rearrange("p a c t -> p (a c t)"))
        bT, arow, x0s, x0m = cv2(DH, [2, J, NR, RB]), cv2(RB, [J, NR, D]), cv2(98, [2, 6]), cv2(98, [2, 2])
        wv, wo = cv2(DK, [NH, D]), cv2(DK, [NH, D])
        cvq = Carve(flat)
        qraw, qraw2 = cvq(DH, [2, 2 * FH]), cvq(128, [FC, D])
        qtmp = cvq(128, [2 * 2 * FH])
        cm = Carve(flat)
        hidp = cm(128, [2, GB, K - 1 + T])
        tsT, bcr, midb = cm(R, [GT]), cm(96, [GT]), cm(96, [GT], BF16)
        sp = cm(128, [2, 2, GT])
        xbt = cm(DH, [2, GB, T])
        ck = Carve(flat)
        hb, xb, ob = ck(TT, [J, D]), ck(TT, [J, D]), ck(TT, [J, D])
        qx, qT = ck(TT, [J, D], BF16), ck(DH, [2, GT], BF16)
        y2, q2 = ck(TT, [J, FH]), ck(TT, [J, FH], BF16)
        sgl, q2T = ck(TT, [2, FH]), ck(128, [2, FC, TT], BF16)

        def signal(name, *keys, credit=0):
            return Signal(sem(name), [k if isinstance(k, tuple) and k[0] == "n" else (k, 1) for k in keys], credit)

        def counted(name, *order, credit=0):
            return Signal(sem(name), list(order), credit)

        s_w = sem("weights_loaded")
        s_qw = sem("quant_weights_loaded")
        SETUP = ("x0 tok", "x0 stats", "x0 mean", "x0 var", "x0 pow", "x0 ln", "x0 turn", "x0T", "gk a", "gk a in", "a", "a in",
                 "gate rep", "gate", "gate in", "gate dec", "gk b", "gk b in", "b", "b in", "turn0", "turn0 b", "turn0 a", "turn1", "turn1 b", "turn1 a", "m") \
            + tuple(("m", j) for j in range(J)) + ("consts", "A exp", "A neg", "sums in", "sums out", "sums", "means", "floor", "inverse",
                                                   "q1", "q2", "q3", "q4", "q5", "q6", "end")
        setup = signal("setup_step", *SETUP)

        front_use = [(s, p) for s in ("tok", "tr1") for p in range(4)]
        front_use += [("sc", 0), ("sc", 1), ("ao", 0), ("sc", 2), ("ao", 1), ("sc", 3), ("ao", 2), ("ao", 3)]
        front_use += [("tr2", p) for p in range(4)]
        for p in range(4):
            front_use += [("hid", 3 * p + i) for i in range(3)] + [("fo", p)]
        front_use += [("tr3", p) for p in range(4)]
        mixer_use = [("inp", i) for i in range(6)] + [("xp", 0), ("bc", 0)] + [("dtp", c) for c in range(IC)]
        back_use = [("op", p) for p in range(4)] + [("qt", p) for p in range(4)] + [("fi", j) for j in range(J)]
        for p, (a, b) in enumerate(PAIRS):
            back_use += [("q2t", j) for j in range(a, b)] + [("out", p)]
        where, order = {}, {}
        for i, k in enumerate(front_use):
            where[k] = 6 + i % 2
        for use in (mixer_use, back_use):
            for i, k in enumerate(use):
                where[k] = i % 3
        for s in (0, 1, 2, 6, 7):
            order[s] = [k for k in front_use + mixer_use if where[k] == s] \
                + ({0: ["dA"], 1: ["B"], 2: ["y"]}.get(s, [])) + [k for k in back_use if where[k] == s]
        bank_full = {s: signal(f"psum{s}_full", *[k for k in order[s] if k not in ("dA", "B", "y")], credit="turn")
                     for s in order}

        LN = ("ln1", "ln2", "ln3")
        four = range(4)
        x_loaded = [counted(f"x_loaded{i}", *[(p, 16) for p in four if p % 2 == i]) for i in range(2)]
        h_ready = signal("h_ready", *four)
        stats_ready = signal("stats_ready", *LN, "ln4")
        coef_ready = signal("coef_ready", *LN, "ln4")
        xln_ready = signal("xln_ready", *[(n, p) for n in LN for p in four])
        xT_ready = signal("xT_ready", *[(n, p) for n in ("tr1", "tr2") for p in four], *[("tr3", j) for j in range(J)],
                          credit="turn")
        scT_ready = signal("scores_ready", *four)
        t_ready = signal("attn_sum_ready", *four)
        h1_ready = signal("h1_ready", *four)
        gT_ready = signal("gelu_ready", *range(12))
        h2_ready = signal("h2_ready", *four)
        h2_saved = counted("h2_saved", ("s", 16), credit="turn")
        hb_loaded = counted("h2_reloaded", ("s", 16))
        hid_ready = signal("hidden_ready", *range(IC))
        conv_step = signal("conv_step", "pad", *[(c, k) for c in range(IC) for k in four])
        hh_ready = signal("h_silu_ready", *range(IC))
        sg_ready = signal("gate_silu_ready", *range(IC))
        ts_ready = signal("ts_ready", 0)
        bc_step = signal("bc_split_step", *range(5))
        sp_step = signal("softplus_step", *[(c, k) for c in range(IC) for k in four])
        dt_ready = signal("dt_sum_ready", *range(IC))
        u_step = signal("u_step", *[(c, k) for c in range(IC) for k in range(2)])
        dA_zero = signal("dA_zeroed", 0)
        dA_full = [counted(f"dA_full{q}", *[(c, N) for c in range(IC)]) for q in range(2)]
        bc_full = counted("spread_full", (0, 2 * N), (1, N), (2, N))
        dbu_ready = counted("dbu_ready", *[(c, N) for c in range(IC)])
        st_ready = [counted(f"state_ready{q}", *[(c, N) for c in range(IC)], credit=1) for q in range(2)]
        cb_ready = counted("c_spread_ready", ("c", N))
        cs_ready = counted("c_state_ready", *[(c, N) for c in range(IC)])
        cs_used = counted("c_state_summed", *[(c, N) for c in range(IC)], credit=2)
        ysum_ready = signal("y_sum_ready", *range(IC))
        yg_step = signal("y_gated_step", *[(c, k) for c in range(IC) for k in range(2)])
        h3_ready = signal("h3_ready", *four)
        xb_ready = signal("xb_ready", 0)
        xg_ready = signal("x_gained", 0)
        peak_ready = signal("peak_ready", *range(1 + J))
        rcp_ready = signal("reciprocal_ready", 1, 2)
        floor_ready = signal("floor_ready", 1, 2)
        scale_ready = signal("scale_ready", 1, 2)
        qr_ready = signal("q_rounded", 0)
        qx_ready = signal("qx_ready", 0)
        qT_ready = signal("qT_ready", *four)
        sgl_ready = signal("silu_gate_ready", *range(J))
        y2_ready = signal("y2_ready", *range(J))
        ss_ready = signal("square_sum_ready", *range(J))
        r2_ready = signal("y2_gained", *range(J))
        q2r_ready = signal("q2_rounded", *range(J))
        q2_ready = signal("q2_ready", *range(J))
        q2T_ready = signal("q2T_ready", *range(J), credit="turn")
        o_ready = signal("o_ready", *range(J), credit="turn")
        stored = counted("stored", ("s", 16), credit="turn")
        POOL_LINKS = 32
        pool_link = sem("pool_link")

        credited = [s for s in (*bank_full.values(), xT_ready, h2_saved, *st_ready, cs_used, o_ready, q2T_ready, stored)]

        reader = {}
        for p, (a, b) in enumerate(PAIRS):
            reader[("tok", p)] = (h_ready, p)
            reader[("tr1", p)], reader[("tr2", p)] = (xT_ready, ("tr1", p)), (xT_ready, ("tr2", p))
            reader[("tr3", p)] = (xT_ready, ("tr3", b - 1))
            reader[("sc", p)], reader[("ao", p)], reader[("fo", p)] = (scT_ready, p), (t_ready, p), (h2_ready, p)
            for i in range(3):
                reader[("hid", 3 * p + i)] = (gT_ready, 3 * p + i)
            reader[("op", p)], reader[("qt", p)], reader[("out", p)] = (h3_ready, p), (qT_ready, p), (o_ready, b - 1)
        for c in range(IC):
            reader[("inp", c)], reader[("inp", IC + c)] = (hid_ready, c), (sg_ready, c)
            reader[("dtp", c)] = (sp_step, (c, 1))
        reader[("xp", 0)], reader[("bc", 0)] = (ts_ready, 0), (bc_step, 1)
        for j in range(J):
            reader[("fi", j)], reader[("q2t", j)] = (y2_ready, j), (q2T_ready, j)
        reader["dA"], reader["B"], reader["y"] = (st_ready[1], IC - 1, N - 1), (dbu_ready, IC - 1, N - 1), (ysum_ready, IC - 1)

        def filled(g, k):
            return bank_full[where[k]].at(g, k)

        def emptied(g, k, s=None):
            uses = order[where[k] if s is None else s]
            i = uses.index(k)
            sig, *key = reader[uses[i - 1]]
            return sig.at(g, *key) if i else sig.last_turn(g, *key)

        def full_of(k):
            return bank_full[where[k]].sem

        def ps(k):
            s = where[k]
            return bank[:, s, :] if s > 5 else bank[:, 2 * s:2 * s + 2, :]

        STAT = range(14)
        MEAN2, DIFF, VAR, RSTD, MEAN, RINV, PEAK, QS, SC, SS, T1, T2, RINV2, QS2 = STAT
        PEAK2, SC2 = 14, 15

        def col(i):
            return small[:, i, :]

        def one(i, j):
            return small[:, i, j:j + 1]

        loads = [(ident, ident_c), (identb, identb_c), (mask, mask_c), (decp, decp_c), (sel, sel_c), (wtok, w_tok),
                 (wfi, ffn_in), (wfo, ffn_out), (winp, w_inp), (wxp, w_xp), (wbc, w_bc), (wdt, w_dt),
                 (wop, w_op), (cw, conv_w), (amat, a_log)]
        loads = [(dst[:], src) for dst, src in loads]
        loads += [(gin[:], g_in.partition_broadcast(TT)), (gout[:], g_out.partition_broadcast(TT))]
        loads += [(cvec[:, i, :], v) for i, v in enumerate((conv_b, b_dt, d_skip, alpha, fgate))]
        loads += [(x0, x0t), (wk, w_key), (wq, w_query), (wv, w_value), (wo, w_outt), (wg, w_gate), (dec, dec_c)]
        W_ALL = 16 * len(loads)
        block = ctx.enter_context(nc.Block())

        @block.sync
        def _(sp):
            for dst, src in loads:
                sp.dma_start(dst, src).then_inc(s_w, 16)
            sp.wait_ge(*setup.at(0, ("m", J - 1)))
            sp.dma_start(qraw, q_in).then_inc(s_qw, 16)
            sp.dma_start(qraw2, q_out).then_inc(s_qw, 16)
            with sp.Fori(0, NG) as g:
                for p, (a, b) in enumerate(PAIRS):
                    prev = ("tok", (p + 2) % 4)
                    sig = bank_full[where[prev]]
                    if p >= 2:
                        sp.wait_ge(*sig.at(g, prev))
                    else:
                        sp.wait_ge(*sig.last_turn(g, prev))
                    sp.nop(nofuse=True)
                    sp.dma_start(xst[:, 2 * (p % 2):2 * (p % 2) + b - a], xt[g, :, a:b]).then_inc(x_loaded[p % 2].sem, 16)
                sp.wait_ge(*h2_ready.at(g, 3))
                sp.nop(nofuse=True)
                sp.dma_start(saved[g], h[:]).then_inc(h2_saved.sem, 16)
                sp.wait_ge(*h2_saved.at(g, "s", 15))
                sp.wait_ge(*cs_ready.at(g, IC - 1, N - 1))
                sp.nop(nofuse=True)
                sp.dma_start(hb, saved[g]).then_inc(hb_loaded.sem, 16)
                sp.wait_ge(*o_ready.at(g, J - 1))
                sp.nop(nofuse=True)
                sp.dma_start(out[g], ob).then_inc(stored.sem, 16)
            sp.wait_ge(stored.sem, 16 * (NG + 1))

        @block.tensor
        def _(pe):
            pe.wait_ge(s_w, W_ALL)
            for t in range(2):
                for k in range(KC):
                    mm = pe.matmul(bank[0:98, t, 0:D], x0[:, k, t * 98:(t + 1) * 98], wtok[:, k, :], start=k == 0, stop=k == KC - 1)
            mm.then_inc(setup.sem, 1)
            pe.wait_ge(*setup.at(0, "x0 ln"))
            for t in range(2):
                for e in range(2):
                    mm = pe.transpose(bank[0:DH, 2, e * T + t * 98:e * T + (t + 1) * 98], x0ln[:, t, e * DH:(e + 1) * DH], ident[0:98, 0:98])
            mm.then_inc(setup.sem, 1)
            for side, (left, right, made) in enumerate(((wk, wq, "x0T"), (wv, wo, "gate dec"))):
                pe.wait_ge(*setup.at(0, made))
                for hd in range(NH):
                    for e in range(2):
                        mm = pe.matmul(bank[0:DH, hd, e * D:(e + 1) * D], left[:, hd, e * DH:(e + 1) * DH], right[:, hd, :], start=True, stop=True)
                mm.then_inc(setup.sem, 1)
                pe.wait_ge(*setup.at(0, ("gk a in", "gk b in")[side]))
                for hd in range(NH):
                    for d in range(2):
                        for e in range(2):
                            mm = pe.matmul(bank[0:DH, hd, d * T:(d + 1) * T], gk[:, hd, e, d * DH:(d + 1) * DH], x0T[:, e, :], start=e == 0, stop=e == 1)
                mm.then_inc(setup.sem, 1)
                if side == 0:
                    pe.wait_ge(*setup.at(0, "gate rep"))
                    for hd in range(NH):
                        for e in range(2):
                            mm = pe.matmul(bank[0:DH, hd, 0:T], wgr[:, e, hd, :], x0T[:, e, :], start=e == 0, stop=e == 1)
                    mm.then_inc(setup.sem, 1)
            for half in range(2):
                pe.wait_ge(*setup.at(0, ("b in", "turn0 a")[half]))
                for i in range(7):
                    jj, r = divmod(half * 7 + i, NR)
                    for d in range(2):
                        pe.transpose(bank[0:RB, i, d * DH:(d + 1) * DH], amask[:, d, jj, r, :], ident[0:DH, 0:DH])
                        mm = pe.transpose(bank[0:RB, i, D + d * DH:D + (d + 1) * DH], bT[:, d, jj, r, :], ident[0:DH, 0:DH])
                mm.then_inc(setup.sem, 1)
            pe.wait_ge(*setup.at(0, "turn1 a"))
            for j in range(J - 1):
                for d in range(2):
                    for r in range(NR):
                        mm = pe.matmul(bank[0:DH, j, d * D:(d + 1) * D], arow[:, j, r, d * DH:(d + 1) * DH], bmat[:, j, r, :],
                                       start=r == 0, stop=r == NR - 1)
            mm.then_inc(setup.sem, 1)
            pe.wait_ge(*setup.at(0, "sums out"))
            pe.matmul(bank[:, 0, 0:1], ones[0:DH, :], wsc[0:DH, 0:1], start=True, stop=True)
            pe.matmul(bank[:, 0, 1:2], ones[:, :], wsc[:, 1:2], start=True, stop=True).then_inc(setup.sem, 1)
            pe.wait_ge(*setup.at(0, "end"))

            def transposes(g, name, p, ln):
                a, b = PAIRS[p]
                pe.wait_ge(*emptied(g, (name, p)))
                pe.wait_ge(*xln_ready.at(g, (ln, p)))
                for e in range(2):
                    for j in range(a, b):
                        mm = pe.transpose(ps((name, p))[0:DH, e * (b - a) * TT + (j - a) * TT:e * (b - a) * TT + (j - a + 1) * TT],
                                          xln[:, j, e * DH:(e + 1) * DH], ident[0:TT, 0:TT])
                mm.then_inc(full_of((name, p)), 1)

            def attn_out(g, p):
                a, b = PAIRS[p]
                pe.wait_ge(*emptied(g, ("ao", p)))
                pe.wait_ge(*scT_ready.at(g, p))
                for j in range(a, b):
                    o = ps(("ao", p))[0:TT, (j - a) * D:(j - a + 1) * D]
                    for r in range(NR):
                        mm = pe.matmul(o, scT[:, p % 2, j - a, r, :], bmat[:, j, r, :], start=r == 0, stop=j == 0 and r == NR - 1)
                    if j:
                        for e in range(2):
                            mm = pe.matmul(o, xT[0:DH, e, j * TT:(j + 1) * TT], mmat[:, j, e, :], start=False, stop=e == 1)
                mm.then_inc(full_of(("ao", p)), 1)

            with pe.Fori(0, NG) as g:
                for p, (a, b) in enumerate(PAIRS):
                    pe.wait_ge(*emptied(g, ("tok", p)))
                    pe.wait_ge(*x_loaded[p % 2].at(g, p, 15))
                    for j in range(a, b):
                        for k in range(KC):
                            mm = pe.matmul(ps(("tok", p))[0:TT, (j - a) * D:(j - a + 1) * D], xst[:, 2 * (p % 2) + j - a, k, :],
                                           wtok[:, k, :], start=k == 0, stop=k == KC - 1)
                    mm.then_inc(full_of(("tok", p)), 1)
                for p in range(4):
                    transposes(g, "tr1", p, "ln1")
                for p, (a, b) in enumerate(PAIRS):
                    pe.wait_ge(*emptied(g, ("sc", p)))
                    pe.wait_ge(*xT_ready.at(g, ("tr1", p)))
                    for j in range(a, b):
                        for r in range(NR):
                            c0 = ((j - a) * NR + r) * TT
                            for e in range(2):
                                mm = pe.matmul(ps(("sc", p))[0:RB, c0:c0 + TT], amask[:, e, j, r, :], xT[0:DH, e, j * TT:(j + 1) * TT],
                                               start=e == 0, stop=e == 1)
                    mm.then_inc(full_of(("sc", p)), 1)
                    if p:
                        attn_out(g, p - 1)
                attn_out(g, 3)
                for p in range(4):
                    transposes(g, "tr2", p, "ln2")
                for p, (a, b) in enumerate(PAIRS):
                    w = (b - a) * TT
                    for i in range(3):
                        pe.wait_ge(*emptied(g, ("hid", 3 * p + i)))
                        pe.wait_ge(*xT_ready.at(g, ("tr2", p)))
                        for m in range(2):
                            hc = 2 * i + m
                            for e in range(2):
                                kk = DH + e
                                mm = pe.matmul(ps(("hid", 3 * p + i))[:, m * w:(m + 1) * w], wfi[0:kk, e, hc * 128:(hc + 1) * 128],
                                               xT[0:kk, e, a * TT:b * TT], start=e == 0, stop=e == 1)
                        mm.then_inc(full_of(("hid", 3 * p + i)), 1)
                    pe.wait_ge(*emptied(g, ("fo", p)))
                    pe.wait_ge(*gT_ready.at(g, 3 * p + 2))
                    for j in range(a, b):
                        for hc in range(HC):
                            mm = pe.matmul(ps(("fo", p))[0:TT, (j - a) * D:(j - a + 1) * D], gT[:, hc, (j - a) * TT:(j - a + 1) * TT],
                                           wfo[:, hc, :], start=hc == 0, stop=hc == HC - 1)
                    mm.then_inc(full_of(("fo", p)), 1)
                for p in range(4):
                    transposes(g, "tr3", p, "ln3")
                xf = xbt[:].rearrange("p e b t -> p e (b t)")
                for i in range(6):
                    pe.wait_ge(*emptied(g, ("inp", i)))
                    pe.wait_ge(*xT_ready.at(g, ("tr3", J - 1)))
                    for q in range(2):
                        for e in range(2):
                            mm = pe.matmul(ps(("inp", i))[:, q, 0:HB], winp[:, e, i * 128:(i + 1) * 128], xf[:, e, q * HB:(q + 1) * HB],
                                           start=e == 0, stop=e == 1)
                    mm.then_inc(full_of(("inp", i)), 1)
                for name, w, m in (("xp", wxp, R), ("bc", wbc, 96)):
                    pe.wait_ge(*emptied(g, (name, 0)))
                    pe.wait_ge(*hh_ready.at(g, IC - 1))
                    for q in range(2):
                        for c in range(IC):
                            mm = pe.matmul(ps((name, 0))[0:m, q, 0:HB], w[:, c, :], hh[:, c, q * HB:(q + 1) * HB], start=c == 0, stop=c == IC - 1)
                    mm.then_inc(full_of((name, 0)), 1)
                for c in range(IC):
                    pe.wait_ge(*emptied(g, ("dtp", c)))
                    pe.wait_ge(*ts_ready.at(g, 0))
                    for q in range(2):
                        mm = pe.matmul(ps(("dtp", c))[:, q, 0:HB], wdt[:, c * 128:(c + 1) * 128], tsT[:, q * HB:(q + 1) * HB], start=True, stop=True)
                    mm.then_inc(full_of(("dtp", c)), 1)

                pe.wait_ge(*bc_step.at(g, 4))
                pe.wait_ge(*emptied(g, "B", 1))

                def spread(c, n):
                    if c == 0:
                        if not isinstance(n, int) or n:
                            pe.wait_ge(*cb_ready.at(g, "c", n - 1))
                    else:
                        pe.wait_ge(*dbu_ready.at(g, c, n - 1))
                    for q in range(2):
                        mm = pe.matmul(bank[:, 2 + q, 0:HB], pick(n), stk[:, q * HB:(q + 1) * HB], start=True, stop=True)
                    mm.then_inc(bc_full.sem, 1)
                    if c == 0:
                        pe.wait_ge(*dbu_ready.at(g, c, n))
                        for q in range(2):
                            mm = pe.matmul(bank[:, 2 + q, 0:HB], pick(n + N), stk[:, q * HB:(q + 1) * HB], start=True, stop=True)
                        mm.then_inc(bc_full.sem, 1)

                def pick(n):
                    return sel[:, bass.ds(n, 1)].to_broadcast([96, 128])

                def sum_state(c, n, par, first=False, last=False):
                    pe.wait_ge(*cs_ready.at(g, c, n))
                    for q in range(2):
                        mm = pe.matmul(bank[:, 4 + q, 0:HB], ident[:, :], st[:, par, q * HB:(q + 1) * HB], start=first, stop=last,
                                       skip_group_check=True)
                    mm.then_inc(cs_used.sem, 1)

                for c in range(IC):
                    spread(c, 0)
                    if c == 0:
                        pe.wait_ge(*emptied(g, "y", 2))
                    else:
                        pe.wait_ge(*ysum_ready.at(g, c - 1))
                    spread(c, 1)
                    sum_state(c, 0, 0, first=True)
                    with pe.Fori(0, (N - 2) // 2) as m:
                        for i in range(2):
                            spread(c, 2 * m + (2 + i))
                            sum_state(c, 2 * m + (1 + i), 1 - i)
                    sum_state(c, N - 1, 1, last=True)

                for p, (a, b) in enumerate(PAIRS):
                    pe.wait_ge(*emptied(g, ("op", p)))
                    pe.wait_ge(*yg_step.at(g, (IC - 1, 1)))
                    for j in range(a, b):
                        for c in range(IC):
                            mm = pe.matmul(ps(("op", p))[0:TT, 0, (j - a) * D:(j - a + 1) * D], hh[:, c, j * TT:(j + 1) * TT], wop[:, c, :], start=c == 0, stop=c == IC - 1)
                    mm.then_inc(full_of(("op", p)), 1)
                for p, (a, b) in enumerate(PAIRS):
                    pe.wait_ge(*emptied(g, ("qt", p)))
                    pe.wait_ge(*qx_ready.at(g, 0))
                    pb = ps(("qt", p))[0:DH, 0, :].bitcast(BF16)
                    for e in range(2):
                        for j in range(a, b):
                            o = e * 2 * TT + (j - a) * TT
                            mm = pe.transpose(pb[:, o:o + TT], qx[:, j, e * DH:(e + 1) * DH], identb[0:TT, 0:TT])
                    mm.then_inc(full_of(("qt", p)), 1)
                for j in range(J):
                    pe.wait_ge(*emptied(g, ("fi", j)))
                    pe.wait_ge(*qT_ready.at(g, j // 2))
                    for half in range(2):
                        for e in range(2):
                            mm = pe.matmul(ps(("fi", j))[0:TT, half, :], qT[:, e, j * TT:(j + 1) * TT], qwi[:, e, half * FH:(half + 1) * FH],
                                           start=e == 0, stop=e == 1)
                    mm.then_inc(full_of(("fi", j)), 1)

                def q2_transposes(j):
                    pe.wait_ge(*emptied(g, ("q2t", j)))
                    pe.wait_ge(*q2_ready.at(g, j))
                    pb = ps(("q2t", j))[:, 0, :].bitcast(BF16)
                    for f in range(FC):
                        mm = pe.transpose(pb[:, f * TT:(f + 1) * TT], q2[:, j, f * 128:(f + 1) * 128], identb[0:TT, 0:TT])
                    mm.then_inc(full_of(("q2t", j)), 1)

                def last_products(p):
                    a, b = PAIRS[p]
                    pe.wait_ge(*emptied(g, ("out", p)))
                    pe.wait_ge(*q2T_ready.at(g, b - 1))
                    for j in range(a, b):
                        for f in range(FC):
                            mm = pe.matmul(ps(("out", p))[0:TT, 0, (j - a) * D:(j - a + 1) * D], q2T[:, j % 2, f, :], qwo[:, f, :],
                                           start=f == 0, stop=f == FC - 1)
                    mm.then_inc(full_of(("out", p)), 1)

                for p, (a, b) in enumerate(PAIRS):
                    for j in range(a, b):
                        q2_transposes(j)
                    last_products(p)

        @block.scalar
        def _(act):
            act.wait_ge(*setup.at(0, "x0 turn"))
            act.activation(x0T.rearrange("p e t -> p (e t)"), bank[0:DH, 2, 0:2 * T], ACT.Copy).then_inc(setup.sem, 1)
            act.wait_ge(*setup.at(0, "gate"))
            act.activation(gate0, bank[0:DH, :, 0:T], ACT.Sigmoid).then_inc(setup.sem, 1)
            for half in range(2):
                act.wait_ge(*setup.at(0, ("turn0 b", "turn1 b")[half]))
                act.activation(arow.rearrange("p j r d -> p (j r) d")[:, half * 7:half * 7 + 7], bank[0:RB, 0:7, 0:D],
                               ACT.Copy, scale=DECAY ** TC).then_inc(setup.sem, 1)
            act.wait_ge(*setup.at(0, "consts"))
            act.activation(amat[:], amat[:], ACT.Exp).then_inc(setup.sem, 1)
            act.wait_ge(s_qw, 32)
            act.wait_ge(*setup.at(0, "A exp"))
            act.activation(amat[:], amat[:], ACT.Copy, scale=-1.0).then_inc(setup.sem, 1)
            qi, qo = qraw.rearrange("p e f -> p (e f)"), qraw2.rearrange("p f d -> p (f d)")
            act.wait_ge(*setup.at(0, "A neg"))
            act.activation(qtmp[0:DH, :], qi, ACT.Abs, accum_out=wsc[0:DH, 0:1]).then_inc(setup.sem, 1)
            act.wait_ge(*setup.at(0, "sums in"))
            act.activation(qtmp[:, 0:FC * D], qo, ACT.Abs, accum_out=wsc[:, 1:2]).then_inc(setup.sem, 1)
            act.wait_ge(*setup.at(0, "end"))

            def turned(g, name, p):
                a, b = PAIRS[p]
                w = (b - a) * TT
                act.wait_ge(*filled(g, (name, p)))
                act.activation(xT[0:DH, :, a * TT:b * TT], ps((name, p))[0:DH, 0:2 * w].rearrange("p (e w) -> p e w", e=2),
                               ACT.Copy).then_inc(xT_ready.sem, 1)

            def decay_factor(g, c, n):
                for q in range(2):
                    act.wait_ge(*st_ready[q].at(g, c, n - 1))
                    act.nop(nofuse=True)
                    act.activation(bank[:, q, 0:HB].rearrange("p (b t) -> p b t", t=T)[:, :, 1:T],
                                   dt[:, c, q * HB:(q + 1) * HB].rearrange("p (b t) -> p b t", t=T)[:, :, 1:T],
                                   ACT.Exp, scale=amat[:, c, bass.ds(n, 1)]).then_inc(dA_full[q].sem, 1)

            with act.Fori(0, NG) as g:
                for p, (a, b) in enumerate(PAIRS):
                    act.wait_ge(*filled(g, ("tok", p)))
                    if p == 0:
                        act.wait_ge(*h2_saved.last_turn(g, "s", 15))
                    act.activation(h[:, a:b, :], ps(("tok", p))[0:TT, 0:(b - a) * D].rearrange("p (j d) -> p j d", d=D),
                                   ACT.Copy).then_inc(h_ready.sem, 1)
                for name in ("tr1", "tr2"):
                    for p in range(4):
                        turned(g, name, p)
                for p, (a, b) in enumerate(PAIRS):
                    w = (b - a) * TT
                    for i in range(3):
                        act.wait_ge(*filled(g, ("hid", 3 * p + i)))
                        if p and i == 0:
                            act.wait_ge(*filled(g, ("fo", p - 1)))
                        act.activation(gT[:, 2 * i:2 * i + 2, 0:w], ps(("hid", 3 * p + i))[:, 0:2 * w].rearrange("p (m w) -> p m w", m=2),
                                       ACT.Gelu).then_inc(gT_ready.sem, 1)
                for p, (a, b) in enumerate(PAIRS):
                    act.wait_ge(*filled(g, ("tr3", p)))
                    if p == 0:
                        act.wait_ge(*stored.last_turn(g, "s", 15))
                    for j in range(a, b):
                        src = ps(("tr3", p))[0:DH, 0:2 * (b - a) * TT].rearrange("p (e j b t) -> p e j b t", e=2, j=b - a, b=GB)
                        act.activation(xbt[:, :, :, j * TC:(j + 1) * TC], src[:, :, j - a], ACT.Copy).then_inc(xT_ready.sem, 1)
                for c in range(IC):
                    act.wait_ge(*filled(g, ("inp", c)))
                    if c < 2:
                        act.wait_ge(*conv_step.at(g, "pad"))
                    else:
                        act.wait_ge(*conv_step.at(g, (c - 2, 3)))
                    act.activation(hidp[:, c % 2, :, K - 1:].rearrange("p (q b) t -> p q b t", q=2),
                                   ps(("inp", c))[:, :, 0:HB].rearrange("p q (b t) -> p q b t", t=T), ACT.Copy).then_inc(hid_ready.sem, 1)
                for c in range(IC):
                    act.wait_ge(*filled(g, ("inp", IC + c)))
                    act.activation(sg[:, c, :].rearrange("p (q t) -> p q t", q=2), ps(("inp", IC + c))[:, :, 0:HB],
                                   ACT.Silu).then_inc(sg_ready.sem, 1)
                    act.wait_ge(*conv_step.at(g, (c, 3)))
                    act.activation(hh[:, c, :], hh[:, c, :], ACT.Silu).then_inc(hh_ready.sem, 1)
                act.wait_ge(*filled(g, ("xp", 0)))
                act.activation(tsT.rearrange("p (q t) -> p q t", q=2), ps(("xp", 0))[0:R, :, 0:HB], ACT.Copy).then_inc(ts_ready.sem, 1)
                for c in range(IC):
                    act.wait_ge(*filled(g, ("dtp", c)))
                    if c >= 2:
                        act.wait_ge(*dt_ready.at(g, c - 2))
                    x, e = sp[:, c % 2, 0, :], sp[:, c % 2, 1, :]
                    src = ps(("dtp", c))[:, :, 0:HB]
                    act.activation(x.rearrange("p (q t) -> p q t", q=2), src, ACT.Identity, bias=cvec[:, 1, c:c + 1]).then_inc(sp_step.sem, 1)
                    act.activation(e.rearrange("p (q t) -> p q t", q=2), src, ACT.Abs, bias=cvec[:, 1, c:c + 1]).then_inc(sp_step.sem, 1)
                    act.wait_ge(*sp_step.at(g, (c, 1)))
                    act.activation(e, e, ACT.Exp, scale=-1.0).then_inc(sp_step.sem, 1)
                    act.wait_ge(*sp_step.at(g, (c, 2)))
                    act.activation(e, e, ACT.Ln, bias=1.0).then_inc(sp_step.sem, 1)
                act.wait_ge(*dA_zero.at(g, 0))
                act.wait_ge(*dt_ready.at(g, IC - 1))
                act.wait_ge(*u_step.at(g, (IC - 1, 1)))
                def copy_c(n):
                    act.wait_ge(*bc_full.at(g, 0, 2 * n + 1))
                    act.nop(nofuse=True)
                    act.activation(cb[:, bass.ds(n, 1), :].rearrange("p n (q t) -> p (n q) t", q=2), bank[:, 2:4, 0:HB],
                                   ACT.Copy).then_inc(cb_ready.sem, 1)

                decay_factor(g, 0, 0)
                with act.Fori(0, N - 1) as n:
                    copy_c(n)
                    decay_factor(g, 0, n + 1)
                copy_c(N - 1)
                for c in range(1, IC):
                    with act.Fori(0, N) as n:
                        decay_factor(g, c, n)
                for p, (a, b) in enumerate(PAIRS):
                    act.wait_ge(*filled(g, ("qt", p)))
                    pb = ps(("qt", p))[0:DH, 0, :].bitcast(BF16)[:, 0:4 * TT].rearrange("p (e w) -> p e w", e=2)
                    act.activation(qT[:, :, a * TT:b * TT], pb[:, :, 0:(b - a) * TT], ACT.Copy).then_inc(qT_ready.sem, 1)

                def squares(j):
                    act.wait_ge(*y2_ready.at(g, j))
                    act.activation(sgl[:, j % 2, :], y2[:, j, :], ACT.Square, accum_out=one(SS, j)).then_inc(ss_ready.sem, 1)

                for j in range(J):
                    act.wait_ge(*filled(g, ("fi", j)))
                    act.wait_ge(*scale_ready.at(g, 1))
                    if j >= 2:
                        act.wait_ge(*ss_ready.at(g, j - 2))
                    act.activation(sgl[:, j % 2, :], ps(("fi", j))[0:TT, 1, :], ACT.Silu, scale=one(SC, j)).then_inc(sgl_ready.sem, 1)
                    if j:
                        squares(j - 1)
                squares(J - 1)
                act.wait_ge(*scale_ready.at(g, 2))
                for j in range(J):
                    act.activation(y2[:, j, :], y2[:, j, :], ACT.Identity, scale=one(QS2, j), bias=consts[0:TT, 1:2]).then_inc(q2r_ready.sem, 1)
                for p, (a, b) in enumerate(PAIRS):
                    for j in range(a, b):
                        act.wait_ge(*filled(g, ("q2t", j)))
                        if p:
                            act.wait_ge(*filled(g, ("out", p - 1)))
                        act.activation(q2T[:, j % 2].rearrange("p f t -> p (f t)"),
                                       ps(("q2t", j))[:, 0, :].bitcast(BF16)[:, 0:FC * TT], ACT.Copy).then_inc(q2T_ready.sem, 1)

        @block.vector
        def _(dve):
            dve.wait_ge(*setup.at(0, "x0 tok"))
            for t in range(2):
                ins = dve.bn_stats(x0s[:, t, :], bank[0:98, t, 0:D])
            ins.then_inc(setup.sem, 1)
            dve.wait_ge(*setup.at(0, "x0 stats"))
            for t in range(2):
                ins = dve.bn_aggr(x0m[:, t, :], x0s[:, t, :])
            ins.then_inc(setup.sem, 1)
            dve.wait_ge(*setup.at(0, "x0 pow"))
            for t in range(2):
                ins = dve.tensor_scalar(x0ln[:, t, :], bank[0:98, t, 0:D], x0m[:, t, 0:1], x0m[:, t, 1:2], ALU.subtract, ALU.mult)
            ins.then_inc(setup.sem, 1)
            dve.wait_ge(*setup.at(0, "gk a"))
            dve.tensor_copy(gk.rearrange("p h e d -> p h (e d)"), bank[0:DH, :, 0:2 * D]).then_inc(setup.sem, 1)
            dve.wait_ge(*setup.at(0, "a"))
            for hd in range(NH):
                for d in range(2):
                    ins = dve.tensor_copy(amask[:, d].rearrange("p j r (h s) -> p h (j r) s", h=NH)[:, hd],
                                          bank[0:DH, hd, d * T:(d + 1) * T].rearrange("p (a s) -> p a s", s=TS))
            ins.then_inc(setup.sem, 1)
            dve.wait_ge(*setup.at(0, "a in"))
            dve.tensor_copy(wgr, wg.unsqueeze(3).to_broadcast([DH, 2, NH, DH])).then_inc(setup.sem, 1)
            dve.wait_ge(*setup.at(0, "gate in"))
            for hd in range(NH):
                ins = dve.tensor_tensor(gate0[:, hd, :], gate0[:, hd, :], dec, ALU.mult)
            ins.then_inc(setup.sem, 1)
            dve.wait_ge(*setup.at(0, "gk b"))
            dve.tensor_copy(gk.rearrange("p h e d -> p h (e d)"), bank[0:DH, :, 0:2 * D]).then_inc(setup.sem, 1)
            dve.wait_ge(*setup.at(0, "b"))
            for hd in range(NH):
                for d in range(2):
                    ins = dve.tensor_tensor(bT[:, d].rearrange("p j r (h s) -> p h (j r) s", h=NH)[:, hd],
                                            bank[0:DH, hd, d * T:(d + 1) * T].rearrange("p (a s) -> p a s", s=TS),
                                            gate0[:, hd, :].rearrange("p (a s) -> p a s", s=TS), ALU.mult)
            ins.then_inc(setup.sem, 1)
            for half in range(2):
                dve.wait_ge(*setup.at(0, ("turn0", "turn1")[half]))
                dve.tensor_copy(bmat[:].rearrange("p j r d -> p (j r) d")[:, half * 7:half * 7 + 7], bank[0:RB, 0:7, D:2 * D]).then_inc(setup.sem, 1)
            dve.wait_ge(*setup.at(0, "m"))
            dve.memset(mmat[:, 0], 0.0).then_inc(setup.sem, 1)
            for j in range(1, J):
                dve.wait_ge(*setup.at(0, ("m", j - 1)))
                dve.scalar_tensor_tensor(mmat[:, j].rearrange("p e d -> p (e d)"), mmat[:, j - 1].rearrange("p e d -> p (e d)"),
                                              DECAY ** TC, bank[0:DH, j - 1, 0:2 * D], ALU.mult, ALU.add).then_inc(setup.sem, 1)
            dve.wait_ge(*setup.at(0, ("m", J - 1)))
            dve.memset(ones[:], 1.0)
            dve.memset(nhalf[:], -0.5)
            dve.memset(consts[:], MAGIC)
            dve.memset(xT[DH:DH + 1, 1, :], 1.0).then_inc(setup.sem, 1)
            dve.wait_ge(*setup.at(0, "sums"))
            dve.tensor_scalar(wsc[:, 2:3], bank[:, 0, 0:1], 1.0 / (2 * FH * D), None, ALU.mult)
            dve.tensor_scalar(wsc[:, 3:4], bank[:, 0, 1:2], 1.0 / (FH * D), None, ALU.mult).then_inc(setup.sem, 1)
            dve.wait_ge(*setup.at(0, "means"))
            dve.tensor_scalar(wsc[:, 4:6], wsc[:, 2:4], Q_EPS, None, ALU.max).then_inc(setup.sem, 1)
            dve.wait_ge(*setup.at(0, "floor"))
            dve.reciprocal(wsc[:, 6:8], wsc[:, 4:6]).then_inc(setup.sem, 1)
            prev = "inverse"
            for i, (parts, raw, whole) in enumerate(((DH, qraw.rearrange("p e f -> p (e f)"), qwi[:].rearrange("p e f -> p (e f)")),
                                                     (128, qraw2.rearrange("p f d -> p (f d)"), qwo[:].rearrange("p f d -> p (f d)")))):
                tmp = qtmp[0:parts, 0:raw.shape[1]]
                dve.wait_ge(*setup.at(0, prev))
                dve.tensor_scalar(tmp, raw, wsc[0:parts, 6 + i:7 + i], MAGIC, ALU.mult, ALU.add).then_inc(setup.sem, 1)
                dve.wait_ge(*setup.at(0, f"q{3 * i + 1}"))
                dve.tensor_scalar(tmp, tmp, MAGIC, 1.0, ALU.subtract, ALU.min).then_inc(setup.sem, 1)
                dve.wait_ge(*setup.at(0, f"q{3 * i + 2}"))
                dve.tensor_scalar(whole, tmp, -1.0, None, ALU.max).then_inc(setup.sem, 1)
                prev = f"q{3 * i + 3}"
            dve.wait_ge(*setup.at(0, prev))
            dve.memset(xT[DH:DH + 1, 1, :], 1.0).then_inc(setup.sem, 1)
            dve.wait_ge(*setup.at(0, "end"))

            def stats_of(g, src, ready, key):
                for p, (a, b) in enumerate(PAIRS):
                    dve.wait_ge(*ready.at(g, p))
                    for j in range(a, b):
                        ins = dve.bn_stats(stats[:, j, :], src[:, j, :])
                ins.then_inc(stats_ready.sem, 1)

            def normed(g, key):
                stats_of(g, h, {"ln1": h_ready, "ln2": h1_ready, "ln3": h2_ready}[key], key)
                dve.wait_ge(*coef_ready.at(g, key))
                for p, (a, b) in enumerate(PAIRS):
                    for j in range(a, b):
                        ins = dve.tensor_scalar(xln[:, j, :], h[:, j, :], one(MEAN, j), one(RSTD, j), ALU.subtract, ALU.mult)
                    ins.then_inc(xln_ready.sem, 1)

            with dve.Fori(0, NG) as g:
                normed(g, "ln1")

                def attn_sum(p):
                    a, b = PAIRS[p]
                    dve.wait_ge(*filled(g, ("ao", p)))
                    dve.scalar_tensor_tensor(xln[:, a:b, :].rearrange("p j d -> p (j d)"), ps(("ao", p))[0:TT, 0:(b - a) * D],
                                             decp[:, 0:1], xln[:, a:b, :].rearrange("p j d -> p (j d)"),
                                             ALU.mult, ALU.add).then_inc(t_ready.sem, 1)

                for p, (a, b) in enumerate(PAIRS):
                    dve.wait_ge(*filled(g, ("sc", p)))
                    if p >= 2:
                        dve.wait_ge(*filled(g, ("ao", p - 2)))
                    w = (b - a) * NR * TT
                    dve.tensor_tensor(scT[:, p % 2].rearrange("p j r t -> p (j r t)")[:, 0:w], ps(("sc", p))[0:RB, 0:w],
                                      mask[:, 0:w], ALU.mult).then_inc(scT_ready.sem, 1)
                    if p:
                        attn_sum(p - 1)
                attn_sum(3)
                normed(g, "ln2")
                for p, (a, b) in enumerate(PAIRS):
                    dve.wait_ge(*filled(g, ("fo", p)))
                    hp = h[:, a:b, :].rearrange("p j d -> p (j d)")
                    dve.tensor_tensor(hp, ps(("fo", p))[0:TT, 0:(b - a) * D], hp, ALU.add).then_inc(h2_ready.sem, 1)
                normed(g, "ln3")
                dve.wait_ge(*stored.last_turn(g, "s", 15))
                dve.memset(hidp[:, :, :, 0:K - 1], 0.0).then_inc(conv_step.sem, 1)
                dve.wait_ge(*conv_step.at(g, "pad"))
                for c in range(IC):
                    dve.wait_ge(*hid_ready.at(g, c))
                    acc = hh[:, c, :].rearrange("p (b t) -> p b t", t=T)
                    dve.tensor_scalar(acc, hidp[:, c % 2, :, K - 1:], cw[:, c, K - 1:K], cvec[:, 0, c:c + 1],
                                      ALU.mult, ALU.add).then_inc(conv_step.sem, 1)
                    for i, k in enumerate(range(K - 1)):
                        dve.wait_ge(*conv_step.at(g, (c, i)))
                        dve.scalar_tensor_tensor(acc, hidp[:, c % 2, :, k:k + T], cw[:, c, k:k + 1], acc,
                                                 ALU.mult, ALU.add).then_inc(conv_step.sem, 1)
                dve.wait_ge(*filled(g, ("bc", 0)))
                src = ps(("bc", 0))[0:96, :, 0:HB]

                def half(ap):
                    return ap.rearrange("p (q t) -> p q t", q=2)

                dve.tensor_copy(half(stk[:, :]), src).then_inc(bc_step.sem, 1)
                dve.wait_ge(*bc_step.at(g, 0))
                dve.tensor_tensor(half(bcr), src, half(stk[:, :]), ALU.subtract).then_inc(bc_step.sem, 1)
                dve.wait_ge(*bc_step.at(g, 1))
                dve.tensor_copy(midb, bcr).then_inc(bc_step.sem, 1)
                dve.wait_ge(*bc_step.at(g, 2))
                dve.tensor_copy(stk[32:64, :], midb[32:64, :]).then_inc(bc_step.sem, 1)
                dve.tensor_tensor(stk[64:96, :], bcr[64:96, :], midb[64:96, :], ALU.subtract).then_inc(bc_step.sem, 1)
                for c in range(IC):
                    dve.wait_ge(*sp_step.at(g, (c, 3)))
                    dve.scalar_tensor_tensor(dt[:, c, :], sp[:, c % 2, 0, :], 0.0, sp[:, c % 2, 1, :], ALU.max, ALU.add).then_inc(dt_ready.sem, 1)
                dve.wait_ge(*emptied(g, "dA", 0))
                dve.memset(bank[:, 0:2, 0:HB].rearrange("p q (b t) -> p q b t", t=T)[:, :, :, 0:1], 0.0).then_inc(dA_zero.sem, 1)

                def unit(c, n, par):
                    dve.wait_ge(*bc_full.at(g, c, 2 * n if c == 0 else n))
                    dve.tensor_tensor(half(dbu[:, par, :]), half(u[:, c, :]), bank[:, 2:4, 0:HB], ALU.mult).then_inc(dbu_ready.sem, 1)
                    for q in range(2):
                        if q == 0:
                            dve.wait_ge(*dA_full[0].at(g, c, n))
                            dve.wait_ge(*dbu_ready.at(g, c, n))
                            dve.wait_ge(*cs_used.at(g, c, n - 2))
                        else:
                            dve.wait_ge(*dA_full[1].at(g, c, n))
                        cols = slice(q * HB, (q + 1) * HB)
                        dve.tensor_tensor_scan(st[:, par, cols], bank[:, q, 0:HB], dbu[:, par, cols], 0.0,
                                               ALU.mult, ALU.add).then_inc(st_ready[q].sem, 1)

                for c in range(IC):
                    dve.wait_ge(*u_step.at(g, (c, 1)))
                    dve.nop(nofuse=True)
                    with dve.Fori(0, N // 2) as m:
                        for par in range(2):
                            unit(c, 2 * m + par, par)
                    dve.wait_ge(*cs_used.at(g, c, N - 1))
                    dve.scalar_tensor_tensor(half(u[:, c, :]), half(hh[:, c, :]), cvec[:, 2, c:c + 1], bank[:, 4:6, 0:HB],
                                             ALU.mult, ALU.add).then_inc(ysum_ready.sem, 1)
                for p, (a, b) in enumerate(PAIRS):
                    dve.wait_ge(*filled(g, ("op", p)))
                    if p == 0:
                        dve.wait_ge(*hb_loaded.at(g, "s", 15))
                    hp = hb[:, a:b, :].rearrange("p j d -> p (j d)")
                    dve.tensor_tensor(hp, ps(("op", p))[0:TT, 0, 0:(b - a) * D], hp, ALU.add).then_inc(h3_ready.sem, 1)
                stats_of(g, hb, h3_ready, "ln4")
                dve.wait_ge(*coef_ready.at(g, "ln4"))
                for j in range(J):
                    ins = dve.tensor_scalar(xb[:, j, :], hb[:, j, :], one(MEAN, j), one(RSTD, j), ALU.subtract, ALU.mult)
                ins.then_inc(xb_ready.sem, 1)
                dve.wait_ge(*xg_ready.at(g, 0))
                dve.tensor_reduce(col(PEAK), xb, AX_X, ALU.max, apply_absolute_value=True).then_inc(peak_ready.sem, 1)
                dve.wait_ge(*floor_ready.at(g, 1))
                dve.reciprocal(col(T1), col(PEAK)).then_inc(rcp_ready.sem, 1)
                dve.wait_ge(*scale_ready.at(g, 1))
                for j in range(J):
                    ins = dve.tensor_scalar(xb[:, j, :], xb[:, j, :], one(QS, j), MAGIC, ALU.mult, ALU.add)
                ins.then_inc(qr_ready.sem, 1)
                dve.wait_ge(*qr_ready.at(g, 0))
                dve.tensor_scalar(qx, xb, MAGIC, 127.0, ALU.subtract, ALU.min).then_inc(qx_ready.sem, 1)

                def peak2(j):
                    dve.wait_ge(*r2_ready.at(g, j))
                    dve.tensor_reduce(one(PEAK2, j), y2[:, j, :], AX_X, ALU.max, apply_absolute_value=True).then_inc(peak_ready.sem, 1)

                for j in range(J):
                    dve.wait_ge(*sgl_ready.at(g, j))
                    dve.scalar_tensor_tensor(y2[:, j, :], ps(("fi", j))[0:TT, 0, :], one(SC, j), sgl[:, j % 2, :],
                                             ALU.mult, ALU.mult).then_inc(y2_ready.sem, 1)
                    if j > 1:
                        peak2(j - 2)
                peak2(J - 2)
                peak2(J - 1)
                dve.wait_ge(*floor_ready.at(g, 2))
                dve.reciprocal(col(T1), col(PEAK2)).then_inc(rcp_ready.sem, 1)
                for j in range(J):
                    dve.wait_ge(*q2r_ready.at(g, j))
                    dve.tensor_scalar(q2[:, j, :], y2[:, j, :], MAGIC, 127.0, ALU.subtract, ALU.min).then_inc(q2_ready.sem, 1)
                for p, (a, b) in enumerate(PAIRS):
                    dve.wait_ge(*filled(g, ("out", p)))
                    for j in range(a, b):
                        dve.scalar_tensor_tensor(ob[:, j, :], ps(("out", p))[0:TT, 0, (j - a) * D:(j - a + 1) * D], one(SC2, j),
                                                 hb[:, j, :], ALU.mult, ALU.add).then_inc(o_ready.sem, 1)

        @block.gpsimd
        def _(pool):
            for sig in credited:
                pool.sem_inc(sig.sem, sig.credit)
            pool.wait_ge(*setup.at(0, "x0 mean"))
            pool.tensor_scalar(x0m[:, :, 1], x0m[:, :, 1], LN_EPS, None, ALU.add)
            pool.memset(nhalf[:], -0.5).then_inc(setup.sem, 1)
            pool.wait_ge(*setup.at(0, "x0 var"))
            pool.tensor_tensor(x0m[:, :, 1], x0m[:, :, 1], nhalf[0:98, 0:2], ALU.pow).then_inc(setup.sem, 1)
            pool.wait_ge(*setup.at(0, "end"))
            links = [0]

            def link(g, ins):
                links[0] += 1
                ins.then_inc(pool_link, 1)
                pool.wait_ge(pool_link, g * POOL_LINKS + links[0])
                pool.nop(nofuse=True)

            def coef(g, key):
                pool.wait_ge(*stats_ready.at(g, key))
                pool.nop(nofuse=True)
                mean_e, m2_e, mean_o, m2_o = (stats[:, :, i] for i in (1, 2, 4, 5))
                pool.tensor_tensor(col(MEAN2), mean_e, mean_o, ALU.add)
                pool.tensor_tensor(col(T1), m2_e, m2_o, ALU.add)
                link(g, pool.tensor_tensor(col(DIFF), mean_e, mean_o, ALU.subtract))
                pool.tensor_scalar(col(MEAN), col(MEAN2), 0.5, None, ALU.mult)
                pool.tensor_scalar(col(T1), col(T1), 1.0 / D, None, ALU.mult)
                link(g, pool.tensor_tensor(col(DIFF), col(DIFF), col(DIFF), ALU.mult))
                link(g, pool.tensor_scalar(col(DIFF), col(DIFF), 0.25, None, ALU.mult))
                link(g, pool.tensor_tensor(col(VAR), col(DIFF), col(T1), ALU.add))
                link(g, pool.tensor_scalar(col(T2), col(VAR), LN_EPS, None, ALU.add))
                pool.tensor_tensor(col(RSTD), col(T2), nhalf[:], ALU.pow).then_inc(coef_ready.sem, 1)

            with pool.Fori(0, NG) as g:
                links[0] = 0
                coef(g, "ln1")
                for p, (a, b) in enumerate(PAIRS):
                    pool.wait_ge(*t_ready.at(g, p))
                    pool.nop(nofuse=True)
                    pool.tensor_tensor(h[:, a:b, :], h[:, a:b, :], xln[:, a:b, :], ALU.add).then_inc(h1_ready.sem, 1)
                coef(g, "ln2")
                coef(g, "ln3")
                for c in range(IC):
                    pool.wait_ge(*dt_ready.at(g, c))
                    pool.nop(nofuse=True)
                    last = dt[:, c, :].rearrange("p (b t) -> p b t", t=T)[:, :, T - 1]
                    pool.tensor_scalar(last, last, cvec[:, 3, c:c + 1], None, ALU.mult).then_inc(u_step.sem, 1)
                    pool.wait_ge(*u_step.at(g, (c, 0)))
                    pool.wait_ge(*hh_ready.at(g, c))
                    pool.nop(nofuse=True)
                    pool.tensor_tensor(u[:, c, :], dt[:, c, :], hh[:, c, :], ALU.mult).then_inc(u_step.sem, 1)
                for c in range(IC):
                    with pool.Fori(0, N // 2) as m:
                        for par in range(2):
                            n = 2 * m + par
                            pool.wait_ge(*st_ready[1].at(g, c, n))
                            if c == 0:
                                pool.wait_ge(*cb_ready.at(g, "c", n))
                            pool.nop(nofuse=True)
                            pool.tensor_tensor(st[:, par, :], st[:, par, :], cb[:, bass.ds(n, 1), :].rearrange("p n t -> p (n t)"),
                                               ALU.mult).then_inc(cs_ready.sem, 1)
                    pool.wait_ge(*ysum_ready.at(g, c))
                    pool.wait_ge(*sg_ready.at(g, c))
                    pool.nop(nofuse=True)
                    pool.tensor_tensor(hh[:, c, :].rearrange("p (j b t) -> p b j t", j=J, b=GB),
                                       u[:, c, :].rearrange("p (b j t) -> p b j t", j=J, b=GB),
                                       sg[:, c, :].rearrange("p (b j t) -> p b j t", j=J, b=GB), ALU.mult).then_inc(yg_step.sem, 1)
                    pool.wait_ge(*yg_step.at(g, (c, 0)))
                    pool.nop(nofuse=True)
                    last = hh[:, c, :].rearrange("p (j b t) -> p j b t", j=J, b=GB)[:, J - 1, :, TC - 1]
                    pool.tensor_scalar(last, last, cvec[:, 4, c:c + 1], None, ALU.mult).then_inc(yg_step.sem, 1)
                coef(g, "ln4")
                pool.wait_ge(*coef_ready.at(g, "ln4"))
                pool.nop(nofuse=True)
                link(g, pool.tensor_tensor(col(T2), col(RSTD), col(RSTD), ALU.mult))
                link(g, pool.tensor_tensor(col(T2), col(T2), col(VAR), ALU.mult))
                link(g, pool.tensor_scalar(col(T2), col(T2), RMS_EPS, None, ALU.add))
                link(g, pool.tensor_tensor(col(RINV), col(T2), nhalf[:], ALU.pow))
                pool.wait_ge(*xb_ready.at(g, 0))
                pool.nop(nofuse=True)
                for j in range(J):
                    ins = pool.tensor_tensor(xb[:, j, :], xb[:, j, :], gin[:], ALU.mult)
                ins.then_inc(xg_ready.sem, 1)

                def quant_scale(i, peak, rinv, scale, qscale):
                    link(g, pool.tensor_tensor(col(peak), col(peak), col(rinv), ALU.mult))
                    link(g, pool.tensor_scalar(col(peak), col(peak), Q_EPS, None, ALU.max))
                    pool.tensor_scalar(col(scale), col(peak), 1.0 / 127.0, wsc[0:TT, 3 + i:4 + i], ALU.mult, ALU.mult).then_inc(floor_ready.sem, 1)
                    pool.wait_ge(*rcp_ready.at(g, i))
                    pool.nop(nofuse=True)
                    link(g, pool.tensor_tensor(col(T2), col(T1), col(rinv), ALU.mult))
                    pool.tensor_scalar(col(qscale), col(T2), 127.0, None, ALU.mult).then_inc(scale_ready.sem, 1)

                pool.wait_ge(*peak_ready.at(g, 0))
                pool.nop(nofuse=True)
                quant_scale(1, PEAK, RINV, SC, QS)
                for j in range(J):
                    pool.wait_ge(*ss_ready.at(g, j))
                    pool.nop(nofuse=True)
                    pool.tensor_tensor(y2[:, j, :], y2[:, j, :], gout[:], ALU.mult).then_inc(r2_ready.sem, 1)
                pool.wait_ge(*rcp_ready.at(g, 1))
                pool.nop(nofuse=True)
                link(g, pool.tensor_scalar(col(T2), col(SS), 1.0 / FH, RMS_EPS, ALU.mult, ALU.add))
                link(g, pool.tensor_tensor(col(RINV2), col(T2), nhalf[:], ALU.pow))
                pool.wait_ge(*peak_ready.at(g, J))
                pool.nop(nofuse=True)
                quant_scale(2, PEAK2, RINV2, SC2, QS2)
                assert links[0] == POOL_LINKS, links[0]


def kernel(**inputs):
    import numpy as np
    import concourse.bacc as bacc
    from concourse.bass_utils import run_bass_kernel_spmd

    a = {k: np.asarray(v) for k, v in inputs.items()}

    def halves(w):
        return w.reshape(2, DH, -1).transpose(1, 0, 2)

    def blocks(w, p=128):
        return w.reshape(-1, p, w.shape[-1]).transpose(1, 0, 2)

    x = a["x"].reshape(B, 3, 14, 16, 14, 16).transpose(3, 5, 1, 0, 2, 4)
    x = x.reshape(KC, 128, NG, GB, J, TC)
    patches = x.transpose(2, 1, 4, 0, 3, 5).reshape(NG, 128, J, KC, TT)
    first = x[:, :, 0, 0].reshape(KC, 128, T).transpose(1, 0, 2)
    bias = a["L0_ffn_in_bias"].reshape(1, 1, HID)
    ffn_in = np.concatenate([halves(a["L0_ffn_in_weight"].T), np.concatenate([np.zeros_like(bias), bias], 1)], 0)
    xp = a["L1_attn_x_proj_w"].T
    bc = np.concatenate([xp[:, R:]] * 3, 1)
    steps = np.arange(TC)
    sigma = np.arange(TS)
    row_step = np.tile(sigma, NH)[:, None, None] + TS * np.arange(NR)[None, :, None]
    col_step = np.tile(steps, GB)[None, None, :]
    mask = (row_step < col_step).astype(np.float32).reshape(RB, 1, -1)
    mask = np.concatenate([mask, mask], 1).reshape(RB, -1)
    decp = (DECAY ** np.tile(steps, GB)).astype(np.float32)[:, None]
    dec = np.broadcast_to((WRITE * DECAY ** (-1.0 - np.arange(T) % TC)).astype(np.float32), (DH, T))
    bf = mybir.dt.np(BF16)
    sel = np.concatenate([np.eye(32, dtype=np.float32)] * 3, 0).astype(bf)
    eye = np.eye(128, dtype=np.float32)
    vec = lambda v: v.reshape(IC, 128).T
    arrays = dict(
        xt=patches, x0t=first, w_tok=blocks(a["L0_tok_W"].T), w_key=blocks(a["L0_attn_w_key"], DK),
        w_query=blocks(a["L0_attn_w_query"], DK), w_value=blocks(a["L0_attn_w_value"], DK),
        w_outt=blocks(a["L0_attn_w_out"].T, DK), w_gate=halves(a["L0_attn_w_gate"].T), ffn_in=ffn_in,
        ffn_out=blocks(a["L0_ffn_out_weight"]), w_inp=halves(a["L1_attn_in_proj_w"].T),
        conv_w=a["L1_attn_conv_w"].reshape(IC, 128, K).transpose(1, 0, 2), conv_b=vec(a["L1_attn_conv_b"]),
        w_xp=blocks(xp[:, :R]), w_bc=blocks(bc), w_dt=a["L1_attn_dt_proj_w"].T, b_dt=vec(a["L1_attn_dt_proj_b"]),
        a_log=blocks(a["L1_attn_A_log"]), d_skip=vec(a["L1_attn_D"]), w_op=blocks(a["L1_attn_out_proj_w"].T),
        alpha=vec(a["L1_attn_alpha"]), fgate=vec(a["L1_attn_feature_gating"]),
        q_in=halves(a["L1_ffn_w_in"].T), g_in=a["L1_ffn_g_in"], q_out=blocks(a["L1_ffn_w_out"].T),
        g_out=a["L1_ffn_g_out"], ident_c=eye, identb_c=eye.astype(bf), mask_c=mask, dec_c=dec, decp_c=decp, sel_c=sel)
    arrays = {k: np.ascontiguousarray(v) for k, v in arrays.items()}

    nc = bacc.Bacc("TRN2", target_bir_lowering=False, num_devices=1)
    aps = {k: nc.dram_tensor(f"in_{k}", v.shape, mybir.dt.from_np(v.dtype), kind="ExternalInput").ap() for k, v in arrays.items()}
    saved = nc.dram_tensor("saved_h2", (NG, TT, J, D), F32).ap()
    out = nc.dram_tensor("out_tiles", (NG, TT, J, D), F32, kind="ExternalOutput").ap()
    program(nc, saved=saved, out=out, **aps)
    r = run_bass_kernel_spmd(nc, [{f"in_{k}": v for k, v in arrays.items()}], core_ids=[0])
    tiles = np.asarray(r.results[0]["out_tiles"]).reshape(NG, GB, TC, J, D)
    return np.ascontiguousarray(tiles.transpose(0, 1, 3, 2, 4).reshape(B, T, D))
```

```python
from contextlib import ExitStack

import concourse.bass as bass
from concourse import mybir

ALU = mybir.AluOpType
ACT = mybir.ActivationFunctionType
AX_X = mybir.AxisListType.X
F32 = mybir.dt.float32
BF16 = mybir.dt.bfloat16

B, T, D, PIX = 64, 196, 192, 768
GB = 4
NG = B // GB
TC = 28
J = T // TC
TT = GB * TC
GT = GB * T
HB = GT // 2
DH = D // 2
KC = PIX // 128
NH, DK = 8, 64
TS = 14
NR = TC // TS
RB = NH * TS
HID = 768
HC = HID // 128
I, N, R, K = 384, 16, 48, 4
IC = I // 128
FH = 512
FC = FH // 128
DECAY, WRITE = 0.95, 0.1
LN_EPS, RMS_EPS, Q_EPS = 1e-5, 1e-6, 1e-5
MAGIC = 12582912.0
PAIRS = [(0, 2), (2, 4), (4, 6), (6, 7)]
XBUF = 4
UNITS = IC * N
AT = dict(
    tok=(0, 2, 4, 6), embed=(1, 3, 5, 7), stats1=(2, 4, 6, 8), coef1=(9,), norm1=(10,),
    tr1=(11, 11, 13, 13), turn1=(12, 12, 14, 14), sc=(15, 15, 17, 19), mask=(16, 16, 18, 20), ao=(17, 19, 21, 21),
    sum=(18, 20, 22, 22), h1=(19, 21, 23, 23), stats2=(20, 22, 24, 24), coef2=(25,), norm2=(26,),
    tr2=(27, 27, 29, 29), turn2=(28, 28, 30, 30),
    hid=(31, 31, 32, 35, 35, 36, 39, 39, 40, 43, 43, 44), gelu=(32, 32, 33, 36, 36, 37, 40, 40, 41, 44, 44, 45),
    fo=(34, 38, 42, 46), h2=(35, 39, 43, 47), stats3=(36, 40, 44, 47), coef3=(47,), norm3=(47,))


class Signal:

    def __init__(self, sem, order, credit=0):
        self.sem = sem
        self.start, n = {}, 0
        for key, count in order:
            self.start[key] = n
            n += count
        self.per_turn = n
        self.credit = n if credit == "turn" else credit

    def at(self, g, key, extra=0):
        return self.sem, g * self.per_turn + (extra + (self.start[key] + 1 + self.credit))

    def last_turn(self, g, key, extra=0):
        assert self.credit == self.per_turn
        return self.sem, g * self.per_turn + (extra + (self.start[key] + 1))


def program(nc, xt, x0t, w_tok, w_key, w_query, w_value, w_outt, w_gate, ffn_in, ffn_out,
            w_inp, conv_w, conv_b, w_xp, w_bc, w_dt, b_dt, a_log, d_skip, w_op, alpha, fgate,
            q_in, g_in, q_out, g_out, ident_c, identb_c, mask_c, dec_c, decp_c, sel_c, saved, out):
    with ExitStack() as ctx:
        def sb(name, shape, dt=F32):
            return ctx.enter_context(nc.sbuf_tensor(name, shape, dt))

        def sem(name):
            return ctx.enter_context(nc.semaphore(name))

        bank = ctx.enter_context(nc.psum_tensor("bank", [128, 8, 512], F32))
        ident = sb("ident", [128, 128])
        identb = sb("identb", [128, 128], BF16)
        mask = sb("mask", [RB, NR * TT])
        decp = sb("decp", [TT, 1])
        sel = sb("sel", [96, 2 * N], BF16)
        wtok = sb("wtok", [128, KC, D])
        wfi = sb("wfi", [DH + 1, 2, HID])
        wfo = sb("wfo", [128, HC, D])
        winp = sb("winp", [DH, 2, 2 * I])
        wxp = sb("wxp", [128, IC, R])
        wbc = sb("wbc", [128, IC, 96])
        wdt = sb("wdt", [R, I])
        wop = sb("wop", [128, IC, D])
        cw = sb("cw", [128, IC, K])
        cvec = sb("cvec", [128, 5, IC])
        amat = sb("amat", [128, IC, N])
        qwi = sb("qwi", [DH, 2, 2 * FH], BF16)
        qwo = sb("qwo", [128, FC, D], BF16)
        gin = sb("gin", [TT, D])
        gout = sb("gout", [TT, FH])
        wsc = sb("wsc", [128, 16])
        amask = sb("amask", [DH, 2, J, NR, RB])
        bmat = sb("bmat", [RB, J, NR, D])
        mmat = sb("mmat", [DH, J, 2, D])
        xst = sb("xst", [128, XBUF, KC, TT])
        h = sb("h", [TT, J, D])
        xln = sb("xln", [TT, J, D])
        stats, stats_b = sb("stats", [TT, J, 6]), sb("stats_b", [TT, J, 6])
        small, small_b = sb("small", [TT, 16, J]), sb("small_b", [TT, 16, J])
        xT = sb("xT", [DH + 1, 2, GT])
        scT = sb("scT", [RB, 2, 2, NR, TT])
        gT = sb("gT", [128, HC, 2 * TT])
        mix = sb("mix", [128, 4, IC, GT])
        hh, dt, sg, u = (mix[:, i] for i in range(4))
        dbu = sb("dbu", [128, GT])
        st = sb("st", [128, 3, GT])
        stk = sb("stk", [96, GT], BF16)

        arena = sb("arena", [128, N, GT])
        consts = sb("consts", [128, 4])
        nhalf = sb("nhalf", [TT, J])

        class Carve:

            def __init__(self, whole):
                self.whole, self.used = whole, 0

            def __call__(self, parts, shape, dt=F32):
                n = 1
                for s in shape:
                    n *= s
                words = n if dt == F32 else (n + 1) // 2
                ap = self.whole[0:parts, self.used:self.used + words]
                self.used += words
                assert self.used <= self.whole.shape[1]
                if dt != F32:
                    ap = ap.bitcast(dt)
                if len(shape) == 1:
                    return ap
                names = "abcd"[:len(shape)]
                return ap.rearrange(f"p ({' '.join(names)}) -> p {' '.join(names)}",
                                    **{names[i]: shape[i] for i in range(len(shape))})

        cb = arena
        flat = arena[:].rearrange("p n t -> p (n t)")
        cv = Carve(flat)
        x0, x0ln, x0T = cv(128, [KC, T]), cv(98, [2, D]), cv(DH, [2, T])
        wk, wq, gk = cv(DK, [NH, D]), cv(DK, [NH, D]), cv(DH, [NH, 2, D])
        wg, wgr, gate0, dec = cv(DH, [2, NH]), cv(DH, [2, NH, DH]), cv(DH, [NH, T]), cv(DH, [T])
        cv2 = Carve(mix[:].rearrange("p a c t -> p (a c t)"))
        bT, arow, x0s, x0m = cv2(DH, [2, J, NR, RB]), cv2(RB, [J, NR, D]), cv2(98, [2, 6]), cv2(98, [2, 2])
        wv, wo = cv2(DK, [NH, D]), cv2(DK, [NH, D])
        cvq = Carve(flat)
        qraw, qraw2 = cvq(DH, [2, 2 * FH]), cvq(128, [FC, D])
        qtmp, ones = cvq(128, [2 * 2 * FH]), cvq(128, [128])
        cm = Carve(flat)
        hidp = cm(128, [2, GB, K - 1 + T])
        tsT, bcr, midb = cm(R, [GT]), cm(96, [GT]), cm(96, [GT], BF16)
        sp = cm(128, [2, 2, GT])
        xbt = cm(DH, [2, GB, T])
        ck = Carve(flat)
        hb, xb, ob = ck(TT, [J, D]), ck(TT, [J, D]), ck(TT, [J, D])
        qx, qT = ck(TT, [J, D], BF16), ck(DH, [2, GT], BF16)
        y2, q2 = ck(TT, [J, FH]), ck(TT, [J, FH], BF16)
        sgl, q2T = ck(TT, [2, FH]), ck(128, [2, FC, TT], BF16)

        def signal(name, *keys, credit=0):
            return Signal(sem(name), [k if isinstance(k, tuple) and k[0] == "n" else (k, 1) for k in keys], credit)

        def counted(name, *order, credit=0):
            return Signal(sem(name), list(order), credit)

        s_w = sem("weights_loaded")
        s_qw = sem("quant_weights_loaded")
        SETUP = ("x0 tok", "x0 stats", "x0 mean", "x0 var", "x0 pow", "x0 ln", "x0 turn", "x0T", "gk a", "gk a in", "a", "a in",
                 "gate rep", "gate", "gate in", "gate dec", "gk b", "gk b in", "b", "b in", "turn0", "turn0 b", "turn0 a", "turn1", "turn1 b", "turn1 a", "m") \
            + tuple(("m", j) for j in range(J)) + ("consts", "A exp", "A neg", "sums in", "sums out", "sums", "means", "floor", "inverse",
                                                   "q1", "q2", "q3", "q4", "q5", "q6", "end")
        setup = signal("setup_step", *SETUP)

        front_use = [(s, p) for s in ("tok", "tr1") for p in range(4)]
        front_use += [("sc", 0), ("sc", 1), ("ao", 0), ("sc", 2), ("ao", 1), ("sc", 3), ("ao", 2), ("ao", 3)]
        front_use += [("tr2", p) for p in range(4)]
        for p in range(4):
            front_use += [("hid", 3 * p + i) for i in range(3)] + [("fo", p)]
        front_use += [("tr3", p) for p in range(4)]
        mixer_use = [("inp", i) for i in range(6)] + [("xp", 0), ("bc", 0)] + [("dtp", c) for c in range(IC)]
        back_use = [("op", p) for p in range(4)] + [("qt", p) for p in range(4)] + [("fi", j) for j in range(J)]
        for p, (a, b) in enumerate(PAIRS):
            back_use += [("q2t", j) for j in range(a, b)] + [("out", p)]
        where, order = {}, {}
        for i, k in enumerate(front_use):
            where[k] = 6 + i % 2
        for use in (mixer_use, back_use):
            for i, k in enumerate(use):
                where[k] = i % 3
        for s in (0, 1, 2, 6, 7):
            order[s] = [k for k in front_use + mixer_use if where[k] == s] \
                + ({0: ["dA"], 1: ["B"], 2: ["y"]}.get(s, [])) + [k for k in back_use if where[k] == s]
        bank_full = {s: signal(f"psum{s}_full", *[k for k in order[s] if k not in ("dA", "B", "y")], credit="turn")
                     for s in order}

        LN = ("ln1", "ln2", "ln3")
        four = range(4)
        x_loaded = [counted(f"x_loaded{i}", *[(p, 16) for p in four if p % 2 == i]) for i in range(2)]
        h_ready = signal("h_ready", *four)
        stats_ready = signal("stats_ready", *LN)
        coef_ready = signal("coef_ready", *LN)
        stats4_ready = signal("stats4_ready", "ln4")
        coef4_ready = signal("coef4_ready", "ln4")
        xln_ready = signal("xln_ready", *[(n, p) for n in LN for p in four])
        xT_ready = signal("xT_ready", *[(n, p) for n in ("tr1", "tr2") for p in four], *[("tr3", j) for j in range(J)],
                          credit="turn")
        scT_ready = signal("scores_ready", *four)
        t_ready = signal("attn_sum_ready", *four)
        h1_ready = signal("h1_ready", *four)
        gT_ready = signal("gelu_ready", *range(12))
        h2_ready = signal("h2_ready", *four)
        h2_saved = counted("h2_saved", ("s", 16), credit="turn")
        hb_loaded = counted("h2_reloaded", ("s", 16))
        hid_ready = signal("hidden_ready", *range(IC))
        conv_step = signal("conv_step", "pad", *[(c, k) for c in range(IC) for k in four])
        hh_ready = signal("h_silu_ready", *range(IC))
        sg_ready = signal("gate_silu_ready", *range(IC))
        ts_ready = signal("ts_ready", 0)
        bc_step = signal("bc_split_step", *range(5))
        sp_step = signal("softplus_step", *[(c, k) for c in range(IC) for k in four])
        dt_ready = signal("dt_sum_ready", *range(IC))
        u_step = signal("u_step", *[(c, k) for c in range(IC) for k in range(2)])
        dA_zero = signal("dA_zeroed", 0)
        dA_full = [counted(f"dA_full{q}", *[(c, N) for c in range(IC)]) for q in range(2)]
        bc_full = counted("spread_full", (0, 2 * N), (1, N), (2, N))
        dbu_ready = counted("dbu_ready", *[(c, N) for c in range(IC)])
        st_ready = [counted(f"state_ready{q}", *[(c, N) for c in range(IC)], credit=1) for q in range(2)]
        cb_ready = counted("c_spread_ready", ("c", N))
        cs_ready = counted("c_state_ready", *[(c, N) for c in range(IC)])
        cs_used = counted("c_state_summed", *[(c, N) for c in range(IC)], credit=3)
        ysum_ready = signal("y_sum_ready", *range(IC))
        yg_step = signal("y_gated_step", *[(c, k) for c in range(IC) for k in range(2)])
        h3_ready = signal("h3_ready", *four)
        xb_ready = signal("xb_ready", 0)
        xg_ready = signal("x_gained", 0)
        peak_ready = signal("peak_ready", *range(1 + J))
        rcp_ready = signal("reciprocal_ready", 1, 2)
        floor_ready = signal("floor_ready", 1, 2)
        scale_ready = signal("scale_ready", 1, 2)
        qr_ready = signal("q_rounded", 0)
        qx_ready = signal("qx_ready", 0)
        qT_ready = signal("qT_ready", *four)
        sgl_ready = signal("silu_gate_ready", *range(J))
        y2_ready = signal("y2_ready", *range(J))
        ss_ready = signal("square_sum_ready", *range(J))
        r2_ready = signal("y2_gained", *range(J))
        q2r_ready = signal("q2_rounded", *range(J))
        q2_ready = signal("q2_ready", *range(J))
        q2T_ready = signal("q2T_ready", *range(J), credit="turn")
        o_ready = signal("o_ready", *range(J), credit="turn")
        stored = counted("stored", ("s", 16), credit="turn")
        FRONT_LINKS, BACK_LINKS = 15, 17
        front_link, back_link = sem("pool_front_link"), sem("pool_back_link")

        credited = [s for s in (*bank_full.values(), xT_ready, h2_saved, *st_ready, cs_used, o_ready, q2T_ready, stored)]

        reader = {}
        for p, (a, b) in enumerate(PAIRS):
            reader[("tok", p)] = (h_ready, p)
            reader[("tr1", p)], reader[("tr2", p)] = (xT_ready, ("tr1", p)), (xT_ready, ("tr2", p))
            reader[("tr3", p)] = (xT_ready, ("tr3", b - 1))
            reader[("sc", p)], reader[("ao", p)], reader[("fo", p)] = (scT_ready, p), (t_ready, p), (h2_ready, p)
            for i in range(3):
                reader[("hid", 3 * p + i)] = (gT_ready, 3 * p + i)
            reader[("op", p)], reader[("qt", p)], reader[("out", p)] = (h3_ready, p), (qT_ready, p), (o_ready, b - 1)
        for c in range(IC):
            reader[("inp", c)], reader[("inp", IC + c)] = (hid_ready, c), (sg_ready, c)
            reader[("dtp", c)] = (sp_step, (c, 1))
        reader[("xp", 0)], reader[("bc", 0)] = (ts_ready, 0), (bc_step, 1)
        for j in range(J):
            reader[("fi", j)], reader[("q2t", j)] = (y2_ready, j), (q2T_ready, j)
        reader["dA"], reader["B"], reader["y"] = (st_ready[1], IC - 1, N - 1), (dbu_ready, IC - 1, N - 1), (ysum_ready, IC - 1)

        def filled(g, k):
            return bank_full[where[k]].at(g, k)

        def emptied(g, k, s=None):
            uses = order[where[k] if s is None else s]
            i = uses.index(k)
            sig, *key = reader[uses[i - 1]]
            return sig.at(g, *key) if i else sig.last_turn(g, *key)

        def full_of(k):
            return bank_full[where[k]].sem

        def ps(k):
            s = where[k]
            return bank[:, s, :] if s > 5 else bank[:, 2 * s:2 * s + 2, :]

        STAT = range(14)
        MEAN2, DIFF, VAR, RSTD, MEAN, RINV, PEAK, QS, SC, SS, T1, T2, RINV2, QS2 = STAT
        PEAK2, SC2 = 14, 15

        def col(i, of=small):
            return of[:, i, :]

        def one(i, j, of=small):
            return of[:, i, j:j + 1]

        loads = [(ident, ident_c), (identb, identb_c), (mask, mask_c), (decp, decp_c), (sel, sel_c), (wtok, w_tok),
                 (wfi, ffn_in), (wfo, ffn_out), (winp, w_inp), (wxp, w_xp), (wbc, w_bc), (wdt, w_dt),
                 (wop, w_op), (cw, conv_w), (amat, a_log)]
        loads = [(dst[:], src) for dst, src in loads]
        loads += [(gin[:], g_in.partition_broadcast(TT)), (gout[:], g_out.partition_broadcast(TT))]
        loads += [(cvec[:, i, :], v) for i, v in enumerate((conv_b, b_dt, d_skip, alpha, fgate))]
        loads += [(x0, x0t), (wk, w_key), (wq, w_query), (wv, w_value), (wo, w_outt), (wg, w_gate), (dec, dec_c)]
        W_ALL = 16 * len(loads)
        block = ctx.enter_context(nc.Block())

        @block.sync
        def _(sp):
            for dst, src in loads:
                sp.dma_start(dst, src).then_inc(s_w, 16)
            sp.wait_ge(*setup.at(0, ("m", J - 1)))
            sp.dma_start(qraw, q_in).then_inc(s_qw, 16)
            sp.dma_start(qraw2, q_out).then_inc(s_qw, 16)

            def load_tokens(g):
                for p, (a, b) in enumerate(PAIRS):
                    prev = ("tok", (p + 2) % 4)
                    if p >= 2:
                        sp.wait_ge(*bank_full[where[prev]].at(g, prev))
                    else:
                        sp.wait_ge(*bank_full[where[prev]].last_turn(g, prev))
                    sp.nop(nofuse=True)
                    sp.dma_start(xst[:, 2 * (p % 2):2 * (p % 2) + b - a], xt[g, :, a:b]).then_inc(x_loaded[p % 2].sem, 16)

            def turn(g, nxt):
                sp.wait_ge(*h2_ready.at(g, 3))
                sp.nop(nofuse=True)
                sp.dma_start(saved[g], h[:]).then_inc(h2_saved.sem, 16)
                if nxt is not None:
                    load_tokens(nxt)
                sp.wait_ge(*h2_saved.at(g, "s", 15))
                sp.wait_ge(*cs_ready.at(g, IC - 1, N - 1))
                sp.nop(nofuse=True)
                sp.dma_start(hb, saved[g]).then_inc(hb_loaded.sem, 16)
                sp.wait_ge(*o_ready.at(g, J - 1))
                sp.nop(nofuse=True)
                sp.dma_start(out[g], ob).then_inc(stored.sem, 16)

            load_tokens(0)
            with sp.Fori(0, NG - 1) as g:
                turn(g, g + 1)
            turn(NG - 1, None)
            sp.wait_ge(stored.sem, 16 * (NG + 1))

        @block.tensor
        def _(pe):
            pe.wait_ge(s_w, W_ALL)
            for t in range(2):
                for k in range(KC):
                    mm = pe.matmul(bank[0:98, t, 0:D], x0[:, k, t * 98:(t + 1) * 98], wtok[:, k, :], start=k == 0, stop=k == KC - 1)
            mm.then_inc(setup.sem, 1)
            pe.wait_ge(*setup.at(0, "x0 ln"))
            for t in range(2):
                for e in range(2):
                    mm = pe.transpose(bank[0:DH, 2, e * T + t * 98:e * T + (t + 1) * 98], x0ln[:, t, e * DH:(e + 1) * DH], ident[0:98, 0:98])
            mm.then_inc(setup.sem, 1)
            for side, (left, right, made) in enumerate(((wk, wq, "x0T"), (wv, wo, "gate dec"))):
                pe.wait_ge(*setup.at(0, made))
                for hd in range(NH):
                    for e in range(2):
                        mm = pe.matmul(bank[0:DH, hd, e * D:(e + 1) * D], left[:, hd, e * DH:(e + 1) * DH], right[:, hd, :], start=True, stop=True)
                mm.then_inc(setup.sem, 1)
                pe.wait_ge(*setup.at(0, ("gk a in", "gk b in")[side]))
                for hd in range(NH):
                    for d in range(2):
                        for e in range(2):
                            mm = pe.matmul(bank[0:DH, hd, d * T:(d + 1) * T], gk[:, hd, e, d * DH:(d + 1) * DH], x0T[:, e, :], start=e == 0, stop=e == 1)
                mm.then_inc(setup.sem, 1)
                if side == 0:
                    pe.wait_ge(*setup.at(0, "gate rep"))
                    for hd in range(NH):
                        for e in range(2):
                            mm = pe.matmul(bank[0:DH, hd, 0:T], wgr[:, e, hd, :], x0T[:, e, :], start=e == 0, stop=e == 1)
                    mm.then_inc(setup.sem, 1)
            for half in range(2):
                pe.wait_ge(*setup.at(0, ("b in", "turn0 a")[half]))
                for i in range(7):
                    jj, r = divmod(half * 7 + i, NR)
                    for d in range(2):
                        pe.transpose(bank[0:RB, i, d * DH:(d + 1) * DH], amask[:, d, jj, r, :], ident[0:DH, 0:DH])
                        mm = pe.transpose(bank[0:RB, i, D + d * DH:D + (d + 1) * DH], bT[:, d, jj, r, :], ident[0:DH, 0:DH])
                mm.then_inc(setup.sem, 1)
            pe.wait_ge(*setup.at(0, "turn1 a"))
            for j in range(J - 1):
                for d in range(2):
                    for r in range(NR):
                        mm = pe.matmul(bank[0:DH, j, d * D:(d + 1) * D], arow[:, j, r, d * DH:(d + 1) * DH], bmat[:, j, r, :],
                                       start=r == 0, stop=r == NR - 1)
            mm.then_inc(setup.sem, 1)
            pe.wait_ge(*setup.at(0, "sums out"))
            pe.matmul(bank[:, 0, 0:1], ones[0:DH, :], wsc[0:DH, 0:1], start=True, stop=True)
            pe.matmul(bank[:, 0, 1:2], ones[:, :], wsc[:, 1:2], start=True, stop=True).then_inc(setup.sem, 1)
            pe.wait_ge(*setup.at(0, "end"))

            def transposes(g, name, p, ln):
                a, b = PAIRS[p]
                pe.wait_ge(*emptied(g, (name, p)))
                pe.wait_ge(*xln_ready.at(g, (ln, p)))
                for e in range(2):
                    for j in range(a, b):
                        mm = pe.transpose(ps((name, p))[0:DH, e * (b - a) * TT + (j - a) * TT:e * (b - a) * TT + (j - a + 1) * TT],
                                          xln[:, j, e * DH:(e + 1) * DH], ident[0:TT, 0:TT])
                mm.then_inc(full_of((name, p)), 1)

            def attn_out(g, p):
                a, b = PAIRS[p]
                pe.wait_ge(*emptied(g, ("ao", p)))
                pe.wait_ge(*scT_ready.at(g, p))
                for j in range(a, b):
                    o = ps(("ao", p))[0:TT, (j - a) * D:(j - a + 1) * D]
                    for r in range(NR):
                        mm = pe.matmul(o, scT[:, p % 2, j - a, r, :], bmat[:, j, r, :], start=r == 0, stop=j == 0 and r == NR - 1)
                    if j:
                        for e in range(2):
                            mm = pe.matmul(o, xT[0:DH, e, j * TT:(j + 1) * TT], mmat[:, j, e, :], start=False, stop=e == 1)
                mm.then_inc(full_of(("ao", p)), 1)

            def front(g, i):
                for p, (a, b) in enumerate(PAIRS):
                    if i == AT["tok"][p]:
                        pe.wait_ge(*emptied(g, ("tok", p)))
                        pe.wait_ge(*x_loaded[p % 2].at(g, p, 15))
                        for j in range(a, b):
                            for k in range(KC):
                                mm = pe.matmul(ps(("tok", p))[0:TT, (j - a) * D:(j - a + 1) * D], xst[:, 2 * (p % 2) + j - a, k, :],
                                               wtok[:, k, :], start=k == 0, stop=k == KC - 1)
                        mm.then_inc(full_of(("tok", p)), 1)
                    if i == AT["tr1"][p]:
                        transposes(g, "tr1", p, "ln1")
                    if i == AT["ao"][p]:
                        attn_out(g, p)
                for p, (a, b) in enumerate(PAIRS):
                    if i == AT["sc"][p]:
                        pe.wait_ge(*emptied(g, ("sc", p)))
                        pe.wait_ge(*xT_ready.at(g, ("tr1", p)))
                        for j in range(a, b):
                            for r in range(NR):
                                c0 = ((j - a) * NR + r) * TT
                                for e in range(2):
                                    mm = pe.matmul(ps(("sc", p))[0:RB, c0:c0 + TT], amask[:, e, j, r, :], xT[0:DH, e, j * TT:(j + 1) * TT],
                                                   start=e == 0, stop=e == 1)
                        mm.then_inc(full_of(("sc", p)), 1)
                    if i == AT["tr2"][p]:
                        transposes(g, "tr2", p, "ln2")
                for k in range(12):
                    if i == AT["hid"][k]:
                        p = k // 3
                        a, b = PAIRS[p]
                        w = (b - a) * TT
                        pe.wait_ge(*emptied(g, ("hid", k)))
                        pe.wait_ge(*xT_ready.at(g, ("tr2", p)))
                        for m in range(2):
                            hc = 2 * (k % 3) + m
                            for e in range(2):
                                kk = DH + e
                                mm = pe.matmul(ps(("hid", k))[:, m * w:(m + 1) * w], wfi[0:kk, e, hc * 128:(hc + 1) * 128],
                                               xT[0:kk, e, a * TT:b * TT], start=e == 0, stop=e == 1)
                        mm.then_inc(full_of(("hid", k)), 1)
                for p, (a, b) in enumerate(PAIRS):
                    if i == AT["fo"][p]:
                        pe.wait_ge(*emptied(g, ("fo", p)))
                        pe.wait_ge(*gT_ready.at(g, 3 * p + 2))
                        for j in range(a, b):
                            for hc in range(HC):
                                mm = pe.matmul(ps(("fo", p))[0:TT, (j - a) * D:(j - a + 1) * D], gT[:, hc, (j - a) * TT:(j - a + 1) * TT],
                                               wfo[:, hc, :], start=hc == 0, stop=hc == HC - 1)
                        mm.then_inc(full_of(("fo", p)), 1)

            def mixer(g):
                for p in range(4):
                    transposes(g, "tr3", p, "ln3")
                xf = xbt[:].rearrange("p e b t -> p e (b t)")
                for i in range(6):
                    pe.wait_ge(*emptied(g, ("inp", i)))
                    pe.wait_ge(*xT_ready.at(g, ("tr3", J - 1)))
                    for q in range(2):
                        for e in range(2):
                            mm = pe.matmul(ps(("inp", i))[:, q, 0:HB], winp[:, e, i * 128:(i + 1) * 128], xf[:, e, q * HB:(q + 1) * HB],
                                           start=e == 0, stop=e == 1)
                    mm.then_inc(full_of(("inp", i)), 1)
                for name, w, m in (("xp", wxp, R), ("bc", wbc, 96)):
                    pe.wait_ge(*emptied(g, (name, 0)))
                    pe.wait_ge(*hh_ready.at(g, IC - 1))
                    for q in range(2):
                        for c in range(IC):
                            mm = pe.matmul(ps((name, 0))[0:m, q, 0:HB], w[:, c, :], hh[:, c, q * HB:(q + 1) * HB], start=c == 0, stop=c == IC - 1)
                    mm.then_inc(full_of((name, 0)), 1)
                for c in range(IC):
                    pe.wait_ge(*emptied(g, ("dtp", c)))
                    pe.wait_ge(*ts_ready.at(g, 0))
                    for q in range(2):
                        mm = pe.matmul(ps(("dtp", c))[:, q, 0:HB], wdt[:, c * 128:(c + 1) * 128], tsT[:, q * HB:(q + 1) * HB], start=True, stop=True)
                    mm.then_inc(full_of(("dtp", c)), 1)

            def units(g, nxt):
                pe.wait_ge(*bc_step.at(g, 4))
                pe.wait_ge(*emptied(g, "B", 1))

                def pick(n):
                    return sel[:, n:n + 1].to_broadcast([96, 128])

                def spread_b(c, n):
                    if c == 0 and n or (c, n) == (1, 0):
                        pe.wait_ge(*cb_ready.at(g, "c", N - 1 if c else n - 1))
                    if c:
                        pe.wait_ge(*dbu_ready.at(g, c, n - 1))
                    for q in range(2):
                        mm = pe.matmul(bank[:, 2 + q, 0:HB], pick(n), stk[:, q * HB:(q + 1) * HB], start=True, stop=True)
                    mm.then_inc(bc_full.sem, 1)

                def spread_c(n):
                    pe.wait_ge(*dbu_ready.at(g, 0, n))
                    for q in range(2):
                        mm = pe.matmul(bank[:, 2 + q, 0:HB], pick(n + N), stk[:, q * HB:(q + 1) * HB], start=True, stop=True)
                    mm.then_inc(bc_full.sem, 1)

                def sum_state(i):
                    c, n = divmod(i, N)
                    if i == 0:
                        pe.wait_ge(*emptied(g, "y", 2))
                    elif n == 0:
                        pe.wait_ge(*ysum_ready.at(g, c - 1))
                    pe.wait_ge(*cs_ready.at(g, c, n))
                    for q in range(2):
                        mm = pe.matmul(bank[:, 4 + q, 0:HB], ident[:, :], st[:, i % 3, q * HB:(q + 1) * HB], start=n == 0, stop=n == N - 1,
                                       skip_group_check=True)
                    mm.then_inc(cs_used.sem, 1)

                spread_b(0, 0)
                for i in range(UNITS):
                    if i < N:
                        spread_c(i)
                        if i:
                            sum_state(i - 1)
                        spread_b(*divmod(i + 1, N))
                        if nxt is not None:
                            front(nxt, i)
                    else:
                        if i + 1 < UNITS:
                            spread_b(*divmod(i + 1, N))
                        if nxt is not None:
                            front(nxt, i)
                        sum_state(i - 1)
                sum_state(UNITS - 1)

            def back(g):
                for p, (a, b) in enumerate(PAIRS):
                    pe.wait_ge(*emptied(g, ("op", p)))
                    pe.wait_ge(*yg_step.at(g, (IC - 1, 1)))
                    for j in range(a, b):
                        for c in range(IC):
                            mm = pe.matmul(ps(("op", p))[0:TT, 0, (j - a) * D:(j - a + 1) * D], hh[:, c, j * TT:(j + 1) * TT], wop[:, c, :], start=c == 0, stop=c == IC - 1)
                    mm.then_inc(full_of(("op", p)), 1)
                for p, (a, b) in enumerate(PAIRS):
                    pe.wait_ge(*emptied(g, ("qt", p)))
                    pe.wait_ge(*qx_ready.at(g, 0))
                    pb = ps(("qt", p))[0:DH, 0, :].bitcast(BF16)
                    for e in range(2):
                        for j in range(a, b):
                            o = e * 2 * TT + (j - a) * TT
                            mm = pe.transpose(pb[:, o:o + TT], qx[:, j, e * DH:(e + 1) * DH], identb[0:TT, 0:TT])
                    mm.then_inc(full_of(("qt", p)), 1)
                for j in range(J):
                    pe.wait_ge(*emptied(g, ("fi", j)))
                    pe.wait_ge(*qT_ready.at(g, j // 2))
                    for half in range(2):
                        for e in range(2):
                            mm = pe.matmul(ps(("fi", j))[0:TT, half, :], qT[:, e, j * TT:(j + 1) * TT], qwi[:, e, half * FH:(half + 1) * FH],
                                           start=e == 0, stop=e == 1)
                    mm.then_inc(full_of(("fi", j)), 1)

                def q2_transposes(j):
                    pe.wait_ge(*emptied(g, ("q2t", j)))
                    pe.wait_ge(*q2_ready.at(g, j))
                    pb = ps(("q2t", j))[:, 0, :].bitcast(BF16)
                    for f in range(FC):
                        mm = pe.transpose(pb[:, f * TT:(f + 1) * TT], q2[:, j, f * 128:(f + 1) * 128], identb[0:TT, 0:TT])
                    mm.then_inc(full_of(("q2t", j)), 1)

                def last_products(p):
                    a, b = PAIRS[p]
                    pe.wait_ge(*emptied(g, ("out", p)))
                    pe.wait_ge(*q2T_ready.at(g, b - 1))
                    for j in range(a, b):
                        for f in range(FC):
                            mm = pe.matmul(ps(("out", p))[0:TT, 0, (j - a) * D:(j - a + 1) * D], q2T[:, j % 2, f, :], qwo[:, f, :],
                                           start=f == 0, stop=f == FC - 1)
                    mm.then_inc(full_of(("out", p)), 1)

                for p, (a, b) in enumerate(PAIRS):
                    for j in range(a, b):
                        q2_transposes(j)
                    last_products(p)

            def turn(g, nxt):
                mixer(g)
                units(g, nxt)
                back(g)

            for i in range(UNITS):
                front(0, i)
            with pe.Fori(0, NG - 1) as g:
                turn(g, g + 1)
            turn(NG - 1, None)

        @block.scalar
        def _(act):
            act.wait_ge(*setup.at(0, "x0 turn"))
            act.activation(x0T.rearrange("p e t -> p (e t)"), bank[0:DH, 2, 0:2 * T], ACT.Copy).then_inc(setup.sem, 1)
            act.wait_ge(*setup.at(0, "gate"))
            act.activation(gate0, bank[0:DH, :, 0:T], ACT.Sigmoid).then_inc(setup.sem, 1)
            for half in range(2):
                act.wait_ge(*setup.at(0, ("turn0 b", "turn1 b")[half]))
                act.activation(arow.rearrange("p j r d -> p (j r) d")[:, half * 7:half * 7 + 7], bank[0:RB, 0:7, 0:D],
                               ACT.Copy, scale=DECAY ** TC).then_inc(setup.sem, 1)
            act.wait_ge(*setup.at(0, "consts"))
            act.activation(amat[:], amat[:], ACT.Exp).then_inc(setup.sem, 1)
            act.wait_ge(s_qw, 32)
            act.wait_ge(*setup.at(0, "A exp"))
            act.activation(amat[:], amat[:], ACT.Copy, scale=-1.0).then_inc(setup.sem, 1)
            qi, qo = qraw.rearrange("p e f -> p (e f)"), qraw2.rearrange("p f d -> p (f d)")
            act.wait_ge(*setup.at(0, "A neg"))
            act.activation(qtmp[0:DH, :], qi, ACT.Abs, accum_out=wsc[0:DH, 0:1]).then_inc(setup.sem, 1)
            act.wait_ge(*setup.at(0, "sums in"))
            act.activation(qtmp[:, 0:FC * D], qo, ACT.Abs, accum_out=wsc[:, 1:2]).then_inc(setup.sem, 1)
            act.wait_ge(*setup.at(0, "end"))

            def turned(g, name, p):
                a, b = PAIRS[p]
                w = (b - a) * TT
                act.wait_ge(*filled(g, (name, p)))
                act.activation(xT[0:DH, :, a * TT:b * TT], ps((name, p))[0:DH, 0:2 * w].rearrange("p (e w) -> p e w", e=2),
                               ACT.Copy).then_inc(xT_ready.sem, 1)

            def decay_factor(g, c, n):
                for q in range(2):
                    act.wait_ge(*st_ready[q].at(g, c, n - 1))
                    act.activation(bank[:, q, 0:HB].rearrange("p (b t) -> p b t", t=T)[:, :, 1:T],
                                   dt[:, c, q * HB:(q + 1) * HB].rearrange("p (b t) -> p b t", t=T)[:, :, 1:T],
                                   ACT.Exp, scale=amat[:, c, n:n + 1]).then_inc(dA_full[q].sem, 1)

            def front(g, i):
                for p, (a, b) in enumerate(PAIRS):
                    if i == AT["embed"][p]:
                        act.wait_ge(*filled(g, ("tok", p)))
                        if p == 0:
                            act.wait_ge(*h2_saved.last_turn(g, "s", 15))
                        act.activation(h[:, a:b, :], ps(("tok", p))[0:TT, 0:(b - a) * D].rearrange("p (j d) -> p j d", d=D),
                                       ACT.Copy).then_inc(h_ready.sem, 1)
                    if i == AT["turn1"][p]:
                        turned(g, "tr1", p)
                    if i == AT["turn2"][p]:
                        turned(g, "tr2", p)
                for k in range(12):
                    if i == AT["gelu"][k]:
                        w = (PAIRS[k // 3][1] - PAIRS[k // 3][0]) * TT
                        act.wait_ge(*filled(g, ("hid", k)))
                        if k >= 3 and k % 3 == 0:
                            act.wait_ge(*filled(g, ("fo", k // 3 - 1)))
                        act.activation(gT[:, 2 * (k % 3):2 * (k % 3) + 2, 0:w], ps(("hid", k))[:, 0:2 * w].rearrange("p (m w) -> p m w", m=2),
                                       ACT.Gelu).then_inc(gT_ready.sem, 1)

            def mixer(g):
                for p, (a, b) in enumerate(PAIRS):
                    act.wait_ge(*filled(g, ("tr3", p)))
                    if p == 0:
                        act.wait_ge(*stored.last_turn(g, "s", 15))
                    for j in range(a, b):
                        src = ps(("tr3", p))[0:DH, 0:2 * (b - a) * TT].rearrange("p (e j b t) -> p e j b t", e=2, j=b - a, b=GB)
                        act.activation(xbt[:, :, :, j * TC:(j + 1) * TC], src[:, :, j - a], ACT.Copy).then_inc(xT_ready.sem, 1)
                for c in range(IC):
                    act.wait_ge(*filled(g, ("inp", c)))
                    if c < 2:
                        act.wait_ge(*conv_step.at(g, "pad"))
                    else:
                        act.wait_ge(*conv_step.at(g, (c - 2, 3)))
                    act.activation(hidp[:, c % 2, :, K - 1:].rearrange("p (q b) t -> p q b t", q=2),
                                   ps(("inp", c))[:, :, 0:HB].rearrange("p q (b t) -> p q b t", t=T), ACT.Copy).then_inc(hid_ready.sem, 1)
                for c in range(IC):
                    act.wait_ge(*filled(g, ("inp", IC + c)))
                    act.activation(sg[:, c, :].rearrange("p (q t) -> p q t", q=2), ps(("inp", IC + c))[:, :, 0:HB],
                                   ACT.Silu).then_inc(sg_ready.sem, 1)
                    act.wait_ge(*conv_step.at(g, (c, 3)))
                    act.activation(hh[:, c, :], hh[:, c, :], ACT.Silu).then_inc(hh_ready.sem, 1)
                act.wait_ge(*filled(g, ("xp", 0)))
                act.activation(tsT.rearrange("p (q t) -> p q t", q=2), ps(("xp", 0))[0:R, :, 0:HB], ACT.Copy).then_inc(ts_ready.sem, 1)
                for c in range(IC):
                    act.wait_ge(*filled(g, ("dtp", c)))
                    if c >= 2:
                        act.wait_ge(*dt_ready.at(g, c - 2))
                    x, e = sp[:, c % 2, 0, :], sp[:, c % 2, 1, :]
                    src = ps(("dtp", c))[:, :, 0:HB]
                    act.activation(x.rearrange("p (q t) -> p q t", q=2), src, ACT.Identity, bias=cvec[:, 1, c:c + 1]).then_inc(sp_step.sem, 1)
                    act.activation(e.rearrange("p (q t) -> p q t", q=2), src, ACT.Abs, bias=cvec[:, 1, c:c + 1]).then_inc(sp_step.sem, 1)
                    act.wait_ge(*sp_step.at(g, (c, 1)))
                    act.activation(e, e, ACT.Exp, scale=-1.0).then_inc(sp_step.sem, 1)
                    act.wait_ge(*sp_step.at(g, (c, 2)))
                    act.activation(e, e, ACT.Ln, bias=1.0).then_inc(sp_step.sem, 1)

            def units(g, nxt):
                act.wait_ge(*dA_zero.at(g, 0))
                act.wait_ge(*dt_ready.at(g, IC - 1))
                act.wait_ge(*u_step.at(g, (IC - 1, 1)))
                decay_factor(g, 0, 0)
                for i in range(UNITS):
                    c, n = divmod(i, N)
                    if c == 0:
                        act.wait_ge(*bc_full.at(g, 0, 2 * n + 1))
                        act.activation(cb[:, n, :].rearrange("p (q t) -> p q t", q=2), bank[:, 2:4, 0:HB], ACT.Copy).then_inc(cb_ready.sem, 1)
                    if i + 1 < UNITS:
                        decay_factor(g, (i + 1) // N, (i + 1) % N)
                    if nxt is not None:
                        front(nxt, i)

            def back(g):
                for p, (a, b) in enumerate(PAIRS):
                    act.wait_ge(*filled(g, ("qt", p)))
                    pb = ps(("qt", p))[0:DH, 0, :].bitcast(BF16)[:, 0:4 * TT].rearrange("p (e w) -> p e w", e=2)
                    act.activation(qT[:, :, a * TT:b * TT], pb[:, :, 0:(b - a) * TT], ACT.Copy).then_inc(qT_ready.sem, 1)

                def squares(j):
                    act.wait_ge(*y2_ready.at(g, j))
                    act.activation(sgl[:, j % 2, :], y2[:, j, :], ACT.Square, accum_out=one(SS, j, small_b)).then_inc(ss_ready.sem, 1)

                for j in range(J):
                    act.wait_ge(*filled(g, ("fi", j)))
                    act.wait_ge(*scale_ready.at(g, 1))
                    if j >= 2:
                        act.wait_ge(*ss_ready.at(g, j - 2))
                    act.activation(sgl[:, j % 2, :], ps(("fi", j))[0:TT, 1, :], ACT.Silu, scale=one(SC, j, small_b)).then_inc(sgl_ready.sem, 1)
                    if j:
                        squares(j - 1)
                squares(J - 1)
                act.wait_ge(*scale_ready.at(g, 2))
                for j in range(J):
                    act.activation(y2[:, j, :], y2[:, j, :], ACT.Identity, scale=one(QS2, j, small_b), bias=consts[0:TT, 1:2]).then_inc(q2r_ready.sem, 1)
                for p, (a, b) in enumerate(PAIRS):
                    for j in range(a, b):
                        act.wait_ge(*filled(g, ("q2t", j)))
                        if p:
                            act.wait_ge(*filled(g, ("out", p - 1)))
                        act.activation(q2T[:, j % 2].rearrange("p f t -> p (f t)"),
                                       ps(("q2t", j))[:, 0, :].bitcast(BF16)[:, 0:FC * TT], ACT.Copy).then_inc(q2T_ready.sem, 1)

            def turn(g, nxt):
                mixer(g)
                units(g, nxt)
                back(g)

            for i in range(UNITS):
                front(0, i)
            with act.Fori(0, NG - 1) as g:
                turn(g, g + 1)
            turn(NG - 1, None)

        @block.vector
        def _(dve):
            dve.wait_ge(*setup.at(0, "x0 tok"))
            for t in range(2):
                ins = dve.bn_stats(x0s[:, t, :], bank[0:98, t, 0:D])
            ins.then_inc(setup.sem, 1)
            dve.wait_ge(*setup.at(0, "x0 stats"))
            for t in range(2):
                ins = dve.bn_aggr(x0m[:, t, :], x0s[:, t, :])
            ins.then_inc(setup.sem, 1)
            dve.wait_ge(*setup.at(0, "x0 pow"))
            for t in range(2):
                ins = dve.tensor_scalar(x0ln[:, t, :], bank[0:98, t, 0:D], x0m[:, t, 0:1], x0m[:, t, 1:2], ALU.subtract, ALU.mult)
            ins.then_inc(setup.sem, 1)
            dve.wait_ge(*setup.at(0, "gk a"))
            dve.tensor_copy(gk.rearrange("p h e d -> p h (e d)"), bank[0:DH, :, 0:2 * D]).then_inc(setup.sem, 1)
            dve.wait_ge(*setup.at(0, "a"))
            for hd in range(NH):
                for d in range(2):
                    ins = dve.tensor_copy(amask[:, d].rearrange("p j r (h s) -> p h (j r) s", h=NH)[:, hd],
                                          bank[0:DH, hd, d * T:(d + 1) * T].rearrange("p (a s) -> p a s", s=TS))
            ins.then_inc(setup.sem, 1)
            dve.wait_ge(*setup.at(0, "a in"))
            dve.tensor_copy(wgr, wg.unsqueeze(3).to_broadcast([DH, 2, NH, DH])).then_inc(setup.sem, 1)
            dve.wait_ge(*setup.at(0, "gate in"))
            for hd in range(NH):
                ins = dve.tensor_tensor(gate0[:, hd, :], gate0[:, hd, :], dec, ALU.mult)
            ins.then_inc(setup.sem, 1)
            dve.wait_ge(*setup.at(0, "gk b"))
            dve.tensor_copy(gk.rearrange("p h e d -> p h (e d)"), bank[0:DH, :, 0:2 * D]).then_inc(setup.sem, 1)
            dve.wait_ge(*setup.at(0, "b"))
            for hd in range(NH):
                for d in range(2):
                    ins = dve.tensor_tensor(bT[:, d].rearrange("p j r (h s) -> p h (j r) s", h=NH)[:, hd],
                                            bank[0:DH, hd, d * T:(d + 1) * T].rearrange("p (a s) -> p a s", s=TS),
                                            gate0[:, hd, :].rearrange("p (a s) -> p a s", s=TS), ALU.mult)
            ins.then_inc(setup.sem, 1)
            for half in range(2):
                dve.wait_ge(*setup.at(0, ("turn0", "turn1")[half]))
                dve.tensor_copy(bmat[:].rearrange("p j r d -> p (j r) d")[:, half * 7:half * 7 + 7], bank[0:RB, 0:7, D:2 * D]).then_inc(setup.sem, 1)
            dve.wait_ge(*setup.at(0, "m"))
            dve.memset(mmat[:, 0], 0.0).then_inc(setup.sem, 1)
            for j in range(1, J):
                dve.wait_ge(*setup.at(0, ("m", j - 1)))
                dve.scalar_tensor_tensor(mmat[:, j].rearrange("p e d -> p (e d)"), mmat[:, j - 1].rearrange("p e d -> p (e d)"),
                                              DECAY ** TC, bank[0:DH, j - 1, 0:2 * D], ALU.mult, ALU.add).then_inc(setup.sem, 1)
            dve.wait_ge(*setup.at(0, ("m", J - 1)))
            dve.memset(ones, 1.0)
            dve.memset(nhalf[:], -0.5)
            dve.memset(consts[:], MAGIC)
            dve.memset(xT[DH:DH + 1, 1, :], 1.0).then_inc(setup.sem, 1)
            dve.wait_ge(*setup.at(0, "sums"))
            dve.tensor_scalar(wsc[:, 2:3], bank[:, 0, 0:1], 1.0 / (2 * FH * D), None, ALU.mult)
            dve.tensor_scalar(wsc[:, 3:4], bank[:, 0, 1:2], 1.0 / (FH * D), None, ALU.mult).then_inc(setup.sem, 1)
            dve.wait_ge(*setup.at(0, "means"))
            dve.tensor_scalar(wsc[:, 4:6], wsc[:, 2:4], Q_EPS, None, ALU.max).then_inc(setup.sem, 1)
            dve.wait_ge(*setup.at(0, "floor"))
            dve.reciprocal(wsc[:, 6:8], wsc[:, 4:6]).then_inc(setup.sem, 1)
            prev = "inverse"
            for i, (parts, raw, whole) in enumerate(((DH, qraw.rearrange("p e f -> p (e f)"), qwi[:].rearrange("p e f -> p (e f)")),
                                                     (128, qraw2.rearrange("p f d -> p (f d)"), qwo[:].rearrange("p f d -> p (f d)")))):
                tmp = qtmp[0:parts, 0:raw.shape[1]]
                dve.wait_ge(*setup.at(0, prev))
                dve.tensor_scalar(tmp, raw, wsc[0:parts, 6 + i:7 + i], MAGIC, ALU.mult, ALU.add).then_inc(setup.sem, 1)
                dve.wait_ge(*setup.at(0, f"q{3 * i + 1}"))
                dve.tensor_scalar(tmp, tmp, MAGIC, 1.0, ALU.subtract, ALU.min).then_inc(setup.sem, 1)
                dve.wait_ge(*setup.at(0, f"q{3 * i + 2}"))
                dve.tensor_scalar(whole, tmp, -1.0, None, ALU.max).then_inc(setup.sem, 1)
                prev = f"q{3 * i + 3}"
            dve.wait_ge(*setup.at(0, prev))
            dve.memset(xT[DH:DH + 1, 1, :], 1.0).then_inc(setup.sem, 1)
            dve.wait_ge(*setup.at(0, "end"))

            def half(ap):
                return ap.rearrange("p (q t) -> p q t", q=2)

            def front(g, i):
                for p, (a, b) in enumerate(PAIRS):
                    w = (b - a) * NR * TT
                    if i == AT["sum"][p]:
                        dve.wait_ge(*filled(g, ("ao", p)))
                        xp = xln[:, a:b, :].rearrange("p j d -> p (j d)")
                        dve.scalar_tensor_tensor(xp, ps(("ao", p))[0:TT, 0:(b - a) * D], decp[:, 0:1], xp,
                                                 ALU.mult, ALU.add).then_inc(t_ready.sem, 1)
                for p, (a, b) in enumerate(PAIRS):
                    w = (b - a) * NR * TT
                    if i == AT["mask"][p]:
                        dve.wait_ge(*filled(g, ("sc", p)))
                        if p >= 2:
                            dve.wait_ge(*filled(g, ("ao", p - 2)))
                        dve.tensor_tensor(scT[:, p % 2, 0:b - a].rearrange("p j r t -> p j (r t)"),
                                          ps(("sc", p))[0:RB, 0:w].rearrange("p (j m) -> p j m", j=b - a),
                                          mask[:].unsqueeze(1).to_broadcast([RB, b - a, NR * TT]), ALU.mult).then_inc(scT_ready.sem, 1)
                    if i == AT["h2"][p]:
                        dve.wait_ge(*filled(g, ("fo", p)))
                        hp = h[:, a:b, :].rearrange("p j d -> p (j d)")
                        dve.tensor_tensor(hp, ps(("fo", p))[0:TT, 0:(b - a) * D], hp, ALU.add).then_inc(h2_ready.sem, 1)
                    for k, ready in ((1, h_ready), (2, h1_ready), (3, h2_ready)):
                        if i == AT[f"stats{k}"][p]:
                            dve.wait_ge(*ready.at(g, p))
                            for j in range(a, b):
                                ins = dve.bn_stats(stats[:, j, :], h[:, j, :])
                            if p == 3:
                                ins.then_inc(stats_ready.sem, 1)
                for k in (1, 2, 3):
                    if i == AT[f"norm{k}"][0]:
                        dve.wait_ge(*coef_ready.at(g, f"ln{k}"))
                        for p, (a, b) in enumerate(PAIRS):
                            for j in range(a, b):
                                ins = dve.tensor_scalar(xln[:, j, :], h[:, j, :], one(MEAN, j), one(RSTD, j), ALU.subtract, ALU.mult)
                            ins.then_inc(xln_ready.sem, 1)

            def mixer(g):
                dve.wait_ge(*stored.last_turn(g, "s", 15))
                dve.memset(hidp[:, :, :, 0:K - 1], 0.0).then_inc(conv_step.sem, 1)
                dve.wait_ge(*conv_step.at(g, "pad"))
                for c in range(IC):
                    dve.wait_ge(*hid_ready.at(g, c))
                    acc = hh[:, c, :].rearrange("p (b t) -> p b t", t=T)
                    dve.tensor_scalar(acc, hidp[:, c % 2, :, K - 1:], cw[:, c, K - 1:K], cvec[:, 0, c:c + 1],
                                      ALU.mult, ALU.add).then_inc(conv_step.sem, 1)
                    for i, k in enumerate(range(K - 1)):
                        dve.wait_ge(*conv_step.at(g, (c, i)))
                        dve.scalar_tensor_tensor(acc, hidp[:, c % 2, :, k:k + T], cw[:, c, k:k + 1], acc,
                                                 ALU.mult, ALU.add).then_inc(conv_step.sem, 1)
                dve.wait_ge(*filled(g, ("bc", 0)))
                src = ps(("bc", 0))[0:96, :, 0:HB]
                dve.tensor_copy(half(stk[:, :]), src).then_inc(bc_step.sem, 1)
                dve.wait_ge(*bc_step.at(g, 0))
                dve.tensor_tensor(half(bcr), src, half(stk[:, :]), ALU.subtract).then_inc(bc_step.sem, 1)
                dve.wait_ge(*bc_step.at(g, 1))
                dve.tensor_copy(midb, bcr).then_inc(bc_step.sem, 1)
                dve.wait_ge(*bc_step.at(g, 2))
                dve.tensor_copy(stk[32:64, :], midb[32:64, :]).then_inc(bc_step.sem, 1)
                dve.tensor_tensor(stk[64:96, :], bcr[64:96, :], midb[64:96, :], ALU.subtract).then_inc(bc_step.sem, 1)
                for c in range(IC):
                    dve.wait_ge(*sp_step.at(g, (c, 3)))
                    dve.scalar_tensor_tensor(dt[:, c, :], sp[:, c % 2, 0, :], 0.0, sp[:, c % 2, 1, :], ALU.max, ALU.add).then_inc(dt_ready.sem, 1)
            def units(g, nxt):
                dve.wait_ge(*emptied(g, "dA", 0))
                dve.memset(bank[:, 0:2, 0:HB].rearrange("p q (b t) -> p q b t", t=T)[:, :, :, 0:1], 0.0).then_inc(dA_zero.sem, 1)


                def unit(i):
                    c, n = divmod(i, N)
                    dve.wait_ge(*bc_full.at(g, c, n if c else 2 * n))
                    dve.wait_ge(*st_ready[1].at(g, c, n - 1))
                    dve.tensor_tensor(half(dbu[:, :]), half(u[:, c, :]), bank[:, 2:4, 0:HB], ALU.mult).then_inc(dbu_ready.sem, 1)
                    dve.wait_ge(*dbu_ready.at(g, c, n))
                    dve.wait_ge(*cs_used.at(g, c, n - 3))
                    for q in range(2):
                        dve.wait_ge(*dA_full[q].at(g, c, n))
                        cols = slice(q * HB, (q + 1) * HB)
                        dve.tensor_tensor_scan(st[:, i % 3, cols], bank[:, q, 0:HB], dbu[:, cols], 0.0,
                                               ALU.mult, ALU.add).then_inc(st_ready[q].sem, 1)

                def y_sum(c):
                    dve.wait_ge(*cs_used.at(g, c, N - 1))
                    dve.scalar_tensor_tensor(half(u[:, c, :]), half(hh[:, c, :]), cvec[:, 2, c:c + 1], bank[:, 4:6, 0:HB],
                                             ALU.mult, ALU.add).then_inc(ysum_ready.sem, 1)

                for i in range(UNITS):
                    c, n = divmod(i, N)
                    if n == 0:
                        dve.wait_ge(*u_step.at(g, (c, 1)))
                    unit(i)
                    if c and n == 1:
                        y_sum(c - 1)
                    if nxt is not None:
                        front(nxt, i)
                y_sum(IC - 1)

            def back(g):
                for p, (a, b) in enumerate(PAIRS):
                    dve.wait_ge(*filled(g, ("op", p)))
                    if p == 0:
                        dve.wait_ge(*hb_loaded.at(g, "s", 15))
                    hp = hb[:, a:b, :].rearrange("p j d -> p (j d)")
                    dve.tensor_tensor(hp, ps(("op", p))[0:TT, 0, 0:(b - a) * D], hp, ALU.add).then_inc(h3_ready.sem, 1)
                for p, (a, b) in enumerate(PAIRS):
                    dve.wait_ge(*h3_ready.at(g, p))
                    for j in range(a, b):
                        ins = dve.bn_stats(stats_b[:, j, :], hb[:, j, :])
                ins.then_inc(stats4_ready.sem, 1)
                dve.wait_ge(*coef4_ready.at(g, "ln4"))
                for j in range(J):
                    ins = dve.tensor_scalar(xb[:, j, :], hb[:, j, :], one(MEAN, j, small_b), one(RSTD, j, small_b), ALU.subtract, ALU.mult)
                ins.then_inc(xb_ready.sem, 1)
                dve.wait_ge(*xg_ready.at(g, 0))
                dve.tensor_reduce(col(PEAK, small_b), xb, AX_X, ALU.max, apply_absolute_value=True).then_inc(peak_ready.sem, 1)
                dve.wait_ge(*floor_ready.at(g, 1))
                dve.reciprocal(col(T1, small_b), col(PEAK, small_b)).then_inc(rcp_ready.sem, 1)
                dve.wait_ge(*scale_ready.at(g, 1))
                for j in range(J):
                    ins = dve.tensor_scalar(xb[:, j, :], xb[:, j, :], one(QS, j, small_b), MAGIC, ALU.mult, ALU.add)
                ins.then_inc(qr_ready.sem, 1)
                dve.wait_ge(*qr_ready.at(g, 0))
                dve.tensor_scalar(qx, xb, MAGIC, 127.0, ALU.subtract, ALU.min).then_inc(qx_ready.sem, 1)

                def peak2(j):
                    dve.wait_ge(*r2_ready.at(g, j))
                    dve.tensor_reduce(one(PEAK2, j, small_b), y2[:, j, :], AX_X, ALU.max, apply_absolute_value=True).then_inc(peak_ready.sem, 1)

                for j in range(J):
                    dve.wait_ge(*sgl_ready.at(g, j))
                    dve.scalar_tensor_tensor(y2[:, j, :], ps(("fi", j))[0:TT, 0, :], one(SC, j, small_b), sgl[:, j % 2, :],
                                             ALU.mult, ALU.mult).then_inc(y2_ready.sem, 1)
                    if j > 1:
                        peak2(j - 2)
                peak2(J - 2)
                peak2(J - 1)
                dve.wait_ge(*floor_ready.at(g, 2))
                dve.reciprocal(col(T1, small_b), col(PEAK2, small_b)).then_inc(rcp_ready.sem, 1)
                for j in range(J):
                    dve.wait_ge(*q2r_ready.at(g, j))
                    dve.tensor_scalar(q2[:, j, :], y2[:, j, :], MAGIC, 127.0, ALU.subtract, ALU.min).then_inc(q2_ready.sem, 1)
                for p, (a, b) in enumerate(PAIRS):
                    dve.wait_ge(*filled(g, ("out", p)))
                    for j in range(a, b):
                        dve.scalar_tensor_tensor(ob[:, j, :], ps(("out", p))[0:TT, 0, (j - a) * D:(j - a + 1) * D], one(SC2, j, small_b),
                                                 hb[:, j, :], ALU.mult, ALU.add).then_inc(o_ready.sem, 1)

            def turn(g, nxt):
                mixer(g)
                units(g, nxt)
                back(g)

            for i in range(UNITS):
                front(0, i)
            with dve.Fori(0, NG - 1) as g:
                turn(g, g + 1)
            turn(NG - 1, None)

        @block.gpsimd
        def _(pool):
            for sig in credited:
                pool.sem_inc(sig.sem, sig.credit)
            pool.wait_ge(*setup.at(0, "x0 mean"))
            pool.tensor_scalar(x0m[:, :, 1], x0m[:, :, 1], LN_EPS, None, ALU.add)
            pool.memset(nhalf[:], -0.5).then_inc(setup.sem, 1)
            pool.wait_ge(*setup.at(0, "x0 var"))
            pool.tensor_tensor(x0m[:, :, 1], x0m[:, :, 1], nhalf[0:98, 0:2], ALU.pow).then_inc(setup.sem, 1)
            pool.wait_ge(*setup.at(0, "end"))
            links = [0, 0]

            def front_step(g, ins):
                links[0] += 1
                ins.then_inc(front_link, 1)
                pool.wait_ge(front_link, g * FRONT_LINKS + links[0])
                pool.nop(nofuse=True)

            def back_step(g, ins):
                links[1] += 1
                ins.then_inc(back_link, 1)
                pool.wait_ge(back_link, g * BACK_LINKS + links[1])
                pool.nop(nofuse=True)

            def coef(g, stats, small, step):
                mean_e, m2_e, mean_o, m2_o = (stats[:, :, i] for i in (1, 2, 4, 5))
                mean2, diff, mean, var, t1, t2, rstd = (col(i, small) for i in (MEAN2, DIFF, MEAN, VAR, T1, T2, RSTD))
                pool.tensor_tensor(mean2, mean_e, mean_o, ALU.add)
                pool.tensor_tensor(t1, m2_e, m2_o, ALU.add)
                step(g, pool.tensor_tensor(diff, mean_e, mean_o, ALU.subtract))
                pool.tensor_scalar(mean, mean2, 0.5, None, ALU.mult)
                pool.tensor_scalar(t1, t1, 1.0 / D, None, ALU.mult)
                step(g, pool.tensor_tensor(diff, diff, diff, ALU.mult))
                step(g, pool.tensor_scalar(diff, diff, 0.25, None, ALU.mult))
                step(g, pool.tensor_tensor(var, diff, t1, ALU.add))
                step(g, pool.tensor_scalar(t2, var, LN_EPS, None, ALU.add))
                return pool.tensor_tensor(rstd, t2, nhalf[:], ALU.pow)

            def front(g, i):
                for k in (1, 2, 3):
                    if i == AT[f"coef{k}"][0]:
                        pool.wait_ge(*stats_ready.at(g, f"ln{k}"))
                        pool.nop(nofuse=True)
                        coef(g, stats, small, front_step).then_inc(coef_ready.sem, 1)
                for p, (a, b) in enumerate(PAIRS):
                    if i == AT["h1"][p]:
                        pool.wait_ge(*t_ready.at(g, p))
                        pool.nop(nofuse=True)
                        pool.tensor_tensor(h[:, a:b, :], h[:, a:b, :], xln[:, a:b, :], ALU.add).then_inc(h1_ready.sem, 1)

            def mixer(g):
                for c in range(IC):
                    pool.wait_ge(*dt_ready.at(g, c))
                    pool.nop(nofuse=True)
                    last = dt[:, c, :].rearrange("p (b t) -> p b t", t=T)[:, :, T - 1]
                    pool.tensor_scalar(last, last, cvec[:, 3, c:c + 1], None, ALU.mult).then_inc(u_step.sem, 1)
                    pool.wait_ge(*u_step.at(g, (c, 0)))
                    pool.wait_ge(*hh_ready.at(g, c))
                    pool.nop(nofuse=True)
                    pool.tensor_tensor(u[:, c, :], dt[:, c, :], hh[:, c, :], ALU.mult).then_inc(u_step.sem, 1)

            def units(g, nxt):
                for i in range(UNITS):
                    c, n = divmod(i, N)
                    pool.wait_ge(*st_ready[1].at(g, c, n))
                    if c == 0:
                        pool.wait_ge(*cb_ready.at(g, "c", n))
                    pool.nop(nofuse=True)
                    pool.tensor_tensor(st[:, i % 3, :], st[:, i % 3, :], cb[:, n, :], ALU.mult).then_inc(cs_ready.sem, 1)
                    if c and n == 2:
                        gated(g, c - 1)
                    if nxt is not None:
                        front(nxt, i)
                gated(g, IC - 1)

            def gated(g, c):
                pool.wait_ge(*ysum_ready.at(g, c))
                pool.wait_ge(*sg_ready.at(g, c))
                pool.nop(nofuse=True)
                pool.tensor_tensor(hh[:, c, :].rearrange("p (j b t) -> p b j t", j=J, b=GB),
                                   u[:, c, :].rearrange("p (b j t) -> p b j t", j=J, b=GB),
                                   sg[:, c, :].rearrange("p (b j t) -> p b j t", j=J, b=GB), ALU.mult).then_inc(yg_step.sem, 1)
                pool.wait_ge(*yg_step.at(g, (c, 0)))
                pool.nop(nofuse=True)
                last = hh[:, c, :].rearrange("p (j b t) -> p j b t", j=J, b=GB)[:, J - 1, :, TC - 1]
                pool.tensor_scalar(last, last, cvec[:, 4, c:c + 1], None, ALU.mult).then_inc(yg_step.sem, 1)

            def back(g):
                pool.wait_ge(*stats4_ready.at(g, "ln4"))
                pool.nop(nofuse=True)
                coef(g, stats_b, small_b, back_step).then_inc(coef4_ready.sem, 1)
                pool.wait_ge(*coef4_ready.at(g, "ln4"))
                pool.nop(nofuse=True)
                back_step(g, pool.tensor_tensor(col(T2, small_b), col(RSTD, small_b), col(RSTD, small_b), ALU.mult))
                back_step(g, pool.tensor_tensor(col(T2, small_b), col(T2, small_b), col(VAR, small_b), ALU.mult))
                back_step(g, pool.tensor_scalar(col(T2, small_b), col(T2, small_b), RMS_EPS, None, ALU.add))
                back_step(g, pool.tensor_tensor(col(RINV, small_b), col(T2, small_b), nhalf[:], ALU.pow))
                pool.wait_ge(*xb_ready.at(g, 0))
                pool.nop(nofuse=True)
                for j in range(J):
                    ins = pool.tensor_tensor(xb[:, j, :], xb[:, j, :], gin[:], ALU.mult)
                ins.then_inc(xg_ready.sem, 1)

                def quant_scale(i, peak, rinv, scale, qscale):
                    back_step(g, pool.tensor_tensor(col(peak, small_b), col(peak, small_b), col(rinv, small_b), ALU.mult))
                    back_step(g, pool.tensor_scalar(col(peak, small_b), col(peak, small_b), Q_EPS, None, ALU.max))
                    pool.tensor_scalar(col(scale, small_b), col(peak, small_b), 1.0 / 127.0, wsc[0:TT, 3 + i:4 + i], ALU.mult, ALU.mult).then_inc(floor_ready.sem, 1)
                    pool.wait_ge(*rcp_ready.at(g, i))
                    pool.nop(nofuse=True)
                    back_step(g, pool.tensor_tensor(col(T2, small_b), col(T1, small_b), col(rinv, small_b), ALU.mult))
                    pool.tensor_scalar(col(qscale, small_b), col(T2, small_b), 127.0, None, ALU.mult).then_inc(scale_ready.sem, 1)

                pool.wait_ge(*peak_ready.at(g, 0))
                pool.nop(nofuse=True)
                quant_scale(1, PEAK, RINV, SC, QS)
                for j in range(J):
                    pool.wait_ge(*ss_ready.at(g, j))
                    pool.nop(nofuse=True)
                    pool.tensor_tensor(y2[:, j, :], y2[:, j, :], gout[:], ALU.mult).then_inc(r2_ready.sem, 1)
                pool.wait_ge(*rcp_ready.at(g, 1))
                pool.nop(nofuse=True)
                back_step(g, pool.tensor_scalar(col(T2, small_b), col(SS, small_b), 1.0 / FH, RMS_EPS, ALU.mult, ALU.add))
                back_step(g, pool.tensor_tensor(col(RINV2, small_b), col(T2, small_b), nhalf[:], ALU.pow))
                pool.wait_ge(*peak_ready.at(g, J))
                pool.nop(nofuse=True)
                quant_scale(2, PEAK2, RINV2, SC2, QS2)

            def turn(g, nxt):
                links[0] = links[1] = 0
                mixer(g)
                units(g, nxt)
                back(g)
                assert links == [FRONT_LINKS if nxt is not None else 0, BACK_LINKS], links

            for i in range(UNITS):
                front(0, i)
            with pool.Fori(0, NG - 1) as g:
                turn(g, g + 1)
            turn(NG - 1, None)


def kernel(**inputs):
    import numpy as np
    import concourse.bacc as bacc
    from concourse.bass_utils import run_bass_kernel_spmd

    a = {k: np.asarray(v) for k, v in inputs.items()}

    def halves(w):
        return w.reshape(2, DH, -1).transpose(1, 0, 2)

    def blocks(w, p=128):
        return w.reshape(-1, p, w.shape[-1]).transpose(1, 0, 2)

    x = a["x"].reshape(B, 3, 14, 16, 14, 16).transpose(3, 5, 1, 0, 2, 4)
    x = x.reshape(KC, 128, NG, GB, J, TC)
    patches = x.transpose(2, 1, 4, 0, 3, 5).reshape(NG, 128, J, KC, TT)
    first = x[:, :, 0, 0].reshape(KC, 128, T).transpose(1, 0, 2)
    bias = a["L0_ffn_in_bias"].reshape(1, 1, HID)
    ffn_in = np.concatenate([halves(a["L0_ffn_in_weight"].T), np.concatenate([np.zeros_like(bias), bias], 1)], 0)
    xp = a["L1_attn_x_proj_w"].T
    bc = np.concatenate([xp[:, R:]] * 3, 1)
    steps = np.arange(TC)
    sigma = np.arange(TS)
    row_step = np.tile(sigma, NH)[:, None, None] + TS * np.arange(NR)[None, :, None]
    col_step = np.tile(steps, GB)[None, None, :]
    mask = (row_step < col_step).astype(np.float32).reshape(RB, -1)
    decp = (DECAY ** np.tile(steps, GB)).astype(np.float32)[:, None]
    dec = np.broadcast_to((WRITE * DECAY ** (-1.0 - np.arange(T) % TC)).astype(np.float32), (DH, T))
    bf = mybir.dt.np(BF16)
    sel = np.concatenate([np.eye(32, dtype=np.float32)] * 3, 0).astype(bf)
    eye = np.eye(128, dtype=np.float32)
    vec = lambda v: v.reshape(IC, 128).T
    arrays = dict(
        xt=patches, x0t=first, w_tok=blocks(a["L0_tok_W"].T), w_key=blocks(a["L0_attn_w_key"], DK),
        w_query=blocks(a["L0_attn_w_query"], DK), w_value=blocks(a["L0_attn_w_value"], DK),
        w_outt=blocks(a["L0_attn_w_out"].T, DK), w_gate=halves(a["L0_attn_w_gate"].T), ffn_in=ffn_in,
        ffn_out=blocks(a["L0_ffn_out_weight"]), w_inp=halves(a["L1_attn_in_proj_w"].T),
        conv_w=a["L1_attn_conv_w"].reshape(IC, 128, K).transpose(1, 0, 2), conv_b=vec(a["L1_attn_conv_b"]),
        w_xp=blocks(xp[:, :R]), w_bc=blocks(bc), w_dt=a["L1_attn_dt_proj_w"].T, b_dt=vec(a["L1_attn_dt_proj_b"]),
        a_log=blocks(a["L1_attn_A_log"]), d_skip=vec(a["L1_attn_D"]), w_op=blocks(a["L1_attn_out_proj_w"].T),
        alpha=vec(a["L1_attn_alpha"]), fgate=vec(a["L1_attn_feature_gating"]),
        q_in=halves(a["L1_ffn_w_in"].T), g_in=a["L1_ffn_g_in"], q_out=blocks(a["L1_ffn_w_out"].T),
        g_out=a["L1_ffn_g_out"], ident_c=eye, identb_c=eye.astype(bf), mask_c=mask, dec_c=dec, decp_c=decp, sel_c=sel)
    arrays = {k: np.ascontiguousarray(v) for k, v in arrays.items()}

    nc = bacc.Bacc("TRN2", target_bir_lowering=False, num_devices=1)
    aps = {k: nc.dram_tensor(f"in_{k}", v.shape, mybir.dt.from_np(v.dtype), kind="ExternalInput").ap() for k, v in arrays.items()}
    saved = nc.dram_tensor("saved_h2", (NG, TT, J, D), F32).ap()
    out = nc.dram_tensor("out_tiles", (NG, TT, J, D), F32, kind="ExternalOutput").ap()
    program(nc, saved=saved, out=out, **aps)
    r = run_bass_kernel_spmd(nc, [{f"in_{k}": v for k, v in arrays.items()}], core_ids=[0])
    tiles = np.asarray(r.results[0]["out_tiles"]).reshape(NG, GB, TC, J, D)
    return np.ascontiguousarray(tiles.transpose(0, 1, 3, 2, 4).reshape(B, T, D))
```

```python
from contextlib import ExitStack

import concourse.bass as bass
from concourse import mybir

ALU = mybir.AluOpType
ACT = mybir.ActivationFunctionType
AX_X = mybir.AxisListType.X
F32 = mybir.dt.float32
BF16 = mybir.dt.bfloat16

B, T, D, PIX = 64, 196, 192, 768
GB = 4
NG = B // GB
TC = 28
J = T // TC
TT = GB * TC
GT = GB * T
HB = GT // 2
DH = D // 2
KC = PIX // 128
NH, DK = 8, 64
TS = 14
NR = TC // TS
RB = NH * TS
HID = 768
HC = HID // 128
I, N, R, K = 384, 16, 48, 4
IC = I // 128
FH = 512
FC = FH // 128
DECAY, WRITE = 0.95, 0.1
LN_EPS, RMS_EPS, Q_EPS = 1e-5, 1e-6, 1e-5
MAGIC = 12582912.0
PAIRS = [(0, 2), (2, 4), (4, 6), (6, 7)]
XBUF = 4
UNITS = IC * N
AT = dict(
    tok=(0, 1, 3, 4), embed=(1, 2, 4, 5), stats1=(2, 3, 5, 6), coef1=(7,), norm1=(9,),
    tr1=(10, 10, 11, 11), turn1=(11, 11, 12, 12), sc=(13, 13, 15, 17), mask=(14, 14, 16, 18), ao=(15, 17, 19, 19),
    sum=(16, 18, 20, 20), h1=(17, 19, 21, 21), stats2=(18, 20, 22, 22), coef2=(23,), norm2=(25,),
    tr2=(26, 26, 27, 27), turn2=(27, 27, 28, 28),
    hid=(28, 28, 29, 32, 32, 33, 36, 36, 37, 40, 40, 41), gelu=(29, 29, 30, 33, 33, 34, 37, 37, 38, 41, 41, 42),
    fo=(31, 35, 39, 43), h2=(32, 36, 40, 44), stats3=(33, 37, 41, 44), coef3=(45,), norm3=(47,),
    tr3=(47, 47, 47, 47), turn3=(47, 47, 47, 47))
BEAT = dict(
    inp=(0, 0, 1, 4, 5, 6), hid=(0, 0, 1), conv=(0, 1, 2), gate=(4, 5, 6), act=(1, 2, 3), xp=2, ts=3, split=4,
    dtp=(3, 4, 5), x=(3, 4, 5), softplus=17, dt=19, u=19,
    op=(1, 1, 1, 1), h3=(2, 2, 2, 2), coef4=3, norm4=4, peak=4, scale=5, round=5, qt=7, turn=7,
    fi=(9, 10, 11, 12, 13, 14, 15), y2=(9, 10, 11, 12, 13, 14, 15), square=(10, 11, 12, 13, 14, 15, 16),
    gain2=(10, 11, 12, 13, 14, 15, 16), peak2=(11, 12, 13, 14, 15, 16, 17), scale2=17, round2=18, q2t=19)
BEATS = 20


class Signal:

    def __init__(self, sem, order, credit=0):
        self.sem = sem
        self.start, n = {}, 0
        for key, count in order:
            self.start[key] = n
            n += count
        self.per_turn = n
        self.credit = n if credit == "turn" else credit

    def at(self, g, key, extra=0):
        return self.sem, g * self.per_turn + (extra + (self.start[key] + 1 + self.credit))


def program(nc, xt, x0t, w_tok, w_key, w_query, w_value, w_outt, w_gate, ffn_in, ffn_out,
            w_inp, conv_w, conv_b, w_xp, w_bc, w_dt, b_dt, a_log, d_skip, w_op, alpha, fgate,
            q_in, g_in, q_out, g_out, ident_c, identb_c, mask_c, dec_c, decp_c, sel_c, saved, out):
    with ExitStack() as ctx:
        def sb(name, shape, dt=F32):
            return ctx.enter_context(nc.sbuf_tensor(name, shape, dt))

        def sem(name):
            return ctx.enter_context(nc.semaphore(name))

        bank = ctx.enter_context(nc.psum_tensor("bank", [128, 8, 512], F32))
        ident = sb("ident", [128, 128])
        identb = sb("identb", [128, 128], BF16)
        mask = sb("mask", [RB, NR * TT])
        decp = sb("decp", [TT, 1])
        sel = sb("sel", [96, 2 * N], BF16)
        wtok = sb("wtok", [128, KC, D])
        wfi = sb("wfi", [DH + 1, 2, HID])
        wfo = sb("wfo", [128, HC, D])
        winp = sb("winp", [DH, 2, 2 * I])
        wxp = sb("wxp", [128, IC, R])
        wbc = sb("wbc", [128, IC, 96])
        wdt = sb("wdt", [R, I])
        wop = sb("wop", [128, IC, D])
        cw = sb("cw", [128, IC, K])
        cvec = sb("cvec", [128, 5, IC])
        amat = sb("amat", [128, IC, N])
        qwi = sb("qwi", [DH, 2, 2 * FH], BF16)
        qwo = sb("qwo", [128, FC, D], BF16)
        gin = sb("gin", [TT, D])
        gout = sb("gout", [TT, FH])
        wsc = sb("wsc", [128, 16])
        amask = sb("amask", [DH, 2, J, NR, RB])
        bmat = sb("bmat", [RB, J, NR, D])
        mmat = sb("mmat", [DH, J, 2, D])
        xst = sb("xst", [128, XBUF, KC, TT])
        h = sb("h", [TT, J, D])
        xln = sb("xln", [TT, J, D])
        stats, stats_b = sb("stats", [TT, J, 6]), sb("stats_b", [TT, J, 6])
        small, small_b = sb("small", [TT, 16, J]), sb("small_b", [TT, 16, J])
        xT = sb("xT", [DH + 1, 2, GT])
        scT = sb("scT", [RB, 2, 2, NR, TT])
        gT = sb("gT", [128, HC, 2 * TT])
        mix = sb("mix", [128, 4, IC, GT])
        hh, dt, sg, u = (mix[:, i] for i in range(4))
        dbu = sb("dbu", [128, GT])
        st = sb("st", [128, 3, GT])
        stk = sb("stk", [96, GT], BF16)

        arena = sb("arena", [128, N, GT])
        consts = sb("consts", [128, 4])
        nhalf = sb("nhalf", [TT, J])

        class Carve:

            def __init__(self, whole):
                self.whole, self.used = whole, 0

            def __call__(self, parts, shape, dt=F32):
                n = 1
                for s in shape:
                    n *= s
                words = n if dt == F32 else (n + 1) // 2
                ap = self.whole[0:parts, self.used:self.used + words]
                self.used += words
                assert self.used <= self.whole.shape[1]
                if dt != F32:
                    ap = ap.bitcast(dt)
                if len(shape) == 1:
                    return ap
                names = "abcd"[:len(shape)]
                return ap.rearrange(f"p ({' '.join(names)}) -> p {' '.join(names)}",
                                    **{names[i]: shape[i] for i in range(len(shape))})

        cb = arena
        flat = arena[:].rearrange("p n t -> p (n t)")
        cv = Carve(flat)
        x0, x0ln, x0T = cv(128, [KC, T]), cv(98, [2, D]), cv(DH, [2, T])
        wk, wq, gk = cv(DK, [NH, D]), cv(DK, [NH, D]), cv(DH, [NH, 2, D])
        wg, wgr, gate0, dec = cv(DH, [2, NH]), cv(DH, [2, NH, DH]), cv(DH, [NH, T]), cv(DH, [T])
        cv2 = Carve(mix[:].rearrange("p a c t -> p (a c t)"))
        bT, arow, x0s, x0m = cv2(DH, [2, J, NR, RB]), cv2(RB, [J, NR, D]), cv2(98, [2, 6]), cv2(98, [2, 2])
        wv, wo = cv2(DK, [NH, D]), cv2(DK, [NH, D])
        cvq = Carve(flat)
        qraw, qraw2 = cvq(DH, [2, 2 * FH]), cvq(128, [FC, D])
        qtmp, ones = cvq(128, [2 * 2 * FH]), cvq(128, [128])
        ck = Carve(flat)
        q2 = ck(TT, [J, FH], BF16)
        y2, sgl, q2T = ck(TT, [J, FH]), ck(TT, [2, FH]), ck(128, [2, 2 * FC * TT], BF16)
        hb = ck(TT, [J, D])
        hidp = ck(128, [2, GB, K - 1 + T])
        midb = ck(96, [GT], BF16)
        C_OVER_OUT = (N * GT - J * D) // GT
        assert ck.used <= N * GT - J * D
        xb = flat[0:TT, N * GT - J * D:].rearrange("p (j d) -> p j d", d=D)
        ob = xb
        cq = Carve(flat)
        qx, qT = cq(TT, [J, D], BF16), cq(DH, [2, GT], BF16)
        over = hidp.rearrange("p a b t -> p (a b t)")
        tsT, bcr = over[0:R, 0:GT], over[0:96, GT:2 * GT]
        xbt = xT[0:DH].rearrange("p e (b t) -> p e b t", b=GB)

        credited = []

        def counted(name, *order, credit="turn"):
            sig = Signal(sem(name), list(order), credit)
            if sig.credit:
                credited.append(sig)
            return sig

        def signal(name, *keys, credit="turn"):
            return counted(name, *[(k, 1) for k in keys], credit=credit)

        s_w = sem("weights_loaded")
        s_qw = sem("quant_weights_loaded")
        SETUP = ("x0 tok", "x0 stats", "x0 mean", "x0 var", "x0 pow", "x0 ln", "x0 turn", "x0T", "gk a", "gk a in", "a", "a in",
                 "gate rep", "gate", "gate in", "gate dec", "gk b", "gk b in", "b", "b in", "turn0", "turn0 b", "turn0 a", "turn1", "turn1 b", "turn1 a", "m") \
            + tuple(("m", j) for j in range(J)) + ("consts", "A exp", "A neg", "sums in", "sums out", "sums", "means", "floor", "inverse",
                                                   "q1", "q2", "q3", "q4", "q5", "q6", "end")
        setup = signal("setup_step", *SETUP, credit=0)

        front_use = [(s, p) for s in ("tok", "tr1") for p in range(4)]
        front_use += [("sc", 0), ("sc", 1), ("ao", 0), ("sc", 2), ("ao", 1), ("sc", 3), ("ao", 2), ("ao", 3)]
        front_use += [("tr2", p) for p in range(4)]
        for p in range(4):
            front_use += [("hid", 3 * p + i) for i in range(3)] + [("fo", p)]
        front_use += [("tr3", p) for p in range(4)]
        mixer_use = [("inp", c) for c in range(IC)] + [("bc", 0), ("xp", 0)]
        for c in range(IC):
            mixer_use += [("dtp", c), ("inp", IC + c)]
        back_use = [("op", p) for p in range(4)] + [("qt", p) for p in range(4)] + [("fi", j) for j in range(J)]
        back_use += [("q2t", 0), ("q2t", 1), ("out", 0), ("q2t", 2), ("out", 1), ("q2t", 3), ("out", 2), ("out", 3)]
        where = {k: 6 + i % 2 for i, k in enumerate(front_use)}
        where.update({k: i % 2 for i, k in enumerate(mixer_use)})
        where.update({k: 2 + i % 2 for i, k in enumerate(back_use)})
        later = {k: 1 for k in front_use + mixer_use}
        placed = {0: ["dA"], 1: ["B"], 2: ["y"], 6: [], 7: []}
        for s in (0, 1, 2, 6, 7):
            placed[s] = placed[s] + [k for k in front_use + mixer_use + back_use if where[k] == s]
            if s > 5:
                placed[s] += [k for k in back_use if where[k] == 3]
        full = {k: None for k in (*front_use, *mixer_use, *back_use)}
        for name, use in (("front", front_use), ("mixer", mixer_use), ("back", back_use)):
            for s in sorted({where[k] for k in use}):
                sig = signal(f"psum_{name}{s}_full", *[k for k in use if where[k] == s])
                full.update({k: sig for k in use if where[k] == s})

        LN = ("ln1", "ln2", "ln3")
        four = range(4)
        x_loaded = [counted(f"x_loaded{i}", *[(p, 16) for p in four if p % 2 == i]) for i in range(2)]
        h_ready = signal("h_ready", *four)
        stats_ready = signal("stats_ready", *LN)
        coef_ready = signal("coef_ready", *LN)
        stats4_ready = signal("stats4_ready", "ln4")
        coef4_ready = signal("coef4_ready", "ln4")
        xln_ready = signal("xln_ready", *[(n, p) for n in LN for p in four])
        xT_ready = signal("xT_ready", *[(n, p) for n in ("tr1", "tr2") for p in four], *[("tr3", j) for j in range(J)])
        scT_ready = signal("scores_ready", *four)
        t_ready = signal("attn_sum_ready", *four)
        h1_ready = signal("h1_ready", *four)
        gT_ready = signal("gelu_ready", *range(12))
        h2_ready = signal("h2_ready", *four)
        h2_saved = counted("h2_saved", ("s", 16))
        hb_loaded = counted("h2_reloaded", ("s", 16))
        hid_ready = signal("hidden_ready", *range(IC))
        conv_step = signal("conv_step", "pad", *[(c, k) for c in range(IC) for k in four])
        hh_ready = signal("h_silu_ready", *range(IC))
        sg_ready = signal("gate_silu_ready", *range(IC))
        ts_ready = signal("ts_ready", 0)
        bc_step = signal("bc_split_step", *range(5))
        sp_step = signal("softplus_step", *[(c, k) for c in range(IC) for k in range(2)], "exp", "ln")
        dt_ready = signal("dt_sum_ready", *range(IC))
        u_step = signal("u_step", *[(c, k) for c in range(IC) for k in range(2)])
        dA_zero = signal("dA_zeroed", 0)
        dA_full = [counted(f"dA_full{q}", *[(c, N) for c in range(IC)]) for q in range(2)]
        bc_full = counted("spread_full", (0, 2 * N), (1, N), (2, N))
        dbu_ready = counted("dbu_ready", *[(c, N) for c in range(IC)])
        st_ready = [counted(f"state_ready{q}", *[(c, N) for c in range(IC)]) for q in range(2)]
        cb_ready = counted("c_spread_ready", ("c", N))
        cs_ready = counted("c_state_ready", *[(c, N) for c in range(IC)])
        cs_used = counted("c_state_summed", *[(c, N) for c in range(IC)])
        ysum_ready = signal("y_sum_ready", *range(IC))
        yg_step = signal("y_gated_step", *[(c, k) for c in range(IC) for k in range(2)])
        h3_ready = signal("h3_ready", *four)
        xb_ready = signal("xb_ready", 0)
        xg_ready = signal("x_gained", 0)
        peak_ready = signal("peak_ready", *range(1 + J))
        rcp_ready = signal("reciprocal_ready", 1, 2)
        floor_ready = signal("floor_ready", 1, 2)
        scale_ready = signal("scale_ready", 1, 2)
        qr_ready = signal("q_rounded", 0)
        qx_ready = signal("qx_ready", 0)
        qT_ready = signal("qT_ready", *four)
        sgl_ready = signal("silu_gate_ready", *range(J))
        y2_ready = signal("y2_ready", *range(J))
        ss_ready = signal("square_sum_ready", *range(J))
        r2_ready = signal("y2_gained", *range(J))
        q2r_ready = signal("q2_rounded", *four)
        q2_ready = signal("q2_ready", *four)
        q2T_ready = signal("q2T_ready", *four)
        o_ready = signal("o_ready", *range(J))
        stored = counted("stored", ("s", 16))
        FRONT_LINKS, BACK_LINKS = 15, 17
        front_link, back_link = sem("pool_front_link"), sem("pool_back_link")

        reader = {}
        for p, (a, b) in enumerate(PAIRS):
            reader[("tok", p)] = (h_ready, p)
            reader[("tr1", p)], reader[("tr2", p)] = (xT_ready, ("tr1", p)), (xT_ready, ("tr2", p))
            reader[("tr3", p)] = (xT_ready, ("tr3", b - 1))
            reader[("sc", p)], reader[("ao", p)], reader[("fo", p)] = (scT_ready, p), (t_ready, p), (h2_ready, p)
            for i in range(3):
                reader[("hid", 3 * p + i)] = (gT_ready, 3 * p + i)
            reader[("op", p)], reader[("qt", p)], reader[("out", p)] = (h3_ready, p), (qT_ready, p), (o_ready, b - 1)
        for c in range(IC):
            reader[("inp", c)], reader[("inp", IC + c)] = (hid_ready, c), (sg_ready, c)
            reader[("dtp", c)] = (sp_step, (c, 1))
        reader[("xp", 0)], reader[("bc", 0)] = (ts_ready, 0), (bc_step, 1)
        for j in range(J):
            reader[("fi", j)] = (y2_ready, j)
        for p in four:
            reader[("q2t", p)] = (q2T_ready, p)
        reader["dA"], reader["B"], reader["y"] = (st_ready[1], IC - 1, N - 1), (dbu_ready, IC - 1, N - 1), (ysum_ready, IC - 1)

        def filled(g, k):
            return full[k].at(g, k)

        def emptied(g, k):
            waits = []
            for s in ((6, 7) if where.get(k) == 3 else (where.get(k, {"dA": 0, "B": 1, "y": 2}.get(k)),)):
                uses = placed[s]
                i = uses.index(k)
                before, wrapped = uses[i - 1], i == 0
                if isinstance(g, int) and g == NG - 1 and k in back_use:
                    mine = [use for use in uses if not later.get(use, 0)]
                    before, wrapped = mine[mine.index(k) - 1], mine[0] == k
                turns = later.get(before, 0) - later.get(k, 0) - wrapped
                sig, *key = reader[before]
                waits.append((sig, turns, key))
            sig, turns, key = waits[-1]
            if isinstance(g, int) and g + turns < -1:
                return sig.sem, 1
            return sig.at(g + turns, *key)

        def full_of(k):
            return full[k].sem

        def ps(k):
            s = where[k]
            return bank[:, s, :] if s > 5 else bank[:, 2 * s:2 * s + 2, :]

        STAT = range(14)
        MEAN2, DIFF, VAR, RSTD, MEAN, RINV, PEAK, QS, SC, SS, T1, T2, RINV2, QS2 = STAT
        PEAK2, SC2 = 14, 15

        def col(i, of=small):
            return of[:, i, :]

        def one(i, j, of=small):
            return of[:, i, j:j + 1]

        loads = [(ident, ident_c), (identb, identb_c), (mask, mask_c), (decp, decp_c), (sel, sel_c), (wtok, w_tok),
                 (wfi, ffn_in), (wfo, ffn_out), (winp, w_inp), (wxp, w_xp), (wbc, w_bc), (wdt, w_dt),
                 (wop, w_op), (cw, conv_w), (amat, a_log)]
        loads = [(dst[:], src) for dst, src in loads]
        loads += [(gin[:], g_in.partition_broadcast(TT)), (gout[:], g_out.partition_broadcast(TT))]
        loads += [(cvec[:, i, :], v) for i, v in enumerate((conv_b, b_dt, d_skip, alpha, fgate))]
        loads += [(x0, x0t), (wk, w_key), (wq, w_query), (wv, w_value), (wo, w_outt), (wg, w_gate), (dec, dec_c)]
        W_ALL = 16 * len(loads)
        block = ctx.enter_context(nc.Block())

        @block.sync
        def _(sp):
            for dst, src in loads:
                sp.dma_start(dst, src).then_inc(s_w, 16)
            sp.wait_ge(*setup.at(0, ("m", J - 1)))
            sp.dma_start(qraw, q_in).then_inc(s_qw, 16)
            sp.dma_start(qraw2, q_out).then_inc(s_qw, 16)

            def load_tokens(g, pairs):
                for p in pairs:
                    a, b = PAIRS[p]
                    if p >= 2:
                        sp.wait_ge(*filled(g, ("tok", p - 2)))
                    else:
                        sp.wait_ge(*filled(g - 1, ("tok", p + 2)))
                    sp.nop(nofuse=True)
                    sp.dma_start(xst[:, 2 * (p % 2):2 * (p % 2) + b - a], xt[g, :, a:b]).then_inc(x_loaded[p % 2].sem, 16)

            def save(g):
                sp.wait_ge(*h2_ready.at(g, 3))
                sp.nop(nofuse=True)
                sp.dma_start(saved[g], h[:]).then_inc(h2_saved.sem, 16)

            def turn(g, nxt, after):
                if nxt is not None:
                    load_tokens(nxt, (2, 3))
                    save(nxt)
                    sp.wait_ge(*h2_saved.at(nxt, "s", 15))
                sp.wait_ge(*cs_ready.at(g, IC - 1, N - 1))
                sp.nop(nofuse=True)
                sp.dma_start(hb, saved[g]).then_inc(hb_loaded.sem, 16)
                if after is not None:
                    load_tokens(after, (0, 1))
                sp.wait_ge(*o_ready.at(g, J - 1))
                sp.nop(nofuse=True)
                sp.dma_start(out[g], ob).then_inc(stored.sem, 16)

            load_tokens(0, range(4))
            load_tokens(1, (0, 1))
            save(0)
            sp.wait_ge(*h2_saved.at(0, "s", 15))
            with sp.Fori(0, NG - 2) as g:
                turn(g, g + 1, g + 2)
            turn(NG - 2, NG - 1, None)
            turn(NG - 1, None, None)
            sp.wait_ge(*stored.at(NG - 1, "s", 15))

        @block.tensor
        def _(pe):
            pe.wait_ge(s_w, W_ALL)
            for t in range(2):
                for k in range(KC):
                    mm = pe.matmul(bank[0:98, t, 0:D], x0[:, k, t * 98:(t + 1) * 98], wtok[:, k, :], start=k == 0, stop=k == KC - 1)
            mm.then_inc(setup.sem, 1)
            pe.wait_ge(*setup.at(0, "x0 ln"))
            for t in range(2):
                for e in range(2):
                    mm = pe.transpose(bank[0:DH, 2, e * T + t * 98:e * T + (t + 1) * 98], x0ln[:, t, e * DH:(e + 1) * DH], ident[0:98, 0:98])
            mm.then_inc(setup.sem, 1)
            for side, (left, right, made) in enumerate(((wk, wq, "x0T"), (wv, wo, "gate dec"))):
                pe.wait_ge(*setup.at(0, made))
                for hd in range(NH):
                    for e in range(2):
                        mm = pe.matmul(bank[0:DH, hd, e * D:(e + 1) * D], left[:, hd, e * DH:(e + 1) * DH], right[:, hd, :], start=True, stop=True)
                mm.then_inc(setup.sem, 1)
                pe.wait_ge(*setup.at(0, ("gk a in", "gk b in")[side]))
                for hd in range(NH):
                    for d in range(2):
                        for e in range(2):
                            mm = pe.matmul(bank[0:DH, hd, d * T:(d + 1) * T], gk[:, hd, e, d * DH:(d + 1) * DH], x0T[:, e, :], start=e == 0, stop=e == 1)
                mm.then_inc(setup.sem, 1)
                if side == 0:
                    pe.wait_ge(*setup.at(0, "gate rep"))
                    for hd in range(NH):
                        for e in range(2):
                            mm = pe.matmul(bank[0:DH, hd, 0:T], wgr[:, e, hd, :], x0T[:, e, :], start=e == 0, stop=e == 1)
                    mm.then_inc(setup.sem, 1)
            for half in range(2):
                pe.wait_ge(*setup.at(0, ("b in", "turn0 a")[half]))
                for i in range(7):
                    jj, r = divmod(half * 7 + i, NR)
                    for d in range(2):
                        pe.transpose(bank[0:RB, i, d * DH:(d + 1) * DH], amask[:, d, jj, r, :], ident[0:DH, 0:DH])
                        mm = pe.transpose(bank[0:RB, i, D + d * DH:D + (d + 1) * DH], bT[:, d, jj, r, :], ident[0:DH, 0:DH])
                mm.then_inc(setup.sem, 1)
            pe.wait_ge(*setup.at(0, "turn1 a"))
            for j in range(J - 1):
                for d in range(2):
                    for r in range(NR):
                        mm = pe.matmul(bank[0:DH, j, d * D:(d + 1) * D], arow[:, j, r, d * DH:(d + 1) * DH], bmat[:, j, r, :],
                                       start=r == 0, stop=r == NR - 1)
            mm.then_inc(setup.sem, 1)
            pe.wait_ge(*setup.at(0, "sums out"))
            pe.matmul(bank[:, 0, 0:1], ones[0:DH, :], wsc[0:DH, 0:1], start=True, stop=True)
            pe.matmul(bank[:, 0, 1:2], ones[:, :], wsc[:, 1:2], start=True, stop=True).then_inc(setup.sem, 1)
            pe.wait_ge(*setup.at(0, "end"))

            def transposes(g, name, p, ln):
                a, b = PAIRS[p]
                pe.wait_ge(*emptied(g, (name, p)))
                pe.wait_ge(*xln_ready.at(g, (ln, p)))
                for e in range(2):
                    for j in range(a, b):
                        mm = pe.transpose(ps((name, p))[0:DH, e * (b - a) * TT + (j - a) * TT:e * (b - a) * TT + (j - a + 1) * TT],
                                          xln[:, j, e * DH:(e + 1) * DH], ident[0:TT, 0:TT])
                mm.then_inc(full_of((name, p)), 1)

            def attn_out(g, p):
                a, b = PAIRS[p]
                pe.wait_ge(*emptied(g, ("ao", p)))
                pe.wait_ge(*scT_ready.at(g, p))
                for j in range(a, b):
                    o = ps(("ao", p))[0:TT, (j - a) * D:(j - a + 1) * D]
                    for r in range(NR):
                        mm = pe.matmul(o, scT[:, p % 2, j - a, r, :], bmat[:, j, r, :], start=r == 0, stop=j == 0 and r == NR - 1)
                    if j:
                        for e in range(2):
                            mm = pe.matmul(o, xT[0:DH, e, j * TT:(j + 1) * TT], mmat[:, j, e, :], start=False, stop=e == 1)
                mm.then_inc(full_of(("ao", p)), 1)

            def front(g, i):
                for p in range(4):
                    if i == AT["tr3"][p]:
                        transposes(g, "tr3", p, "ln3")
                for p, (a, b) in enumerate(PAIRS):
                    if i == AT["tok"][p]:
                        pe.wait_ge(*emptied(g, ("tok", p)))
                        pe.wait_ge(*x_loaded[p % 2].at(g, p, 15))
                        for j in range(a, b):
                            for k in range(KC):
                                mm = pe.matmul(ps(("tok", p))[0:TT, (j - a) * D:(j - a + 1) * D], xst[:, 2 * (p % 2) + j - a, k, :],
                                               wtok[:, k, :], start=k == 0, stop=k == KC - 1)
                        mm.then_inc(full_of(("tok", p)), 1)
                    if i == AT["tr1"][p]:
                        transposes(g, "tr1", p, "ln1")
                    if i == AT["ao"][p]:
                        attn_out(g, p)
                for p, (a, b) in enumerate(PAIRS):
                    if i == AT["sc"][p]:
                        pe.wait_ge(*emptied(g, ("sc", p)))
                        pe.wait_ge(*xT_ready.at(g, ("tr1", p)))
                        for j in range(a, b):
                            for r in range(NR):
                                c0 = ((j - a) * NR + r) * TT
                                for e in range(2):
                                    mm = pe.matmul(ps(("sc", p))[0:RB, c0:c0 + TT], amask[:, e, j, r, :], xT[0:DH, e, j * TT:(j + 1) * TT],
                                                   start=e == 0, stop=e == 1)
                        mm.then_inc(full_of(("sc", p)), 1)
                    if i == AT["tr2"][p]:
                        transposes(g, "tr2", p, "ln2")
                for k in range(12):
                    if i == AT["hid"][k]:
                        p = k // 3
                        a, b = PAIRS[p]
                        w = (b - a) * TT
                        pe.wait_ge(*emptied(g, ("hid", k)))
                        pe.wait_ge(*xT_ready.at(g, ("tr2", p)))
                        for m in range(2):
                            hc = 2 * (k % 3) + m
                            for e in range(2):
                                kk = DH + e
                                mm = pe.matmul(ps(("hid", k))[:, m * w:(m + 1) * w], wfi[0:kk, e, hc * 128:(hc + 1) * 128],
                                               xT[0:kk, e, a * TT:b * TT], start=e == 0, stop=e == 1)
                        mm.then_inc(full_of(("hid", k)), 1)
                for p, (a, b) in enumerate(PAIRS):
                    if i == AT["fo"][p]:
                        pe.wait_ge(*emptied(g, ("fo", p)))
                        pe.wait_ge(*gT_ready.at(g, 3 * p + 2))
                        for j in range(a, b):
                            for hc in range(HC):
                                mm = pe.matmul(ps(("fo", p))[0:TT, (j - a) * D:(j - a + 1) * D], gT[:, hc, (j - a) * TT:(j - a + 1) * TT],
                                               wfo[:, hc, :], start=hc == 0, stop=hc == HC - 1)
                        mm.then_inc(full_of(("fo", p)), 1)

            def mixer(g, i):
                xf = xbt.rearrange("p e b t -> p e (b t)")
                for k in range(6):
                    if i == BEAT["inp"][k]:
                        pe.wait_ge(*emptied(g, ("inp", k)))
                        pe.wait_ge(*xT_ready.at(g, ("tr3", J - 1)))
                        for q in range(2):
                            for e in range(2):
                                mm = pe.matmul(ps(("inp", k))[:, q, 0:HB], winp[:, e, k * 128:(k + 1) * 128], xf[:, e, q * HB:(q + 1) * HB],
                                               start=e == 0, stop=e == 1)
                        mm.then_inc(full_of(("inp", k)), 1)
                if i == BEAT["xp"]:
                    for name, w, m in (("bc", wbc, 96), ("xp", wxp, R)):
                        pe.wait_ge(*emptied(g, (name, 0)))
                        pe.wait_ge(*hh_ready.at(g, IC - 1))
                        for q in range(2):
                            for c in range(IC):
                                mm = pe.matmul(ps((name, 0))[0:m, q, 0:HB], w[:, c, :], hh[:, c, q * HB:(q + 1) * HB], start=c == 0, stop=c == IC - 1)
                        mm.then_inc(full_of((name, 0)), 1)
                for c in range(IC):
                    if i == BEAT["dtp"][c]:
                        pe.wait_ge(*emptied(g, ("dtp", c)))
                        pe.wait_ge(*ts_ready.at(g, 0))
                        for q in range(2):
                            mm = pe.matmul(ps(("dtp", c))[:, q, 0:HB], wdt[:, c * 128:(c + 1) * 128], tsT[:, q * HB:(q + 1) * HB], start=True, stop=True)
                        mm.then_inc(full_of(("dtp", c)), 1)

            def units(g, nxt):
                pe.wait_ge(*bc_step.at(g, 4))
                pe.wait_ge(*emptied(g, "B"))

                def pick(n):
                    return sel[:, n:n + 1].to_broadcast([96, 128])

                def spread_b(c, n):
                    if c == 0 and n or (c, n) == (1, 0):
                        pe.wait_ge(*cb_ready.at(g, "c", N - 1 if c else n - 1))
                    if c:
                        pe.wait_ge(*dbu_ready.at(g, c, n - 1))
                    for q in range(2):
                        mm = pe.matmul(bank[:, 2 + q, 0:HB], pick(n), stk[:, q * HB:(q + 1) * HB], start=True, stop=True)
                    mm.then_inc(bc_full.sem, 1)

                def spread_c(n):
                    pe.wait_ge(*dbu_ready.at(g, 0, n))
                    for q in range(2):
                        mm = pe.matmul(bank[:, 2 + q, 0:HB], pick(n + N), stk[:, q * HB:(q + 1) * HB], start=True, stop=True)
                    mm.then_inc(bc_full.sem, 1)

                def sum_state(i):
                    c, n = divmod(i, N)
                    if i == 0:
                        pe.wait_ge(*emptied(g, "y"))
                    elif n == 0:
                        pe.wait_ge(*ysum_ready.at(g, c - 1))
                    pe.wait_ge(*cs_ready.at(g, c, n))
                    for q in range(2):
                        mm = pe.matmul(bank[:, 4 + q, 0:HB], ident[:, :], st[:, i % 3, q * HB:(q + 1) * HB], start=n == 0, stop=n == N - 1,
                                       skip_group_check=True)
                    mm.then_inc(cs_used.sem, 1)

                spread_b(0, 0)
                for i in range(UNITS):
                    if i < N:
                        spread_c(i)
                        if i:
                            sum_state(i - 1)
                        spread_b(*divmod(i + 1, N))
                        if nxt is not None:
                            front(nxt, i)
                    else:
                        if i + 1 < UNITS:
                            spread_b(*divmod(i + 1, N))
                        if nxt is not None:
                            front(nxt, i)
                        sum_state(i - 1)
                sum_state(UNITS - 1)

            def back(g, i):
                for p, (a, b) in enumerate(PAIRS):
                    if i == BEAT["op"][p]:
                        pe.wait_ge(*emptied(g, ("op", p)))
                        pe.wait_ge(*yg_step.at(g, (IC - 1, 1)))
                        for j in range(a, b):
                            for c in range(IC):
                                mm = pe.matmul(ps(("op", p))[0:TT, 0, (j - a) * D:(j - a + 1) * D], dt[:, c, j * TT:(j + 1) * TT], wop[:, c, :], start=c == 0, stop=c == IC - 1)
                        mm.then_inc(full_of(("op", p)), 1)
                if i == BEAT["qt"]:
                    for p, (a, b) in enumerate(PAIRS):
                        pe.wait_ge(*emptied(g, ("qt", p)))
                        pe.wait_ge(*qx_ready.at(g, 0))
                        pb = ps(("qt", p))[0:DH, 0, :].bitcast(BF16)
                        for e in range(2):
                            for j in range(a, b):
                                o = e * 2 * TT + (j - a) * TT
                                mm = pe.transpose(pb[:, o:o + TT], qx[:, j, e * DH:(e + 1) * DH], identb[0:TT, 0:TT])
                        mm.then_inc(full_of(("qt", p)), 1)
                for j in range(J):
                    if i == BEAT["fi"][j]:
                        pe.wait_ge(*emptied(g, ("fi", j)))
                        pe.wait_ge(*qT_ready.at(g, j // 2))
                        for half in range(2):
                            for e in range(2):
                                mm = pe.matmul(ps(("fi", j))[0:TT, half, :], qT[:, e, j * TT:(j + 1) * TT], qwi[:, e, half * FH:(half + 1) * FH],
                                               start=e == 0, stop=e == 1)
                        mm.then_inc(full_of(("fi", j)), 1)

                def q2_transposes(p):
                    a, b = PAIRS[p]
                    pe.wait_ge(*emptied(g, ("q2t", p)))
                    pe.wait_ge(*q2_ready.at(g, p))
                    pb = ps(("q2t", p))[:, 0, :].bitcast(BF16)
                    for j in range(a, b):
                        for f in range(FC):
                            o = ((j - a) * FC + f) * TT
                            mm = pe.transpose(pb[:, o:o + TT], q2[:, j, f * 128:(f + 1) * 128], identb[0:TT, 0:TT])
                    mm.then_inc(full_of(("q2t", p)), 1)

                def last_products(p):
                    a, b = PAIRS[p]
                    pe.wait_ge(*emptied(g, ("out", p)))
                    pe.wait_ge(*q2T_ready.at(g, p))
                    for j in range(a, b):
                        for f in range(FC):
                            o = ((j - a) * FC + f) * TT
                            mm = pe.matmul(ps(("out", p))[0:TT, 0, (j - a) * D:(j - a + 1) * D], q2T[:, p % 2, o:o + TT], qwo[:, f, :],
                                           start=f == 0, stop=f == FC - 1)
                    mm.then_inc(full_of(("out", p)), 1)

                if i == BEAT["q2t"]:
                    q2_transposes(0)
                    for p in range(4):
                        if p < 3:
                            q2_transposes(p + 1)
                        last_products(p)

            def turn(g, nxt):
                units(g, nxt)
                for i in range(BEATS):
                    if nxt is not None:
                        mixer(nxt, i)
                    back(g, i)

            for i in range(UNITS):
                front(0, i)
            for i in range(BEATS):
                mixer(0, i)
            with pe.Fori(0, NG - 1) as g:
                turn(g, g + 1)
            turn(NG - 1, None)

        @block.scalar
        def _(act):
            act.wait_ge(*setup.at(0, "x0 turn"))
            act.activation(x0T.rearrange("p e t -> p (e t)"), bank[0:DH, 2, 0:2 * T], ACT.Copy).then_inc(setup.sem, 1)
            act.wait_ge(*setup.at(0, "gate"))
            act.activation(gate0, bank[0:DH, :, 0:T], ACT.Sigmoid).then_inc(setup.sem, 1)
            for half in range(2):
                act.wait_ge(*setup.at(0, ("turn0 b", "turn1 b")[half]))
                act.activation(arow.rearrange("p j r d -> p (j r) d")[:, half * 7:half * 7 + 7], bank[0:RB, 0:7, 0:D],
                               ACT.Copy, scale=DECAY ** TC).then_inc(setup.sem, 1)
            act.wait_ge(*setup.at(0, "consts"))
            act.activation(amat[:], amat[:], ACT.Exp).then_inc(setup.sem, 1)
            act.wait_ge(s_qw, 32)
            act.wait_ge(*setup.at(0, "A exp"))
            act.activation(amat[:], amat[:], ACT.Copy, scale=-1.0).then_inc(setup.sem, 1)
            qi, qo = qraw.rearrange("p e f -> p (e f)"), qraw2.rearrange("p f d -> p (f d)")
            act.wait_ge(*setup.at(0, "A neg"))
            act.activation(qtmp[0:DH, :], qi, ACT.Abs, accum_out=wsc[0:DH, 0:1]).then_inc(setup.sem, 1)
            act.wait_ge(*setup.at(0, "sums in"))
            act.activation(qtmp[:, 0:FC * D], qo, ACT.Abs, accum_out=wsc[:, 1:2]).then_inc(setup.sem, 1)
            act.wait_ge(*setup.at(0, "end"))

            def turned(g, name, p):
                a, b = PAIRS[p]
                w = (b - a) * TT
                act.wait_ge(*filled(g, (name, p)))
                act.activation(xT[0:DH, :, a * TT:b * TT], ps((name, p))[0:DH, 0:2 * w].rearrange("p (e w) -> p e w", e=2),
                               ACT.Copy).then_inc(xT_ready.sem, 1)

            def decay_factor(g, c, n):
                for q in range(2):
                    act.wait_ge(*st_ready[q].at(g, c, n - 1))
                    act.activation(bank[:, q, 0:HB].rearrange("p (b t) -> p b t", t=T)[:, :, 1:T],
                                   dt[:, c, q * HB:(q + 1) * HB].rearrange("p (b t) -> p b t", t=T)[:, :, 1:T],
                                   ACT.Exp, scale=amat[:, c, n:n + 1]).then_inc(dA_full[q].sem, 1)

            def front(g, i):
                for p, (a, b) in enumerate(PAIRS):
                    if i == AT["turn3"][p]:
                        act.wait_ge(*filled(g, ("tr3", p)))
                        for j in range(a, b):
                            src = ps(("tr3", p))[0:DH, 0:2 * (b - a) * TT].rearrange("p (e j b t) -> p e j b t", e=2, j=b - a, b=GB)
                            act.activation(xbt[:, :, :, j * TC:(j + 1) * TC], src[:, :, j - a], ACT.Copy).then_inc(xT_ready.sem, 1)
                for p, (a, b) in enumerate(PAIRS):
                    if i == AT["embed"][p]:
                        act.wait_ge(*filled(g, ("tok", p)))
                        if p == 0:
                            act.wait_ge(*h2_saved.at(g - 1, "s", 15))
                        act.activation(h[:, a:b, :], ps(("tok", p))[0:TT, 0:(b - a) * D].rearrange("p (j d) -> p j d", d=D),
                                       ACT.Copy).then_inc(h_ready.sem, 1)
                    if i == AT["turn1"][p]:
                        turned(g, "tr1", p)
                    if i == AT["turn2"][p]:
                        turned(g, "tr2", p)
                for k in range(12):
                    if i == AT["gelu"][k]:
                        w = (PAIRS[k // 3][1] - PAIRS[k // 3][0]) * TT
                        act.wait_ge(*filled(g, ("hid", k)))
                        if k >= 3 and k % 3 == 0:
                            act.wait_ge(*filled(g, ("fo", k // 3 - 1)))
                        act.activation(gT[:, 2 * (k % 3):2 * (k % 3) + 2, 0:w], ps(("hid", k))[:, 0:2 * w].rearrange("p (m w) -> p m w", m=2),
                                       ACT.Gelu).then_inc(gT_ready.sem, 1)

            def mixer(g, i):
                for c in range(IC):
                    if i == BEAT["hid"][c]:
                        act.wait_ge(*filled(g, ("inp", c)))
                        if c < 2:
                            act.wait_ge(*conv_step.at(g, "pad"))
                        else:
                            act.wait_ge(*conv_step.at(g, (c - 2, 3)))
                        act.activation(hidp[:, c % 2, :, K - 1:].rearrange("p (q b) t -> p q b t", q=2),
                                       ps(("inp", c))[:, :, 0:HB].rearrange("p q (b t) -> p q b t", t=T), ACT.Copy).then_inc(hid_ready.sem, 1)
                    if i == BEAT["gate"][c]:
                        act.wait_ge(*filled(g, ("inp", IC + c)))
                        if c == 0:
                            act.wait_ge(*yg_step.at(g - 1, (IC - 1, 0)))
                        act.activation(sg[:, c, :].rearrange("p (q t) -> p q t", q=2), ps(("inp", IC + c))[:, :, 0:HB],
                                       ACT.Silu).then_inc(sg_ready.sem, 1)
                    if i == BEAT["act"][c]:
                        act.wait_ge(*conv_step.at(g, (c, 3)))
                        act.activation(hh[:, c, :], hh[:, c, :], ACT.Silu).then_inc(hh_ready.sem, 1)
                if i == BEAT["ts"]:
                    act.wait_ge(*filled(g, ("xp", 0)))
                    act.activation(tsT.rearrange("p (q t) -> p q t", q=2), ps(("xp", 0))[0:R, :, 0:HB], ACT.Copy).then_inc(ts_ready.sem, 1)
                for c in range(IC):
                    if i == BEAT["x"][c]:
                        act.wait_ge(*filled(g, ("dtp", c)))
                        src = ps(("dtp", c))[:, :, 0:HB]
                        act.activation(dt[:, c, :].rearrange("p (q t) -> p q t", q=2), src, ACT.Identity,
                                       bias=cvec[:, 1, c:c + 1]).then_inc(sp_step.sem, 1)
                        act.activation(u[:, c, :].rearrange("p (q t) -> p q t", q=2), src, ACT.Abs,
                                       bias=cvec[:, 1, c:c + 1]).then_inc(sp_step.sem, 1)
                if i == BEAT["softplus"]:
                    act.wait_ge(*sp_step.at(g, (IC - 1, 1)))
                    act.activation(u, u, ACT.Exp, scale=-1.0).then_inc(sp_step.sem, 1)
                    act.wait_ge(*sp_step.at(g, "exp"))
                    act.activation(u, u, ACT.Ln, bias=1.0).then_inc(sp_step.sem, 1)

            def units(g, nxt):
                act.wait_ge(*dA_zero.at(g, 0))
                act.wait_ge(*dt_ready.at(g, IC - 1))
                act.wait_ge(*u_step.at(g, (IC - 1, 1)))
                decay_factor(g, 0, 0)
                for i in range(UNITS):
                    c, n = divmod(i, N)
                    if c == 0:
                        act.wait_ge(*bc_full.at(g, 0, 2 * n + 1))
                        if n == C_OVER_OUT:
                            act.wait_ge(*stored.at(g - 1, "s", 15))
                        act.activation(cb[:, n, :].rearrange("p (q t) -> p q t", q=2), bank[:, 2:4, 0:HB], ACT.Copy).then_inc(cb_ready.sem, 1)
                    if i + 1 < UNITS:
                        decay_factor(g, (i + 1) // N, (i + 1) % N)
                    if nxt is not None:
                        front(nxt, i)

            def back(g, i):
                if i == BEAT["turn"]:
                    for p, (a, b) in enumerate(PAIRS):
                        act.wait_ge(*filled(g, ("qt", p)))
                        pb = ps(("qt", p))[0:DH, 0, :].bitcast(BF16)[:, 0:4 * TT].rearrange("p (e w) -> p e w", e=2)
                        act.activation(qT[:, :, a * TT:b * TT], pb[:, :, 0:(b - a) * TT], ACT.Copy).then_inc(qT_ready.sem, 1)
                for j in range(J):
                    if i == BEAT["fi"][j]:
                        act.wait_ge(*filled(g, ("fi", j)))
                        act.wait_ge(*scale_ready.at(g, 1))
                        if j >= 2:
                            act.wait_ge(*ss_ready.at(g, j - 2))
                        act.activation(sgl[:, j % 2, :], ps(("fi", j))[0:TT, 1, :], ACT.Silu, scale=one(SC, j, small_b)).then_inc(sgl_ready.sem, 1)
                for j in range(J):
                    if i == BEAT["square"][j]:
                        squares(g, j)
                if i == BEAT["q2t"]:
                    for p, (a, b) in enumerate(PAIRS):
                        act.wait_ge(*filled(g, ("q2t", p)))
                        if p >= 2:
                            act.wait_ge(*filled(g, ("out", p - 2)))
                        w = (b - a) * FC * TT
                        act.activation(q2T[:, p % 2, 0:w], ps(("q2t", p))[:, 0, :].bitcast(BF16)[:, 0:w], ACT.Copy).then_inc(q2T_ready.sem, 1)

            def squares(g, j):
                act.wait_ge(*y2_ready.at(g, j))
                act.activation(sgl[:, j % 2, :], y2[:, j, :], ACT.Square, accum_out=one(SS, j, small_b)).then_inc(ss_ready.sem, 1)

            def turn(g, nxt):
                units(g, nxt)
                for i in range(BEATS):
                    if nxt is not None:
                        mixer(nxt, i)
                    back(g, i)

            for i in range(UNITS):
                front(0, i)
            for i in range(BEATS):
                mixer(0, i)
            with act.Fori(0, NG - 1) as g:
                turn(g, g + 1)
            turn(NG - 1, None)

        @block.vector
        def _(dve):
            dve.wait_ge(*setup.at(0, "x0 tok"))
            for t in range(2):
                ins = dve.bn_stats(x0s[:, t, :], bank[0:98, t, 0:D])
            ins.then_inc(setup.sem, 1)
            dve.wait_ge(*setup.at(0, "x0 stats"))
            for t in range(2):
                ins = dve.bn_aggr(x0m[:, t, :], x0s[:, t, :])
            ins.then_inc(setup.sem, 1)
            dve.wait_ge(*setup.at(0, "x0 pow"))
            for t in range(2):
                ins = dve.tensor_scalar(x0ln[:, t, :], bank[0:98, t, 0:D], x0m[:, t, 0:1], x0m[:, t, 1:2], ALU.subtract, ALU.mult)
            ins.then_inc(setup.sem, 1)
            dve.wait_ge(*setup.at(0, "gk a"))
            dve.tensor_copy(gk.rearrange("p h e d -> p h (e d)"), bank[0:DH, :, 0:2 * D]).then_inc(setup.sem, 1)
            dve.wait_ge(*setup.at(0, "a"))
            for hd in range(NH):
                for d in range(2):
                    ins = dve.tensor_copy(amask[:, d].rearrange("p j r (h s) -> p h (j r) s", h=NH)[:, hd],
                                          bank[0:DH, hd, d * T:(d + 1) * T].rearrange("p (a s) -> p a s", s=TS))
            ins.then_inc(setup.sem, 1)
            dve.wait_ge(*setup.at(0, "a in"))
            dve.tensor_copy(wgr, wg.unsqueeze(3).to_broadcast([DH, 2, NH, DH])).then_inc(setup.sem, 1)
            dve.wait_ge(*setup.at(0, "gate in"))
            for hd in range(NH):
                ins = dve.tensor_tensor(gate0[:, hd, :], gate0[:, hd, :], dec, ALU.mult)
            ins.then_inc(setup.sem, 1)
            dve.wait_ge(*setup.at(0, "gk b"))
            dve.tensor_copy(gk.rearrange("p h e d -> p h (e d)"), bank[0:DH, :, 0:2 * D]).then_inc(setup.sem, 1)
            dve.wait_ge(*setup.at(0, "b"))
            for hd in range(NH):
                for d in range(2):
                    ins = dve.tensor_tensor(bT[:, d].rearrange("p j r (h s) -> p h (j r) s", h=NH)[:, hd],
                                            bank[0:DH, hd, d * T:(d + 1) * T].rearrange("p (a s) -> p a s", s=TS),
                                            gate0[:, hd, :].rearrange("p (a s) -> p a s", s=TS), ALU.mult)
            ins.then_inc(setup.sem, 1)
            for half in range(2):
                dve.wait_ge(*setup.at(0, ("turn0", "turn1")[half]))
                dve.tensor_copy(bmat[:].rearrange("p j r d -> p (j r) d")[:, half * 7:half * 7 + 7], bank[0:RB, 0:7, D:2 * D]).then_inc(setup.sem, 1)
            dve.wait_ge(*setup.at(0, "m"))
            dve.memset(mmat[:, 0], 0.0).then_inc(setup.sem, 1)
            for j in range(1, J):
                dve.wait_ge(*setup.at(0, ("m", j - 1)))
                dve.scalar_tensor_tensor(mmat[:, j].rearrange("p e d -> p (e d)"), mmat[:, j - 1].rearrange("p e d -> p (e d)"),
                                              DECAY ** TC, bank[0:DH, j - 1, 0:2 * D], ALU.mult, ALU.add).then_inc(setup.sem, 1)
            dve.wait_ge(*setup.at(0, ("m", J - 1)))
            dve.memset(ones, 1.0)
            dve.memset(nhalf[:], -0.5)
            dve.memset(consts[:], MAGIC)
            dve.memset(xT[DH:DH + 1, 1, :], 1.0).then_inc(setup.sem, 1)
            dve.wait_ge(*setup.at(0, "sums"))
            dve.tensor_scalar(wsc[:, 2:3], bank[:, 0, 0:1], 1.0 / (2 * FH * D), None, ALU.mult)
            dve.tensor_scalar(wsc[:, 3:4], bank[:, 0, 1:2], 1.0 / (FH * D), None, ALU.mult).then_inc(setup.sem, 1)
            dve.wait_ge(*setup.at(0, "means"))
            dve.tensor_scalar(wsc[:, 4:6], wsc[:, 2:4], Q_EPS, None, ALU.max).then_inc(setup.sem, 1)
            dve.wait_ge(*setup.at(0, "floor"))
            dve.reciprocal(wsc[:, 6:8], wsc[:, 4:6]).then_inc(setup.sem, 1)
            prev = "inverse"
            for i, (parts, raw, whole) in enumerate(((DH, qraw.rearrange("p e f -> p (e f)"), qwi[:].rearrange("p e f -> p (e f)")),
                                                     (128, qraw2.rearrange("p f d -> p (f d)"), qwo[:].rearrange("p f d -> p (f d)")))):
                tmp = qtmp[0:parts, 0:raw.shape[1]]
                dve.wait_ge(*setup.at(0, prev))
                dve.tensor_scalar(tmp, raw, wsc[0:parts, 6 + i:7 + i], MAGIC, ALU.mult, ALU.add).then_inc(setup.sem, 1)
                dve.wait_ge(*setup.at(0, f"q{3 * i + 1}"))
                dve.tensor_scalar(tmp, tmp, MAGIC, 1.0, ALU.subtract, ALU.min).then_inc(setup.sem, 1)
                dve.wait_ge(*setup.at(0, f"q{3 * i + 2}"))
                dve.tensor_scalar(whole, tmp, -1.0, None, ALU.max).then_inc(setup.sem, 1)
                prev = f"q{3 * i + 3}"
            dve.wait_ge(*setup.at(0, prev))
            dve.memset(xT[DH:DH + 1, 1, :], 1.0).then_inc(setup.sem, 1)
            dve.wait_ge(*setup.at(0, "end"))

            def half(ap):
                return ap.rearrange("p (q t) -> p q t", q=2)

            def front(g, i):
                for p, (a, b) in enumerate(PAIRS):
                    w = (b - a) * NR * TT
                    if i == AT["sum"][p]:
                        dve.wait_ge(*filled(g, ("ao", p)))
                        xp = xln[:, a:b, :].rearrange("p j d -> p (j d)")
                        dve.scalar_tensor_tensor(xp, ps(("ao", p))[0:TT, 0:(b - a) * D], decp[:, 0:1], xp,
                                                 ALU.mult, ALU.add).then_inc(t_ready.sem, 1)
                for p, (a, b) in enumerate(PAIRS):
                    w = (b - a) * NR * TT
                    if i == AT["mask"][p]:
                        dve.wait_ge(*filled(g, ("sc", p)))
                        if p >= 2:
                            dve.wait_ge(*filled(g, ("ao", p - 2)))
                        dve.tensor_tensor(scT[:, p % 2, 0:b - a].rearrange("p j r t -> p j (r t)"),
                                          ps(("sc", p))[0:RB, 0:w].rearrange("p (j m) -> p j m", j=b - a),
                                          mask[:].unsqueeze(1).to_broadcast([RB, b - a, NR * TT]), ALU.mult).then_inc(scT_ready.sem, 1)
                    if i == AT["h2"][p]:
                        dve.wait_ge(*filled(g, ("fo", p)))
                        hp = h[:, a:b, :].rearrange("p j d -> p (j d)")
                        dve.tensor_tensor(hp, ps(("fo", p))[0:TT, 0:(b - a) * D], hp, ALU.add).then_inc(h2_ready.sem, 1)
                    for k, ready in ((1, h_ready), (2, h1_ready), (3, h2_ready)):
                        if i == AT[f"stats{k}"][p]:
                            dve.wait_ge(*ready.at(g, p))
                            for j in range(a, b):
                                ins = dve.bn_stats(stats[:, j, :], h[:, j, :])
                            if p == 3:
                                ins.then_inc(stats_ready.sem, 1)
                for k in (1, 2, 3):
                    if i == AT[f"norm{k}"][0]:
                        dve.wait_ge(*coef_ready.at(g, f"ln{k}"))
                        for p, (a, b) in enumerate(PAIRS):
                            for j in range(a, b):
                                ins = dve.tensor_scalar(xln[:, j, :], h[:, j, :], one(MEAN, j), one(RSTD, j), ALU.subtract, ALU.mult)
                            ins.then_inc(xln_ready.sem, 1)

            def mixer(g, i):
                if i == BEAT["conv"][0]:
                    dve.wait_ge(*cs_ready.at(g - 1, IC - 1, N - 1))
                    dve.memset(hidp[:, :, :, 0:K - 1], 0.0).then_inc(conv_step.sem, 1)
                    dve.wait_ge(*conv_step.at(g, "pad"))
                for c in range(IC):
                    if i == BEAT["conv"][c]:
                        dve.wait_ge(*hid_ready.at(g, c))
                        acc = hh[:, c, :].rearrange("p (b t) -> p b t", t=T)
                        dve.tensor_scalar(acc, hidp[:, c % 2, :, K - 1:], cw[:, c, K - 1:K], cvec[:, 0, c:c + 1],
                                          ALU.mult, ALU.add).then_inc(conv_step.sem, 1)
                        for m in range(K - 1):
                            dve.wait_ge(*conv_step.at(g, (c, m)))
                            dve.scalar_tensor_tensor(acc, hidp[:, c % 2, :, m:m + T], cw[:, c, m:m + 1], acc,
                                                     ALU.mult, ALU.add).then_inc(conv_step.sem, 1)
                if i == BEAT["split"]:
                    dve.wait_ge(*filled(g, ("bc", 0)))
                    src = ps(("bc", 0))[0:96, :, 0:HB]
                    dve.tensor_copy(half(stk[:, :]), src).then_inc(bc_step.sem, 1)
                    dve.wait_ge(*bc_step.at(g, 0))
                    dve.tensor_tensor(half(bcr), src, half(stk[:, :]), ALU.subtract).then_inc(bc_step.sem, 1)
                    dve.wait_ge(*bc_step.at(g, 1))
                    dve.tensor_copy(midb, bcr).then_inc(bc_step.sem, 1)
                    dve.wait_ge(*bc_step.at(g, 2))
                    dve.tensor_copy(stk[32:64, :], midb[32:64, :]).then_inc(bc_step.sem, 1)
                    dve.tensor_tensor(stk[64:96, :], bcr[64:96, :], midb[64:96, :], ALU.subtract).then_inc(bc_step.sem, 1)
                if i == BEAT["dt"]:
                    dve.wait_ge(*sp_step.at(g, "ln"))
                    for c in range(IC):
                        dve.scalar_tensor_tensor(dt[:, c, :], dt[:, c, :], 0.0, u[:, c, :], ALU.max, ALU.add).then_inc(dt_ready.sem, 1)

            def units(g, nxt):
                dve.wait_ge(*emptied(g, "dA"))
                dve.memset(bank[:, 0:2, 0:HB].rearrange("p q (b t) -> p q b t", t=T)[:, :, :, 0:1], 0.0).then_inc(dA_zero.sem, 1)


                def unit(i):
                    c, n = divmod(i, N)
                    dve.wait_ge(*bc_full.at(g, c, n if c else 2 * n))
                    dve.wait_ge(*st_ready[1].at(g, c, n - 1))
                    dve.tensor_tensor(half(dbu[:, :]), half(u[:, c, :]), bank[:, 2:4, 0:HB], ALU.mult).then_inc(dbu_ready.sem, 1)
                    dve.wait_ge(*dbu_ready.at(g, c, n))
                    dve.wait_ge(*cs_used.at(g, c, n - 3))
                    for q in range(2):
                        dve.wait_ge(*dA_full[q].at(g, c, n))
                        cols = slice(q * HB, (q + 1) * HB)
                        dve.tensor_tensor_scan(st[:, i % 3, cols], bank[:, q, 0:HB], dbu[:, cols], 0.0,
                                               ALU.mult, ALU.add).then_inc(st_ready[q].sem, 1)

                def y_sum(c):
                    dve.wait_ge(*cs_used.at(g, c, N - 1))
                    dve.scalar_tensor_tensor(half(u[:, c, :]), half(hh[:, c, :]), cvec[:, 2, c:c + 1], bank[:, 4:6, 0:HB],
                                             ALU.mult, ALU.add).then_inc(ysum_ready.sem, 1)

                for i in range(UNITS):
                    c, n = divmod(i, N)
                    if n == 0:
                        dve.wait_ge(*u_step.at(g, (c, 1)))
                    unit(i)
                    if c and n == 1:
                        y_sum(c - 1)
                    if nxt is not None:
                        front(nxt, i)
                y_sum(IC - 1)
                gated(g, IC - 1)

            def gated(g, c):
                dve.wait_ge(*ysum_ready.at(g, c))
                dve.wait_ge(*sg_ready.at(g, c))
                dve.tensor_tensor(dt[:, c, :].rearrange("p (j b t) -> p b j t", j=J, b=GB),
                                  u[:, c, :].rearrange("p (b j t) -> p b j t", j=J, b=GB),
                                  sg[:, c, :].rearrange("p (b j t) -> p b j t", j=J, b=GB), ALU.mult).then_inc(yg_step.sem, 1)
                dve.wait_ge(*yg_step.at(g, (c, 0)))
                last = dt[:, c, :].rearrange("p (j b t) -> p j b t", j=J, b=GB)[:, J - 1, :, TC - 1]
                dve.tensor_scalar(last, last, cvec[:, 4, c:c + 1], None, ALU.mult).then_inc(yg_step.sem, 1)

            def back(g, i):
                for p, (a, b) in enumerate(PAIRS):
                    if i == BEAT["h3"][p]:
                        dve.wait_ge(*filled(g, ("op", p)))
                        if p == 0:
                            dve.wait_ge(*hb_loaded.at(g, "s", 15))
                        hp = hb[:, a:b, :].rearrange("p j d -> p (j d)")
                        dve.tensor_tensor(hp, ps(("op", p))[0:TT, 0, 0:(b - a) * D], hp, ALU.add).then_inc(h3_ready.sem, 1)
                        dve.wait_ge(*h3_ready.at(g, p))
                        for j in range(a, b):
                            ins = dve.bn_stats(stats_b[:, j, :], hb[:, j, :])
                        if p == 3:
                            ins.then_inc(stats4_ready.sem, 1)
                if i == BEAT["norm4"]:
                    dve.wait_ge(*coef4_ready.at(g, "ln4"))
                    for j in range(J):
                        ins = dve.tensor_scalar(xb[:, j, :], hb[:, j, :], one(MEAN, j, small_b), one(RSTD, j, small_b), ALU.subtract, ALU.mult)
                    ins.then_inc(xb_ready.sem, 1)
                    dve.wait_ge(*xb_ready.at(g, 0))
                    for j in range(J):
                        ins = dve.tensor_tensor(xb[:, j, :], xb[:, j, :], gin[:], ALU.mult)
                    ins.then_inc(xg_ready.sem, 1)
                if i == BEAT["peak"]:
                    dve.wait_ge(*xg_ready.at(g, 0))
                    dve.tensor_reduce(col(PEAK, small_b), xb, AX_X, ALU.max, apply_absolute_value=True).then_inc(peak_ready.sem, 1)
                if i == BEAT["scale"]:
                    dve.wait_ge(*floor_ready.at(g, 1))
                    dve.reciprocal(col(T1, small_b), col(PEAK, small_b)).then_inc(rcp_ready.sem, 1)
                if i == BEAT["round"]:
                    dve.wait_ge(*scale_ready.at(g, 1))
                    for j in range(J):
                        ins = dve.tensor_scalar(xb[:, j, :], xb[:, j, :], one(QS, j, small_b), MAGIC, ALU.mult, ALU.add)
                    ins.then_inc(qr_ready.sem, 1)
                    dve.wait_ge(*qr_ready.at(g, 0))
                    dve.tensor_scalar(qx, xb, MAGIC, 127.0, ALU.subtract, ALU.min).then_inc(qx_ready.sem, 1)
                for j in range(J):
                    if i == BEAT["y2"][j]:
                        dve.wait_ge(*sgl_ready.at(g, j))
                        dve.scalar_tensor_tensor(y2[:, j, :], ps(("fi", j))[0:TT, 0, :], one(SC, j, small_b), sgl[:, j % 2, :],
                                                 ALU.mult, ALU.mult).then_inc(y2_ready.sem, 1)
                for j in range(J):
                    if i == BEAT["peak2"][j]:
                        dve.wait_ge(*r2_ready.at(g, j))
                        dve.tensor_reduce(one(PEAK2, j, small_b), y2[:, j, :], AX_X, ALU.max, apply_absolute_value=True).then_inc(peak_ready.sem, 1)
                if i == BEAT["scale2"]:
                    dve.wait_ge(*floor_ready.at(g, 2))
                    dve.reciprocal(col(T1, small_b), col(PEAK2, small_b)).then_inc(rcp_ready.sem, 1)
                if i == BEAT["round2"]:
                    dve.wait_ge(*scale_ready.at(g, 2))
                    for p, (a, b) in enumerate(PAIRS):
                        for j in range(a, b):
                            ins = dve.tensor_scalar(y2[:, j, :], y2[:, j, :], one(QS2, j, small_b), MAGIC, ALU.mult, ALU.add)
                        ins.then_inc(q2r_ready.sem, 1)
                        dve.wait_ge(*q2r_ready.at(g, p))
                        dve.tensor_scalar(q2[:, a:b, :], y2[:, a:b, :], MAGIC, 127.0, ALU.subtract, ALU.min).then_inc(q2_ready.sem, 1)
                if i == BEAT["q2t"]:
                    for p, (a, b) in enumerate(PAIRS):
                        dve.wait_ge(*filled(g, ("out", p)))
                        for j in range(a, b):
                            dve.scalar_tensor_tensor(ob[:, j, :], ps(("out", p))[0:TT, 0, (j - a) * D:(j - a + 1) * D], one(SC2, j, small_b),
                                                     hb[:, j, :], ALU.mult, ALU.add).then_inc(o_ready.sem, 1)

            def turn(g, nxt):
                units(g, nxt)
                for i in range(BEATS):
                    if nxt is not None:
                        mixer(nxt, i)
                    back(g, i)

            for i in range(UNITS):
                front(0, i)
            for i in range(BEATS):
                mixer(0, i)
            with dve.Fori(0, NG - 1) as g:
                turn(g, g + 1)
            turn(NG - 1, None)

        @block.gpsimd
        def _(pool):
            for sig in credited:
                pool.sem_inc(sig.sem, sig.credit)
            pool.wait_ge(*setup.at(0, "x0 mean"))
            pool.tensor_scalar(x0m[:, :, 1], x0m[:, :, 1], LN_EPS, None, ALU.add)
            pool.memset(nhalf[:], -0.5).then_inc(setup.sem, 1)
            pool.wait_ge(*setup.at(0, "x0 var"))
            pool.tensor_tensor(x0m[:, :, 1], x0m[:, :, 1], nhalf[0:98, 0:2], ALU.pow).then_inc(setup.sem, 1)
            pool.wait_ge(*setup.at(0, "end"))
            links = [0, 0]

            def front_step(g, ins):
                links[0] += 1
                ins.then_inc(front_link, 1)
                pool.wait_ge(front_link, g * FRONT_LINKS + links[0])
                pool.nop(nofuse=True)

            def back_step(g, ins):
                links[1] += 1
                ins.then_inc(back_link, 1)
                pool.wait_ge(back_link, g * BACK_LINKS + links[1])
                pool.nop(nofuse=True)

            def coef(g, stats, small, step):
                mean_e, m2_e, mean_o, m2_o = (stats[:, :, i] for i in (1, 2, 4, 5))
                mean2, diff, mean, var, t1, t2, rstd = (col(i, small) for i in (MEAN2, DIFF, MEAN, VAR, T1, T2, RSTD))
                pool.tensor_tensor(mean2, mean_e, mean_o, ALU.add)
                pool.tensor_tensor(t1, m2_e, m2_o, ALU.add)
                step(g, pool.tensor_tensor(diff, mean_e, mean_o, ALU.subtract))
                pool.tensor_scalar(mean, mean2, 0.5, None, ALU.mult)
                pool.tensor_scalar(t1, t1, 1.0 / D, None, ALU.mult)
                step(g, pool.tensor_tensor(diff, diff, diff, ALU.mult))
                step(g, pool.tensor_scalar(diff, diff, 0.25, None, ALU.mult))
                step(g, pool.tensor_tensor(var, diff, t1, ALU.add))
                step(g, pool.tensor_scalar(t2, var, LN_EPS, None, ALU.add))
                return pool.tensor_tensor(rstd, t2, nhalf[:], ALU.pow)

            def front(g, i):
                for k in (1, 2, 3):
                    if i == AT[f"coef{k}"][0]:
                        pool.wait_ge(*stats_ready.at(g, f"ln{k}"))
                        pool.nop(nofuse=True)
                        coef(g, stats, small, front_step).then_inc(coef_ready.sem, 1)
                for p, (a, b) in enumerate(PAIRS):
                    if i == AT["h1"][p]:
                        pool.wait_ge(*t_ready.at(g, p))
                        pool.nop(nofuse=True)
                        pool.tensor_tensor(h[:, a:b, :], h[:, a:b, :], xln[:, a:b, :], ALU.add).then_inc(h1_ready.sem, 1)

            def mixer(g, i):
                if i == BEAT["u"]:
                    for c in range(IC):
                        pool.wait_ge(*dt_ready.at(g, c))
                        pool.nop(nofuse=True)
                        last = dt[:, c, :].rearrange("p (b t) -> p b t", t=T)[:, :, T - 1]
                        pool.tensor_scalar(last, last, cvec[:, 3, c:c + 1], None, ALU.mult).then_inc(u_step.sem, 1)
                        pool.wait_ge(*u_step.at(g, (c, 0)))
                        pool.wait_ge(*hh_ready.at(g, c))
                        pool.nop(nofuse=True)
                        pool.tensor_tensor(u[:, c, :], dt[:, c, :], hh[:, c, :], ALU.mult).then_inc(u_step.sem, 1)

            def units(g, nxt):
                for i in range(UNITS):
                    c, n = divmod(i, N)
                    pool.wait_ge(*st_ready[1].at(g, c, n))
                    if c == 0:
                        pool.wait_ge(*cb_ready.at(g, "c", n))
                    pool.nop(nofuse=True)
                    pool.tensor_tensor(st[:, i % 3, :], st[:, i % 3, :], cb[:, n, :], ALU.mult).then_inc(cs_ready.sem, 1)
                    if c and n == 2:
                        gated(g, c - 1)
                    if nxt is not None:
                        front(nxt, i)

            def gated(g, c):
                pool.wait_ge(*ysum_ready.at(g, c))
                pool.wait_ge(*sg_ready.at(g, c))
                pool.nop(nofuse=True)
                pool.tensor_tensor(dt[:, c, :].rearrange("p (j b t) -> p b j t", j=J, b=GB),
                                   u[:, c, :].rearrange("p (b j t) -> p b j t", j=J, b=GB),
                                   sg[:, c, :].rearrange("p (b j t) -> p b j t", j=J, b=GB), ALU.mult).then_inc(yg_step.sem, 1)
                pool.wait_ge(*yg_step.at(g, (c, 0)))
                pool.nop(nofuse=True)
                last = dt[:, c, :].rearrange("p (j b t) -> p j b t", j=J, b=GB)[:, J - 1, :, TC - 1]
                pool.tensor_scalar(last, last, cvec[:, 4, c:c + 1], None, ALU.mult).then_inc(yg_step.sem, 1)

            def back(g, i):
                if i == BEAT["coef4"]:
                    pool.wait_ge(*stats4_ready.at(g, "ln4"))
                    pool.nop(nofuse=True)
                    coef(g, stats_b, small_b, back_step).then_inc(coef4_ready.sem, 1)
                    pool.wait_ge(*coef4_ready.at(g, "ln4"))
                    pool.nop(nofuse=True)
                    back_step(g, pool.tensor_tensor(col(T2, small_b), col(RSTD, small_b), col(RSTD, small_b), ALU.mult))
                    back_step(g, pool.tensor_tensor(col(T2, small_b), col(T2, small_b), col(VAR, small_b), ALU.mult))
                    back_step(g, pool.tensor_scalar(col(T2, small_b), col(T2, small_b), RMS_EPS, None, ALU.add))
                    back_step(g, pool.tensor_tensor(col(RINV, small_b), col(T2, small_b), nhalf[:], ALU.pow))
                def quant_scale(i, peak, rinv, scale, qscale):
                    back_step(g, pool.tensor_tensor(col(peak, small_b), col(peak, small_b), col(rinv, small_b), ALU.mult))
                    back_step(g, pool.tensor_scalar(col(peak, small_b), col(peak, small_b), Q_EPS, None, ALU.max))
                    pool.tensor_scalar(col(scale, small_b), col(peak, small_b), 1.0 / 127.0, wsc[0:TT, 3 + i:4 + i], ALU.mult, ALU.mult).then_inc(floor_ready.sem, 1)
                    pool.wait_ge(*rcp_ready.at(g, i))
                    pool.nop(nofuse=True)
                    back_step(g, pool.tensor_tensor(col(T2, small_b), col(T1, small_b), col(rinv, small_b), ALU.mult))
                    pool.tensor_scalar(col(qscale, small_b), col(T2, small_b), 127.0, None, ALU.mult).then_inc(scale_ready.sem, 1)

                if i == BEAT["scale"]:
                    pool.wait_ge(*peak_ready.at(g, 0))
                    pool.nop(nofuse=True)
                    quant_scale(1, PEAK, RINV, SC, QS)
                for j in range(J):
                    if i == BEAT["gain2"][j]:
                        pool.wait_ge(*ss_ready.at(g, j))
                        pool.nop(nofuse=True)
                        pool.tensor_tensor(y2[:, j, :], y2[:, j, :], gout[:], ALU.mult).then_inc(r2_ready.sem, 1)
                if i == BEAT["scale2"]:
                    pool.wait_ge(*rcp_ready.at(g, 1))
                    pool.nop(nofuse=True)
                    back_step(g, pool.tensor_scalar(col(T2, small_b), col(SS, small_b), 1.0 / FH, RMS_EPS, ALU.mult, ALU.add))
                    back_step(g, pool.tensor_tensor(col(RINV2, small_b), col(T2, small_b), nhalf[:], ALU.pow))
                    pool.wait_ge(*peak_ready.at(g, J))
                    pool.nop(nofuse=True)
                    quant_scale(2, PEAK2, RINV2, SC2, QS2)

            def turn(g, nxt):
                links[0] = links[1] = 0
                units(g, nxt)
                for i in range(BEATS):
                    if nxt is not None:
                        mixer(nxt, i)
                    back(g, i)
                assert links == [FRONT_LINKS if nxt is not None else 0, BACK_LINKS], links

            links[0] = 0
            for i in range(UNITS):
                front(0, i)
            for i in range(BEATS):
                mixer(0, i)
            with pool.Fori(0, NG - 1) as g:
                turn(g, g + 1)
            turn(NG - 1, None)


def kernel(**inputs):
    import numpy as np
    import concourse.bacc as bacc
    from concourse.bass_utils import run_bass_kernel_spmd

    a = {k: np.asarray(v) for k, v in inputs.items()}

    def halves(w):
        return w.reshape(2, DH, -1).transpose(1, 0, 2)

    def blocks(w, p=128):
        return w.reshape(-1, p, w.shape[-1]).transpose(1, 0, 2)

    x = a["x"].reshape(B, 3, 14, 16, 14, 16).transpose(3, 5, 1, 0, 2, 4)
    x = x.reshape(KC, 128, NG, GB, J, TC)
    patches = x.transpose(2, 1, 4, 0, 3, 5).reshape(NG, 128, J, KC, TT)
    first = x[:, :, 0, 0].reshape(KC, 128, T).transpose(1, 0, 2)
    bias = a["L0_ffn_in_bias"].reshape(1, 1, HID)
    ffn_in = np.concatenate([halves(a["L0_ffn_in_weight"].T), np.concatenate([np.zeros_like(bias), bias], 1)], 0)
    xp = a["L1_attn_x_proj_w"].T
    bc = np.concatenate([xp[:, R:]] * 3, 1)
    steps = np.arange(TC)
    sigma = np.arange(TS)
    row_step = np.tile(sigma, NH)[:, None, None] + TS * np.arange(NR)[None, :, None]
    col_step = np.tile(steps, GB)[None, None, :]
    mask = (row_step < col_step).astype(np.float32).reshape(RB, -1)
    decp = (DECAY ** np.tile(steps, GB)).astype(np.float32)[:, None]
    dec = np.broadcast_to((WRITE * DECAY ** (-1.0 - np.arange(T) % TC)).astype(np.float32), (DH, T))
    bf = mybir.dt.np(BF16)
    sel = np.concatenate([np.eye(32, dtype=np.float32)] * 3, 0).astype(bf)
    eye = np.eye(128, dtype=np.float32)
    vec = lambda v: v.reshape(IC, 128).T
    arrays = dict(
        xt=patches, x0t=first, w_tok=blocks(a["L0_tok_W"].T), w_key=blocks(a["L0_attn_w_key"], DK),
        w_query=blocks(a["L0_attn_w_query"], DK), w_value=blocks(a["L0_attn_w_value"], DK),
        w_outt=blocks(a["L0_attn_w_out"].T, DK), w_gate=halves(a["L0_attn_w_gate"].T), ffn_in=ffn_in,
        ffn_out=blocks(a["L0_ffn_out_weight"]), w_inp=halves(a["L1_attn_in_proj_w"].T),
        conv_w=a["L1_attn_conv_w"].reshape(IC, 128, K).transpose(1, 0, 2), conv_b=vec(a["L1_attn_conv_b"]),
        w_xp=blocks(xp[:, :R]), w_bc=blocks(bc), w_dt=a["L1_attn_dt_proj_w"].T, b_dt=vec(a["L1_attn_dt_proj_b"]),
        a_log=blocks(a["L1_attn_A_log"]), d_skip=vec(a["L1_attn_D"]), w_op=blocks(a["L1_attn_out_proj_w"].T),
        alpha=vec(a["L1_attn_alpha"]), fgate=vec(a["L1_attn_feature_gating"]),
        q_in=halves(a["L1_ffn_w_in"].T), g_in=a["L1_ffn_g_in"], q_out=blocks(a["L1_ffn_w_out"].T),
        g_out=a["L1_ffn_g_out"], ident_c=eye, identb_c=eye.astype(bf), mask_c=mask, dec_c=dec, decp_c=decp, sel_c=sel)
    arrays = {k: np.ascontiguousarray(v) for k, v in arrays.items()}

    nc = bacc.Bacc("TRN2", target_bir_lowering=False, num_devices=1)
    aps = {k: nc.dram_tensor(f"in_{k}", v.shape, mybir.dt.from_np(v.dtype), kind="ExternalInput").ap() for k, v in arrays.items()}
    saved = nc.dram_tensor("saved_h2", (NG, TT, J, D), F32).ap()
    out = nc.dram_tensor("out_tiles", (NG, TT, J, D), F32, kind="ExternalOutput").ap()
    program(nc, saved=saved, out=out, **aps)
    r = run_bass_kernel_spmd(nc, [{f"in_{k}": v for k, v in arrays.items()}], core_ids=[0])
    tiles = np.asarray(r.results[0]["out_tiles"]).reshape(NG, GB, TC, J, D)
    return np.ascontiguousarray(tiles.transpose(0, 1, 3, 2, 4).reshape(B, T, D))
```
